# Optimizing a Trainium2 kernel written in Bass

```python
import numpy as np
import jax
import jax.numpy as jnp

def _softmax(x, axis=-1):
    return jax.nn.softmax(x, axis=axis)

def _gelu(x):
    return jax.nn.gelu(x, approximate=True)

def _silu(x):
    return jax.nn.silu(x)

def _sigmoid(x):
    return jax.nn.sigmoid(x)

def _layernorm(x, axis=-1, eps=1e-05):
    m = jnp.mean(x, axis=axis, keepdims=True)
    v = jnp.var(x, axis=axis, keepdims=True)
    return (x - m) / jnp.sqrt(v + eps)

def _scatter_add(tgt, idx, src, axis=0):
    return tgt.at[idx].add(src)

def _segment_sum(src, seg, n):
    return jax.ops.segment_sum(src, seg, n)
kernel_name = 'mk_vit_tower_d1_tok_img256_r4_ccaee5'

def setup_inputs(seed: int=0):
    np.random.seed(seed)
    _w = jnp.asarray

    def _rec_inputs():
        import jax
        import jax.numpy as jnp
        _rk = jax.random.key(seed)
        x = -0.000209053 + 0.999977 * jax.random.normal(jax.random.fold_in(_rk, 1), (4, 64, 56, 56), jnp.float32)
        return x
    x = _rec_inputs()

    def _L0_tok_setup():
        import jax, jax.numpy as jnp
        import numpy as np
        B, EMB, HT, WD = (32, 64, 56, 56)
        NH, WS, SHIFTED = (8, 4, True)

        def _rel_indices(ws):
            coords = np.array([[i, j] for i in range(ws) for j in range(ws)])
            rel = coords[None, :, :] - coords[:, None, :] + ws - 1
            return jnp.asarray(rel)

        def _shift_masks(ws):
            m = np.zeros((ws * ws, ws * ws), np.float32)
            s = ws * (ws // 2)
            m[-s:, :-s] = -np.inf
            m[:-s, -s:] = -np.inf
            col = m.reshape(ws, ws, ws, ws).transpose(1, 0, 3, 2).reshape(ws * ws, ws * ws)
            return (jnp.asarray(m), jnp.asarray(col))
        key = jax.random.key(seed)
        ks = jax.random.split(key, 6)
        x = jax.random.normal(ks[0], (B, EMB, HT, WD), jnp.float32)
        s = 1.0 / np.sqrt(EMB)
        w1 = jax.random.uniform(ks[1], (3 * EMB, EMB), jnp.float32, -s, s)
        b1 = jax.random.uniform(ks[2], (3 * EMB,), jnp.float32, -s, s)
        w2 = jax.random.uniform(ks[3], (EMB, EMB), jnp.float32, -s, s)
        b2 = jax.random.uniform(ks[4], (EMB,), jnp.float32, -s, s)
        pos_emb = jax.random.normal(ks[5], (2 * WS - 1, 2 * WS - 1), jnp.float32)
        return {'x': x, 'w1': w1, 'b1': b1, 'w2': w2, 'b2': b2, 'pos_emb': pos_emb}
    _L0_tok_all = _L0_tok_setup()
    _L0_tok_in = {k: v for k, v in _L0_tok_all.items() if k in ('w1', 'b1', 'w2', 'b2', 'pos_emb')}
    del _L0_tok_all

    def _L0_attn_setup():
        import jax, jax.numpy as jnp
        import numpy as np
        B, N, D = (8, 512, 64)
        key = jax.random.key(seed)
        k1, k2, k3, k4 = jax.random.split(key, 4)
        s = D ** (-0.5)
        return {'x': jax.random.normal(k1, (B, N, D), dtype=jnp.float32), 'Wq': jax.random.normal(k2, (D, D), dtype=jnp.float32) * s, 'Wk': jax.random.normal(k3, (D, D), dtype=jnp.float32) * s, 'Wv': jax.random.normal(k4, (D, D), dtype=jnp.float32) * s}
    _L0_attn_all = _L0_attn_setup()
    _L0_attn_in = {k: v for k, v in _L0_attn_all.items() if k in ('Wq', 'Wk', 'Wv')}
    del _L0_attn_all

    def _L0_ffn_setup():
        import math
        import jax, jax.numpy as jnp
        import numpy as np
        CAPACITY_FACTOR = 1.25
        TOP_K = 2
        LN_EPS = 1e-05

        def _layer_norm(x, gamma, beta):
            mu = jnp.mean(x, axis=-1, keepdims=True)
            var = jnp.var(x, axis=-1, keepdims=True)
            return (x - mu) * jax.lax.rsqrt(var + LN_EPS) * gamma + beta
        key = jax.random.key(seed)
        ks = jax.random.split(key, 4)
        B, S, D, F, E = (8, 1024, 64, 128, 8)
        x = jax.random.normal(ks[0], (B, S, D), dtype=jnp.float32)
        Wr = jax.random.normal(ks[1], (D, E), dtype=jnp.float32) / np.sqrt(D)
        br = jnp.zeros((E,), jnp.float32)
        W1 = jax.random.normal(ks[2], (E, D, F), dtype=jnp.float32) / np.sqrt(D)
        b1 = jnp.zeros((E, F), jnp.float32)
        W2 = jax.random.normal(ks[3], (E, F, D), dtype=jnp.float32) / np.sqrt(F)
        b2 = jnp.zeros((E, D), jnp.float32)
        gamma = jnp.ones((D,), jnp.float32)
        beta = jnp.zeros((D,), jnp.float32)
        return {'x': x, 'Wr': Wr, 'br': br, 'W1': W1, 'b1': b1, 'W2': W2, 'b2': b2, 'gamma': gamma, 'beta': beta}
    _L0_ffn_all = _L0_ffn_setup()
    _L0_ffn_in = {k: v for k, v in _L0_ffn_all.items() if k in ('Wr', 'br', 'W1', 'b1', 'W2', 'b2', 'gamma', 'beta')}
    del _L0_ffn_all
    return {'x': x, 'L0_tok_w1': _L0_tok_in['w1'], 'L0_tok_b1': _L0_tok_in['b1'], 'L0_tok_w2': _L0_tok_in['w2'], 'L0_tok_b2': _L0_tok_in['b2'], 'L0_tok_pos_emb': _L0_tok_in['pos_emb'], 'L0_attn_Wq': _L0_attn_in['Wq'], 'L0_attn_Wk': _L0_attn_in['Wk'], 'L0_attn_Wv': _L0_attn_in['Wv'], 'L0_ffn_Wr': _L0_ffn_in['Wr'], 'L0_ffn_br': _L0_ffn_in['br'], 'L0_ffn_W1': _L0_ffn_in['W1'], 'L0_ffn_b1': _L0_ffn_in['b1'], 'L0_ffn_W2': _L0_ffn_in['W2'], 'L0_ffn_b2': _L0_ffn_in['b2'], 'L0_ffn_gamma': _L0_ffn_in['gamma'], 'L0_ffn_beta': _L0_ffn_in['beta']}

def reference(x, L0_tok_w1, L0_tok_b1, L0_tok_w2, L0_tok_b2, L0_tok_pos_emb, L0_attn_Wq, L0_attn_Wk, L0_attn_Wv, L0_ffn_Wr, L0_ffn_br, L0_ffn_W1, L0_ffn_b1, L0_ffn_W2, L0_ffn_b2, L0_ffn_gamma, L0_ffn_beta):
    import jax
    import jax.numpy as jnp

    def _L0_tok_ref(x, w1, b1, w2, b2, pos_emb):
        import jax, jax.numpy as jnp
        import numpy as np
        B, EMB, HT, WD = (32, 64, 56, 56)
        NH, WS, SHIFTED = (8, 4, True)

        def _rel_indices(ws):
            coords = np.array([[i, j] for i in range(ws) for j in range(ws)])
            rel = coords[None, :, :] - coords[:, None, :] + ws - 1
            return jnp.asarray(rel)

        def _shift_masks(ws):
            m = np.zeros((ws * ws, ws * ws), np.float32)
            s = ws * (ws // 2)
            m[-s:, :-s] = -np.inf
            m[:-s, -s:] = -np.inf
            col = m.reshape(ws, ws, ws, ws).transpose(1, 0, 3, 2).reshape(ws * ws, ws * ws)
            return (jnp.asarray(m), jnp.asarray(col))
        b, c, ht, wd = x.shape
        ws, nh = (WS, NH)
        e = c // nh
        xt = x.reshape(b, c, ht * wd).transpose(0, 2, 1)
        qkv = xt @ w1.T + b1
        qkv = qkv.reshape(b, ht, wd, c, 3)
        if SHIFTED:
            qkv = jnp.roll(qkv, (-ws // 2, -ws // 2), axis=(1, 2))
        Wh, Ww = (ht // ws, wd // ws)
        qkv = qkv.reshape(b, Wh, ws, Ww, ws, e, nh, 3)
        qkv = qkv.transpose(0, 6, 1, 3, 2, 4, 5, 7).reshape(b, nh, Wh, Ww, ws * ws, e, 3)
        Q, K, V = (qkv[..., 0], qkv[..., 1], qkv[..., 2])
        scale = jnp.sqrt(jnp.float32(c / nh))
        wei = jnp.einsum('bhijpe,bhijqe->bhijpq', Q, K) / scale
        rel = _rel_indices(ws)
        wei = wei + pos_emb[rel[..., 0], rel[..., 1]]
        if SHIFTED:
            row_mask, col_mask = _shift_masks(ws)
            wei = wei.at[:, :, -1, :].add(row_mask)
            wei = wei.at[:, :, :, -1].add(col_mask)
        attn = jax.nn.softmax(wei, axis=-1)
        out = jnp.einsum('bhijpq,bhijqe->bhijpe', attn, V)
        out = out.reshape(b, nh, Wh, Ww, ws, ws, e)
        out = out.transpose(0, 2, 4, 3, 5, 1, 6).reshape(b, ht, wd, nh * e)
        out = out.reshape(b, ht * wd, c)
        return out @ w2.T + b2

    def _L0_attn_ref(x, Wq, Wk, Wv):
        import jax, jax.numpy as jnp
        import numpy as np
        B, N, D = (8, 512, 64)
        q = jnp.einsum('bnd,ed->bne', x, Wq)
        k = jnp.einsum('bnd,ed->bne', x, Wk)
        v = jnp.einsum('bnd,ed->bne', x, Wv)
        energy = jnp.einsum('bqd,bkd->bqk', q, k)
        scaling = jnp.asarray(x.shape[-1] ** (-0.5), x.dtype)
        att = jax.nn.softmax(energy, axis=-1) * scaling
        out = jnp.einsum('bqk,bkv->bqv', att, v)
        return out

    def _L0_ffn_ref(x, Wr, br, W1, b1, W2, b2, gamma, beta):
        import math
        import jax, jax.numpy as jnp
        import numpy as np
        CAPACITY_FACTOR = 1.25
        TOP_K = 2
        LN_EPS = 1e-05

        def _layer_norm(x, gamma, beta):
            mu = jnp.mean(x, axis=-1, keepdims=True)
            var = jnp.var(x, axis=-1, keepdims=True)
            return (x - mu) * jax.lax.rsqrt(var + LN_EPS) * gamma + beta
        B, S, D = x.shape
        E = Wr.shape[1]
        N = B * S
        K = TOP_K
        logits = jnp.mean(x, axis=1) @ Wr + br
        routing_weights = jax.nn.softmax(logits, axis=-1)
        capacity = float(math.ceil(N * CAPACITY_FACTOR / E))
        expected_loads = routing_weights.sum(axis=0) * (N / B)
        scale = jnp.where(expected_loads > capacity, capacity / expected_loads, 1.0)
        routing_weights = jax.nn.softmax(routing_weights * scale, axis=-1)
        rw_tok = jnp.broadcast_to(routing_weights[:, None, :], (B, S, E)).reshape(N, E)
        top_w, top_i = jax.lax.top_k(rw_tok, K)
        top_w = jax.nn.softmax(top_w, axis=-1)
        xf = x.reshape(N, D)
        h = jax.nn.gelu(jnp.einsum('nd,edf->enf', xf, W1) + b1[:, None, :], approximate=False)
        y = jnp.einsum('enf,efd->end', h, W2) + b2[:, None, :]
        w_dense = jnp.zeros((N, E), x.dtype).at[jnp.arange(N)[:, None], top_i].add(top_w)
        out = jnp.einsum('ne,end->nd', w_dense, y).reshape(B, S, D)
        out = _layer_norm(out + x, gamma, beta)
        return out
    h = _L0_tok_ref(x, L0_tok_w1, L0_tok_b1, L0_tok_w2, L0_tok_b2, L0_tok_pos_emb)
    h = h + _L0_attn_ref(_layernorm(h, axis=-1), L0_attn_Wq, L0_attn_Wk, L0_attn_Wv)
    h = h + _L0_ffn_ref(_layernorm(h, axis=-1), L0_ffn_Wr, L0_ffn_br, L0_ffn_W1, L0_ffn_b1, L0_ffn_W2, L0_ffn_b2, L0_ffn_gamma, L0_ffn_beta)
    return h

_drawn_inputs = setup_inputs


def setup_inputs(seed=0):
    import zlib

    import numpy as np

    out = dict(_drawn_inputs(seed))
    spreads = {'L0_ffn_br': (0.0, 0.8),
     'L0_ffn_b1': (0.0, 0.1),
     'L0_ffn_b2': (0.0, 0.1),
     'L0_ffn_gamma': (1.0, 0.2),
     'L0_ffn_beta': (0.0, 0.1)}
    factors = {}
    for name, (base, spread) in spreads.items():
        noise = np.random.default_rng([zlib.crc32(name.encode()), seed]).standard_normal(out[name].shape)
        drawn = base * np.exp(spread * noise) if base else spread * noise
        out[name] = jnp.asarray(drawn.astype(out[name].dtype))
    for name, factor in factors.items():
        out[name] = (out[name] * factor).astype(out[name].dtype)
    return out
```

```python
import math

import numpy as np
import concourse.bass as bass
from concourse import mybir
from contextlib import ExitStack

F32 = mybir.dt.float32
F16 = mybir.dt.float16
BF16 = mybir.dt.bfloat16
I32 = mybir.dt.int32
ALU = mybir.AluOpType
ACT = mybir.ActivationFunctionType
AX = mybir.AxisListType

B, C, HT = 4, 64, 56
WS, NH = 4, 8
WT = WS * WS
NTOK = HT * HT
NW = HT // WS
NPAIR = NW * NW // 2
TILES = -(-NTOK // 128)
UT = 5
UPB = TILES // UT
UNITS = B * UPB
UP = UT * 4
UC = UP * WT
UTOK = UT * 128
HF = UTOK // 2
NE, NF = 8, 128
EPS = 1e-5
RW = HT + 2
RAWW = 6 + HT * RW + 2
KC = 448
NKC = NTOK // KC
CAPACITY = float(math.ceil(B * NTOK * 1.25 / NE))
MAGIC = float(0x5F3759DF)

C_ID, C_REP, C_HEAD, C_PAR, C_WIN, C_EDGE = 0, 128, 384, 392, 408, 410
C_RANK = C_EDGE + TILES * WT
C_DIAG = C_RANK + NE
C_END = C_DIAG + B


def constants():
    p = np.arange(128)
    c = np.zeros((128, C_END), np.float32)
    c[:, C_ID:C_ID + 128] = np.eye(128)
    for j in range(8):
        m = np.arange(32)
        c[:, C_REP + 32 * j:C_REP + 32 * j + 32] = (p[:, None] // WT == j) & (p[:, None] % WT == m[None] % WT)
    c[:, C_HEAD:C_HEAD + NH] = p[:, None] % NH == np.arange(NH)[None]
    c[:, C_PAR:C_PAR + 16] = p[:, None] % 32 // 16 == np.arange(16)[None] // 8
    c[:, C_WIN:C_WIN + 2] = p[:, None] % 32 // 16 == np.arange(2)[None]
    half = WS // 2
    edge = np.zeros((128, TILES, WT), np.float32)
    for t in range(TILES):
        for q in range(128):
            pair = 4 * t + q // 32
            if pair >= NPAIR:
                continue
            wi, wj = pair // (NW // 2), 2 * (pair % (NW // 2)) + q % 32 // 16
            qi, qj = q % WT // WS, q % WS
            for k in range(WT):
                ki, kj = k // WS, k % WS
                if (wi == NW - 1 and (qi >= half) != (ki >= half)) or (wj == NW - 1 and (qj >= half) != (kj >= half)):
                    edge[q, t, k] = -1e30
    c[:, C_EDGE:C_EDGE + TILES * WT] = edge.reshape(128, -1)
    c[:, C_RANK:C_RANK + NE] = NE - np.arange(NE)[None]
    c[:, C_DIAG:C_DIAG + B] = p[:, None] == np.arange(B)[None]
    return c


def vit_tower(nc, x, wq_t, wk_t, wv_t, bq, bk, bv, w2_t, b2, pos, Wq, Wk, Wv, Wr, br, W1, b1_t, W2, fb2, gamma, beta, cst, out):
    ctx = ExitStack()
    with ctx:
        def sb(name, shape, dt=F32):
            return ctx.enter_context(nc.sbuf_tensor(name, shape, dt))

        def sem(name):
            return ctx.enter_context(nc.semaphore(name))

        bank = [ctx.enter_context(nc.psum_tensor(f"bank{i}", [128, 512], F32)) for i in range(8)]

        xw = sb("xw", [128, UNITS * UC])
        x3 = xw[:, :].rearrange("p (t c) -> p t c", c=C)
        h = sb("h", [128, B * TILES, C])
        xn = sb("xn", [128, B * TILES, 128], F16)
        xt = sb("xt", [128, B * TILES * 128], F16)
        cs = sb("cs", [128, C_END])
        id16 = sb("id16", [128, 128], F16)
        bias = sb("bias", [128, TILES, WT])
        posq = sb("posq", [128, WT])
        valid = sb("valid", [128, UT])
        wqb, wkb, wvb, w2b = (sb(n, [128, 128]) for n in ("wqb", "wkb", "wvb", "w2b"))
        bqc, bkc, bqs = (sb(n, [128, 1]) for n in ("bqc", "bkc", "bqs"))
        bkm = sb("bkm", [128, NH])
        bvr = sb("bvr", [128, 128])
        b2r = sb("b2r", [128, C])
        ident = cs[:, C_ID:C_ID + 128]

        scr = sb("scr", [128, 21600])
        at = [0]

        def cut(n, dt=F32):
            words = n if dt in (F32, I32) else -(-n // 2)
            a = scr[:, at[0]:at[0] + words]
            at[0] += words
            assert at[0] <= 21600, at[0]
            return a if dt == F32 else a.bitcast(dt)

        raw = [cut(RAWW) for _ in range(2)]
        xu = [cut(384) for _ in range(2)]
        qb = [cut(UP * 32).rearrange("p (n q) -> p n q", q=32) for _ in range(2)]
        km = cut(UP * 128).rearrange("p (n h k) -> p n h k", h=NH, k=WT)
        v2 = cut(384)
        rs = cut(768)
        vb = [cut(8 * 3 * 2 * C).rearrange("p (n c) -> p n c", c=C) for _ in range(2)]
        s1 = cut(UTOK)
        mx, den, rden = (cut(UT * NH) for _ in range(3))
        pn = cut(UTOK)
        pts = cut(UTOK)
        o = cut(6 * C)
        ots = cut(384)
        xnu = cut(UTOK, F16).rearrange("p (t c) -> p t c", c=128)
        end1 = at[0]
        ln_s = sb("ln_s", [128, 8 * UT])
        ln_c = sb("ln_c", [128, UT * C])
        ln_q = sb("ln_q", [128, UT * C])

        at[0] = 0
        NP = 3
        p32 = [cut(UTOK) for _ in range(NP)]
        plo = [cut(UTOK, BF16) for _ in range(NP)]
        qh = [cut(UTOK, F16) for _ in range(2)]
        ql = [cut(UTOK, F16) for _ in range(2)]
        un = cut(UTOK)
        att = cut(UT * C)
        rd = cut(UT)
        mxk = cut(UT * NKC).rearrange("p (t k) -> p t k", k=NKC)
        mq = cut(UT)
        zm = cut(UT * C, F16).rearrange("p (t c) -> p t c", c=C)
        xn3 = cut(UTOK, F16).rearrange("p (t c) -> p t c", c=128)
        xt3 = [cut(UTOK, F16) for _ in range(2)]
        hs = [[cut(UTOK) for _ in range(2)] for _ in range(2)]
        y1 = cut(UT * C)
        yo = [cut(UT * C).rearrange("p (t c) -> p t c", c=C) for _ in range(2)]
        acc3 = cut(B * C).rearrange("p (b c) -> p b c", c=C)
        acc3t = cut(B)
        rt = cut(160)
        cf = cut(2 * B * NE * 2)
        w1f = cut(NF)
        w1s = cut(B * 2 * 3 * NF, BF16).rearrange("p (n j f) -> p n j f", j=3, f=NF)
        w2s = cut(B * 2 * C).rearrange("p (n c) -> p n c", c=C)
        b1s = cut(B * 2)
        b2s = cut(B * C).rearrange("p (b c) -> p b c", c=C)

        wq2, wk2, wv2 = (sb(n, [64, 128]) for n in ("wq2", "wk2", "wv2"))
        an = sb("an", [128, 128])
        a3 = sb("a3", [128, 3, 128], BF16)
        wvx = sb("wvx", [128, 66])
        sc = sb("sc", [128, 4])
        wr = sb("wr", [64, NE])
        brr = sb("brr", [B, NE])
        gar, ber = (sb(n, [128, C]) for n in ("gar", "ber"))
        ones = sb("ones", [128, 128])
        w1d = sb("w1d", [128, NE, NF])
        w2d = sb("w2d", [128, NE, C])
        b1d = sb("b1d", [128, NE])
        fb2r = sb("fb2r", [128, NE, C])

        names = """s_cst s_w s_w2 s_raw s_raw1 s_wrap s_xw s_v s_a s_g s_set s_xu s_qkv s_qb s_km s_v2 s_rep s_rs s_vb s_sc s_s1 s_s2 s_ex s_pn
            s_pt s_pts s_av s_o s_ot s_ots s_op s_h1 s_xnu s_xtp s_xt s_xn s_p1
            s_ab s_am s_a3 s_wvt s_e s_exp s_lo s_logp s_pv s_un s_x s_xd s_qh s_lnq s_p2 s_fx
            s_r s_rc s_w1 s_x3 s_x3p s_xt3 s_hp s_hs s_y s_yd s_yo s_out0 s_out1 s_k0 s_k1""".split()
        S = {n: sem(n) for n in names}
        block = ctx.enter_context(nc.Block())

        class Chain:

            def __init__(self, eng, name):
                self.eng, self.sem, self.n = eng, S[name], 0

            def __call__(self, ins):
                self.n += 1
                ins.then_inc(self.sem, 1)
                self.eng.wait_ge(self.sem, self.n)

        def halves(ap):
            return ap.rearrange("p (n q) -> p n q", q=WT)

        def bc(ap, shape):
            return ap.to_broadcast(shape)

        def tk(ap, c=C):
            return ap.rearrange("p (t c) -> p t c", c=c)

        def unit_tiles(u):
            return slice(u * UT, u * UT + UT)

        QK = 5

        def x_base(i):
            return 38 + 40 * i

        def unnorm(a, i):
            a.wait_ge(S["s_pv"], (i + 1) * TILES)
            if i >= 1:
                a.wait_ge(S["s_x"], x_base(i) + 1)
            for hf in range(2):
                a.activation(un[:, HF * hf:HF * hf + HF], bank[4 + hf][:, 0:HF], ACT.Copy).then_inc(S["s_un"], 1)

        def stored(u):
            return sum(min(8 * UT, NW * NW - 8 * UT * (w % UPB)) for w in range(u % 2, u + 1, 2))

        @block.sync
        def _(sp):
            sp.dma_start(cs[:, :], cst).then_inc(S["s_cst"], 16)

            def load_x(b):
                for hf in range(2):
                    off = 4 * (1 - hf)
                    im = raw[b % 2][64 * hf:64 * hf + 64, off:off + HT * RW].rearrange("p (r c) -> p r c", c=RW)
                    sp.dma_start(im[:, 0:HT - 2, 0:HT], x[b, :, 2:HT, :]).then_inc(S[f"s_raw{b % 2 or ''}"], 16)
                    sp.dma_start(im[:, HT - 2:HT, 0:HT], x[b, :, 0:2, :]).then_inc(S[f"s_raw{b % 2 or ''}"], 16)

            sp.wait_ge(S["s_k0"], 1)
            load_x(0)
            for w, s in ((wqb, wq_t), (wkb, wk_t), (wvb, wv_t), (w2b, w2_t)):
                for hf in range(2):
                    sp.dma_start(w[64 * hf:64 * hf + 64, 64 * hf:64 * hf + 64], s).then_inc(S["s_w"], 16)
            for d, s in ((bqc, bq), (bkc, bk)):
                for hf in range(2):
                    sp.dma_start(d[64 * hf:64 * hf + 64, :], s).then_inc(S["s_w"], 16)
            for hf in range(2):
                sp.dma_start(bvr[:, 64 * hf:64 * hf + 64], bv.to_broadcast([128, C])).then_inc(S["s_w"], 16)
            sp.dma_start(b2r[:, :], b2.to_broadcast([128, C])).then_inc(S["s_w"], 16)
            for q in range(WT):
                qi, qj = q // WS, q % WS
                src = pos[3 - qi:7 - qi, 3 - qj:7 - qj].rearrange("(o a) b -> o a b", o=1).to_broadcast([8, WS, WS])
                sp.dma_start(posq[q:q + 7 * 16 + 1:16, :].rearrange("p (a b) -> p a b", b=WS), src).then_inc(S["s_w"], 16)
            load_x(1)
            for d, s in ((wq2, Wq), (wk2, Wk), (wv2, Wv)):
                for hf in range(2):
                    sp.dma_start(d[:, 64 * hf:64 * hf + 64], s).then_inc(S["s_w2"], 16)
            for b in range(2, B):
                sp.wait_ge(S["s_xw"], NW * (b - 1))
                load_x(b)
            sp.dma_start(wr[:, :], Wr).then_inc(S["s_w2"], 16)
            sp.dma_start(brr[:, :], br.to_broadcast([B, NE])).then_inc(S["s_w2"], 16)
            sp.dma_start(gar[:, :], gamma.to_broadcast([128, C])).then_inc(S["s_w2"], 16)
            sp.dma_start(ber[:, :], beta.to_broadcast([128, C])).then_inc(S["s_w2"], 16)
            for hf in range(2):
                sp.dma_start(w1d[64 * hf:64 * hf + 64, :, :], W1.rearrange("e d f -> d e f")).then_inc(S["s_w2"], 16)
            sp.dma_start(w2d[:, :, :], W2.rearrange("e f d -> f e d")).then_inc(S["s_w2"], 16)
            sp.dma_start(b1d[:, :], b1_t).then_inc(S["s_w2"], 16)
            sp.dma_start(fb2r[:, :, :], fb2.rearrange("(o e) d -> o e d", o=1).to_broadcast([128, NE, C])).then_inc(S["s_w2"], 16)
            for u in range(UNITS):
                sp.wait_ge(S["s_xnu"], u + 1)
                sp.dma_start(xn[:, unit_tiles(u), :], xnu).then_inc(S["s_xn"], 16)
            n = 0
            for u in range(UNITS):
                b, t0 = u // UPB, u % UPB * UT
                sp.wait_ge(S["s_yo"], u + 1)
                for i in range(UT):
                    w, end = 8 * (t0 + i), min(8 * (t0 + i) + 8, NW * NW)
                    while w < end:
                        wi, wj = w // NW, w % NW
                        k = min(end - w, NW - wj)
                        src = yo[u % 2][(w % 8) * WT:(w % 8 + k) * WT, i, :]
                        dst = out[b].rearrange("(a i b j) c -> a b i j c", a=NW, i=WS, b=NW)[wi, wj:wj + k]
                        for m in range(k):
                            sp.dma_start(dst[m], src[m * WT:(m + 1) * WT, :]).then_inc(S[f"s_out{u % 2}"], 16)
                        w += k
            sp.wait_ge(S["s_out0"], 16 * stored(UNITS - 2))
            sp.wait_ge(S["s_out1"], 16 * stored(UNITS - 1))

        NW1 = 16 * (8 + 4 + 2 + 1 + WT)
        NW2 = 16 * (6 + 4 + 2 + 3)

        @block.gpsimd
        def _(g):
            ch = Chain(g, "s_g")
            ch(g.memset(scr[:, 0:2 * RAWW], 0.0))
            for w in (wqb, wkb, wvb, w2b):
                ch(g.memset(w[:, :], 0.0))
            g.memset(scr[:, 2 * RAWW:end1], 0.0).then_inc(S["s_k0"], 1)
            ch(g.memset(xw[:, :], 0.0))
            ch(g.memset(ones[:, :], 1.0))
            g.wait_ge(S["s_k0"], 1)
            ch(g.memset(xnu[:, :, 63:64], 1.0))
            ch(g.memset(valid[:, :], 1.0))
            ch(g.memset(valid[64:128, UT - 1:UT], 0.0))
            g.wait_ge(S["s_cst"], 16)
            g.tensor_copy(id16[:, :], ident).then_inc(S["s_set"], 1)
            g.wait_ge(S["s_w"], NW1)
            g.wait_ge(S["s_set"], 1)
            g.tensor_tensor(bias[:, :, :], cs[:, C_EDGE:C_EDGE + TILES * WT].rearrange("p (t k) -> p t k", k=WT),
                            bc(posq[:, :].rearrange("p (o k) -> p o k", o=1), [128, TILES, WT]), ALU.add).then_inc(S["s_set"], 1)

            g.wait_ge(S["s_set"], 2)

            def order(b):
                im = raw[b % 2]
                g.wait_ge(S[f"s_raw{b % 2 or ''}"], 64 * (b // 2 + 1))
                rows = im[64:128, 0:HT * RW].rearrange("p (r c) -> p r c", c=RW)
                ch(g.tensor_copy(rows[:, :, HT:HT + 2], rows[:, :, 0:2]))
                for wi in range(NW):
                    band = im[:, 6 + wi * WS * RW:6 + (wi + 1) * WS * RW].rearrange("p (i c) -> p i c", c=RW)
                    src = band[:, :, 0:56].rearrange("p i (m q) -> p m i q", q=8)[:, :, :, 0:4]
                    at0 = b * UPB * UC + wi * (NW // 2) * WT
                    dst = xw[:, at0:at0 + (NW // 2) * WT].rearrange("p (m i q) -> p m i q", i=WS, q=WS)
                    g.tensor_copy(dst, src).then_inc(S["s_xw"], 1)
                g.wait_ge(S["s_xw"], NW * (b + 1))

            def v_mask(u):
                g.wait_ge(S["s_rs"], u + 1)
                if u >= 2:
                    g.wait_ge(S["s_av"], u - 1)
                for q in range(4):
                    r = slice(32 * q, 32 * q + 32)
                    l = g.tensor_tensor(vb[u % 2][r, :, 16 * q:16 * q + 16], rs[r, :].rearrange("p (n c) -> p n c", c=16),
                                        bc(cs[r, C_PAR:C_PAR + 16].rearrange("p (o c) -> p o c", o=1), [32, 48, 16]), ALU.mult)
                    l.then_inc(S["s_vb"], 1)
                    g.wait_ge(S["s_vb"], 4 * u + q + 1)

            def s_shift(u):
                g.wait_ge(S["s_s1"], 2 * u + 2)
                s = s1.rearrange("p (n k) -> p n k", k=WT)
                g.tensor_tensor(s, s, bc(mx.rearrange("p (n o) -> p n o", o=1), [128, UT * NH, WT]), ALU.subtract).then_inc(S["s_s2"], 1)
                g.wait_ge(S["s_s2"], u + 1)

            def p_norm(u):
                g.wait_ge(S["s_ex"], 2 * u + 2)
                g.tensor_tensor(pn.rearrange("p (n k) -> p n k", k=WT), pn.rearrange("p (n k) -> p n k", k=WT),
                                bc(rden.rearrange("p (n o) -> p n o", o=1), [128, UT * NH, WT]), ALU.mult).then_inc(S["s_pn"], 1)
                g.wait_ge(S["s_pn"], u + 1)

            order(0)
            for u in range(UNITS):
                v_mask(u)
                s_shift(u)
                p_norm(u)
                if u % UPB == 0 and u // UPB + 1 < B:
                    order(u // UPB + 1)
            g.wait_ge(S["s_am"], 1)
            g.partition_all_reduce(sc[:, 1:2], sc[:, 0:1], 128, bass.bass_isa.ReduceOp.max).then_inc(S["s_am"], 1)
            for s in range(UNITS * TILES):
                if s % TILES % 5 in (1, 3):
                    g.wait_ge(S["s_exp"], 2 * s + 2)
                    if s >= NP:
                        g.wait_ge(S["s_pv"], s - NP + 1)
                    pp = p32[s % NP]
                    g.tensor_tensor(plo[s % NP], pp, pp.bitcast(BF16)[:, 1::2], ALU.subtract).then_inc(S["s_logp"], 1)

        @block.scalar
        def _(a):
            ch = Chain(a, "s_a")
            a.wait_ge(S["s_w"], NW1)
            a.wait_ge(S["s_cst"], 16)
            ch(a.activation(bqs[:, :], bqc[:, :], ACT.Copy, scale=float(1 / math.sqrt(C / NH))))
            for hh in range(NH):
                l = a.activation(bkm[:, hh:hh + 1], bkc[:, :], ACT.Copy, scale=cs[:, C_HEAD + hh:C_HEAD + hh + 1])
                ch(l)
            for u in range(UNITS + 1):
                if u < UNITS:
                    b, s = u // UPB, u % UPB
                    a.wait_ge(S["s_xw"], NW * b + min(NW, -(-UP * (s + 1) // (NW // 2))))
                    if u >= 2:
                        a.wait_ge(S["s_qkv"], u - 1)
                    a.activation(xu[u % 2][:, 0:UC], xw[:, u * UC:(u + 1) * UC], ACT.Copy).then_inc(S["s_xu"], 1)
                    a.wait_ge(S["s_qkv"], u + 1)
                    if u >= 2:
                        a.wait_ge(S["s_sc"], u - 1)
                    for hf in range(2):
                        r = slice(64 * hf, 64 * hf + 64)
                        a.activation(qb[u % 2][r, :, 16 * hf:16 * hf + 16], halves(bank[0][r, 0:UC]), ACT.Identity,
                                     bias=bqs[r, :], scale=float(1 / math.sqrt(C / NH))).then_inc(S["s_qb"], 1)
                    if u >= 1:
                        a.wait_ge(S["s_sc"], u)
                    for hh in range(NH):
                        a.activation(km[:, :, hh, :], halves(bank[1][:, 0:UC]), ACT.Identity, bias=bkm[:, hh:hh + 1],
                                     scale=cs[:, C_HEAD + hh:C_HEAD + hh + 1]).then_inc(S["s_km"], 1)
                if u >= 1:
                    v = u - 1
                    a.wait_ge(S["s_pt"], v + 1)
                    if v >= 1:
                        a.wait_ge(S["s_av"], v)
                    for i, n in ((0, 512), (1, 128)):
                        a.activation(pts[:, 512 * i:512 * i + n], bank[5 + i][:, 0:n], ACT.Copy).then_inc(S["s_pts"], 1)
                if u < UNITS:
                    a.wait_ge(S["s_rep"], u + 1)
                    if u >= 1:
                        a.wait_ge(S["s_vb"], 4 * u)
                    for i in range(2):
                        l = a.activation(rs[:, 384 * i:384 * i + 384], bank[3 + i][:, 0:384], ACT.Copy)
                        if i == 0:
                            ch(l)
                        else:
                            l.then_inc(S["s_rs"], 1)
                if u >= 1:
                    v = u - 1
                    a.wait_ge(S["s_ot"], v + 1)
                    if v >= 1:
                        a.wait_ge(S["s_op"], v)
                    a.activation(ots, bank[7][:, 0:384], ACT.Copy).then_inc(S["s_ots"], 1)
                    a.wait_ge(S["s_xtp"], v + 1)
                    a.activation(xt[:, v * UTOK:(v + 1) * UTOK], bank[7][:, :].bitcast(F16)[:, 0:UTOK],
                                 ACT.Copy).then_inc(S["s_xt"], 1)
                if u < UNITS:
                    a.wait_ge(S["s_s2"], u + 1)
                    if u >= 1:
                        a.wait_ge(S["s_pt"], u)
                    a.activation(pn, s1, ACT.Exp).then_inc(S["s_ex"], 1)
            a.wait_ge(S["s_a3"], 3)
            a.wait_ge(S["s_p1"], 1)

            def q_high(i, hf, idx):
                a.wait_ge(S["s_x"], idx + 1)
                a.activation(qh[i % 2][:, HF * hf:HF * hf + HF], bank[6 + idx % 2][:, 0:HF], ACT.Copy).then_inc(S["s_qh"], 1)

            q_high(0, 0, 0)
            q_high(0, 1, 1)
            for i in range(UNITS):
                for k in range(TILES):
                    s = i * TILES + k
                    if s >= NP:
                        a.wait_ge(S["s_pv"], s - NP + 1)
                    for hf in range(2):
                        n = 2 * s + hf
                        a.wait_ge(S["s_e"], n + 1)
                        a.activation(p32[s % NP][:, HF * hf:HF * hf + HF], bank[n % 4][:, 0:HF], ACT.Exp, scale=sc[:, 1:2]).then_inc(S["s_exp"], 1)
                    if k == 2 and i >= 1:
                        unnorm(a, i - 1)
                    if k == QK and i + 1 < UNITS:
                        if i >= 1:
                            a.wait_ge(S["s_e"], 2 * i * TILES)
                        q_high(i + 1, 0, x_base(i) + 1)
                        q_high(i + 1, 1, x_base(i) + 2)
            unnorm(a, UNITS - 1)
            for j, (src, dst, n) in enumerate(((3, 4, NE), (3, 4, NE), (17, 18, 2))):
                a.wait_ge(S["s_k1"], j + 1)
                a.activation(rt[0:B, 8 * dst:8 * dst + n], rt[0:B, 8 * src:8 * src + n], ACT.Exp).then_inc(S["s_fx"], 1)
            for u in range(UNITS):
                a.wait_ge(S["s_x3p"], u + 1)
                if u >= 2:
                    a.wait_ge(S["s_hp"], 4 * (u - 1))
                a.activation(xt3[u % 2], bank[u % 2][:, :].bitcast(F16)[:, 0:UTOK], ACT.Copy).then_inc(S["s_xt3"], 1)
                if u >= 2:
                    a.wait_ge(S["s_y"], u - 1)
                if u == 0:
                    a.wait_ge(S["s_w1"], 1)
                for k in range(2):
                    for hf in range(2):
                        n = 2 * k + hf
                        a.wait_ge(S["s_hp"], 4 * u + n + 1)
                        bk_ = 2 * (u // UPB) + k
                        a.activation(hs[u % 2][k][:, HF * hf:HF * hf + HF], bank[2 + n][:, 0:HF], ACT.Gelu, bias=b1s[:, bk_:bk_ + 1])\
                            .then_inc(S["s_hs"], 1)

        @block.tensor
        def _(t):
            t.wait_ge(S["s_w"], NW1)
            t.wait_ge(S["s_cst"], 16)
            t.wait_ge(S["s_set"], 1)
            for u in range(UNITS + 1):
                v = u - 1
                if u < UNITS:
                    t.wait_ge(S["s_xu"], u + 1)
                    if u >= 1:
                        t.wait_ge(S["s_qb"], 2 * u)
                        t.wait_ge(S["s_km"], 8 * u)
                    if u >= 2:
                        t.wait_ge(S["s_h1"], u - 1)
                    t.matmul(bank[0][:, 0:UC], wqb[:, :], xw[:, u * UC:(u + 1) * UC], start=True, stop=True)
                    t.matmul(bank[1][:, 0:UC], wkb[:, :], xw[:, u * UC:(u + 1) * UC], start=True, stop=True)
                    for j in range(3):
                        l = t.matmul(bank[2][:, 128 * j:128 * j + 128], xu[u % 2][:, 128 * j:128 * j + 128], wvb[:, :], start=True, stop=True)
                    l.then_inc(S["s_qkv"], 1)
                if v >= 0:
                    t.wait_ge(S["s_pn"], v + 1)
                    for i in range(UT):
                        l = t.transpose(bank[5 + i // 4][:, i % 4 * 128:i % 4 * 128 + 128], pn[:, i * 128:i * 128 + 128], ident)
                    l.then_inc(S["s_pt"], 1)
                    t.wait_ge(S["s_pts"], 2 * v + 2)
                    t.wait_ge(S["s_vb"], 4 * v + 4)
                    for p in range(UP):
                        tt, q = p // 4, p % 4
                        j, tj = p % 8, p // 8
                        w0 = (3 * j + tj) * 2
                        l = t.matmul(bank[3 + tt // 4][32 * q:32 * q + 32, tt % 4 * 128:tt % 4 * 128 + 128],
                                     pts[:, tt * 128 + 32 * q:tt * 128 + 32 * q + 32], vb[v % 2][:, w0:w0 + 2, :], start=True, stop=True)
                    l.then_inc(S["s_av"], 1)
                if u < UNITS:
                    t.wait_ge(S["s_v2"], u + 1)
                    if v >= 0:
                        t.wait_ge(S["s_o"], v + 1)
                    for j in range(8):
                        for q in range(4):
                            l = t.matmul(bank[3 + j // 4][32 * q:32 * q + 32, j % 4 * 96:j % 4 * 96 + 96], cs[:, C_REP + 32 * j:C_REP + 32 * j + 32],
                                         v2.rearrange("p (n c) -> p n c", c=C)[:, :, 16 * q:16 * q + 16], start=True, stop=True)
                    l.then_inc(S["s_rep"], 1)
                    t.wait_ge(S["s_qb"], 2 * u + 2)
                    t.wait_ge(S["s_km"], 8 * u + 8)
                    for p in range(UP):
                        tt, q = p // 4, p % 4
                        l = t.matmul(bank[5 + tt // 4][32 * q:32 * q + 32, tt % 4 * 128:tt % 4 * 128 + 128],
                                     qb[u % 2][:, p, :], km[:, p, :, :], start=True, stop=True)
                    l.then_inc(S["s_sc"], 1)
                if v >= 0:
                    t.wait_ge(S["s_o"], v + 1)
                    if v >= 1:
                        t.wait_ge(S["s_xt"], v)
                    for j in range(3):
                        l = t.transpose(bank[7][:, 128 * j:128 * j + 128], o[:, 128 * j:128 * j + 128], ident)
                    l.then_inc(S["s_ot"], 1)
                    t.wait_ge(S["s_ots"], v + 1)
                    if u < UNITS:
                        t.wait_ge(S["s_v2"], u + 1)
                    for j in range(3):
                        l = t.matmul(bank[2][:, 128 * j:128 * j + 128], ots[:, 128 * j:128 * j + 128], w2b[:, :], start=True, stop=True)
                    l.then_inc(S["s_op"], 1)
                    t.wait_ge(S["s_xnu"], v + 1)
                    for i in range(UT):
                        l = t.transpose(bank[7][:, :].bitcast(F16)[:, i * 128:i * 128 + 128], xnu[:, i, :], id16[:, :])
                    l.then_inc(S["s_xtp"], 1)
            t.wait_ge(S["s_ab"], 3)
            t.wait_ge(S["s_h1"], UNITS)
            t.matmul(bank[2][:, 0:128], wq2[:, :], wk2[:, :], start=True, stop=True).then_inc(S["s_wvt"], 1)
            t.transpose(bank[3][:, 0:64], wv2[:, :], cs[0:64, C_ID:C_ID + 64]).then_inc(S["s_wvt"], 1)
            t.wait_ge(S["s_a3"], 3)
            t.wait_ge(S["s_p1"], 1)
            t.wait_ge(S["s_xt"], UNITS)
            t.wait_ge(S["s_xn"], 16 * UNITS)

            def xslot(idx):
                if idx >= 2:
                    t.wait_ge(S["s_xd"], idx - 1)
                return bank[6 + idx % 2]

            def q_proj(i, hf, idx):
                bk_ = xslot(idx)
                c0 = i * UTOK + hf * HF
                for j in range(3):
                    l = t.matmul(bk_[:, 0:HF], a3[:, j, :], xt[:, c0:c0 + HF], start=j == 0, stop=j == 2)
                l.then_inc(S["s_x"], 1)

            def q_max(i, n, idx):
                tt, kc = n // NKC, n % NKC
                bk_ = xslot(idx)
                c0 = i // UPB * TILES * 128 + kc * KC
                if n == 0:
                    t.wait_ge(S["s_qh"], 2 * i + 2)
                t.matmul(bk_[:, 0:KC], qh[i % 2][:, tt * 128:tt * 128 + 128], xt[:, c0:c0 + KC], start=True, stop=True).then_inc(S["s_x"], 1)

            def max_rows(i, hf, idx):
                t.wait_ge(S["s_lnq"], i + 1)
                bk_ = xslot(idx)
                for c0 in (0, 128, 256):
                    lo = hf * HF + c0
                    n = min(128, HF - c0)
                    while n > 0:
                        tt, p0 = lo // 128, lo % 128
                        m = min(n, 128 - p0)
                        l = t.matmul(bk_[0:64, lo - hf * HF:lo - hf * HF + m], zm[:, tt, :], id16[:, p0:p0 + m], start=True, stop=True)
                        lo += m
                        n -= m
                l.then_inc(S["s_x"], 1)

            def finish(i, idx):
                t.wait_ge(S["s_un"], 2 * i + 2)
                bk_ = xslot(idx)
                for j in range(UT):
                    l = t.matmul(bk_[:, 66 * j:66 * j + 66], un[:, 128 * j:128 * j + 128], wvx[:, :], start=True, stop=True)
                l.then_inc(S["s_x"], 1)

            q_proj(0, 0, 0)
            q_proj(0, 1, 1)
            for n in range(UT * NKC):
                q_max(0, n, 2 + n)
            max_rows(0, 0, 37)
            max_rows(0, 1, 38)

            def energies(i, k):
                s = i * TILES + k
                if k == 0:
                    t.wait_ge(S["s_xd"], x_base(i) if i else 39)
                kt = i // UPB * TILES + k
                for hf in range(2):
                    n = 2 * s + hf
                    if n >= 4:
                        t.wait_ge(S["s_exp"], n - 3)
                    for j, q in enumerate((qh, ql)):
                        l = t.matmul(bank[n % 4][:, 0:HF], xt[:, kt * 128:kt * 128 + 128], q[i % 2][:, HF * hf:HF * hf + HF], start=j == 0, stop=j == 1)
                    l.then_inc(S["s_e"], 1)

            def values(s):
                i, k = s // TILES, s % TILES
                kt = i // UPB * TILES + k
                if k == 0 and i >= 1:
                    t.wait_ge(S["s_un"], 2 * i)
                if k % 5 in (1, 3):
                    t.wait_ge(S["s_logp"], i * 10 + k // 5 * 2 + k % 5 // 2 + 1)
                else:
                    t.wait_ge(S["s_lo"], i * 15 + k // 5 * 3 + k % 5 // 2 + 1)
                t.wait_ge(S["s_exp"], 2 * s + 2)
                for hf in range(2):
                    c0 = HF * hf
                    t.matmul(bank[4 + hf][:, 0:HF], xn[:, kt, :], p32[s % NP].bitcast(BF16)[:, 2 * c0 + 1:2 * c0 + 2 * HF:2], start=k == 0, stop=False)
                    l = t.matmul(bank[4 + hf][:, 0:HF], xn[:, kt, :], plo[s % NP][:, c0:c0 + HF], start=False, stop=k == TILES - 1)
                l.then_inc(S["s_pv"], 1)

            for i in range(UNITS):
                done = 0
                for k in range(TILES):
                    energies(i, k)
                    s = i * TILES + k - 2
                    if s >= 0:
                        values(s)
                    if k == 3 and i >= 1:
                        finish(i - 1, x_base(i) + 0)
                    if i + 1 < UNITS:
                        if k == 4:
                            q_proj(i + 1, 0, x_base(i) + 1)
                            q_proj(i + 1, 1, x_base(i) + 2)
                        if k >= 6:
                            want = min(UT * NKC, -(-UT * NKC * (k - 5) // 17))
                            while done < want:
                                q_max(i + 1, done, x_base(i) + 3 + done)
                                done += 1
                        if k == 24:
                            max_rows(i + 1, 0, x_base(i) + 38)
                            max_rows(i + 1, 1, x_base(i) + 39)
            values(UNITS * TILES - 2)
            values(UNITS * TILES - 1)
            finish(UNITS - 1, x_base(UNITS - 1) + 1)
            t.wait_ge(S["s_r"], 1)
            for b in range(B):
                l = t.matmul(bank[6][0:64, b:b + 1], acc3[:, b, :], ones[:, 0:1], start=True, stop=True)
            l.then_inc(S["s_rc"], 1)
            t.wait_ge(S["s_r"], 2)
            t.matmul(bank[6][0:B, 16:16 + NE], acc3t[0:64, :], wr[:, :], start=True, stop=True).then_inc(S["s_rc"], 1)
            t.wait_ge(S["s_r"], 3)
            t.matmul(bank[6][0:B, 32:32 + NE], ones[0:B, 0:B], rt[0:B, 0:NE], start=True, stop=True).then_inc(S["s_rc"], 1)
            t.wait_ge(S["s_r"], 4)
            t.matmul(bank[6][:, 64:64 + 4 * B * NE], ones[0:B, :], cf[0:B, :], start=True, stop=True).then_inc(S["s_rc"], 1)
            for u in range(UNITS):
                t.wait_ge(S["s_x3"], u + 1)
                if u >= 2:
                    t.wait_ge(S["s_xt3"], u - 1)
                for i in range(UT):
                    l = t.transpose(bank[u % 2][:, :].bitcast(F16)[:, i * 128:i * 128 + 128], xn3[:, i, :], id16[:, :])
                l.then_inc(S["s_x3p"], 1)
                t.wait_ge(S["s_xt3"], u + 1)
                if u == 0:
                    t.wait_ge(S["s_w1"], 1)
                for k in range(2):
                    for hf in range(2):
                        n = 2 * k + hf
                        if u >= 1:
                            t.wait_ge(S["s_hs"], 4 * (u - 1) + n + 1)
                        for j in range(3):
                            l = t.matmul(bank[2 + n][:, 0:HF], w1s[:, 2 * (u // UPB) + k, j, :], xt3[u % 2][:, HF * hf:HF * hf + HF], start=j == 0, stop=j == 2)
                        l.then_inc(S["s_hp"], 1)
                t.wait_ge(S["s_hs"], 4 * u + 4)
                if u >= 2:
                    t.wait_ge(S["s_yd"], u - 1)
                for i in range(UT):
                    for k in range(2):
                        l = t.matmul(bank[6 + u % 2][:, C * i:C * i + C], hs[u % 2][k][:, 128 * i:128 * i + 128], w2s[:, 2 * (u // UPB) + k, :],
                                     start=k == 0, stop=k == 1)
                l.then_inc(S["s_y"], 1)

        @block.vector
        def _(v_):
            v = v_
            ch = Chain(v, "s_v")

            def rsqrt(y, var):
                t0, t1 = ln_s[:, 5 * UT:6 * UT], ln_s[:, 6 * UT:7 * UT]
                ch(v.tensor_scalar(t0.bitcast(I32), var.bitcast(I32), 1, None, ALU.logical_shift_right))
                ch(v.tensor_scalar(y.bitcast(I32), t0.bitcast(I32), -1.0, MAGIC, ALU.mult, ALU.add))
                for _ in range(3):
                    ch(v.tensor_tensor(t0, y, y, ALU.mult))
                    ch(v.tensor_tensor(t1, t0, var, ALU.mult))
                    ch(v.tensor_scalar(t1, t1, -0.5, 1.5, ALU.mult, ALU.add))
                    ch(v.tensor_tensor(y, y, t1, ALU.mult))

            def norm(src, dst, masked):
                s, m, q, var, y = (ln_s[:, j * UT:(j + 1) * UT] for j in range(5))
                c3, q3 = tk(ln_c[:, :]), tk(ln_q[:, :])
                ch(v.tensor_reduce(s, src, AX.X, ALU.add))
                ch(v.tensor_scalar(m, s, 1.0 / C, None, ALU.mult))
                ch(v.tensor_tensor(c3, src, bc(m.rearrange("p (t o) -> p t o", o=1), [128, UT, C]), ALU.subtract))
                ch(v.tensor_tensor(q3, c3, c3, ALU.mult))
                ch(v.tensor_reduce(q, q3, AX.X, ALU.add))
                ch(v.tensor_scalar(var, q, 1.0 / C, EPS, ALU.mult, ALU.add))
                rsqrt(y, var)
                if masked:
                    ch(v.tensor_tensor(y, y, valid[:, :], ALU.mult))
                ch(v.tensor_tensor(dst, c3, bc(y.rearrange("p (t o) -> p t o", o=1), [128, UT, C]), ALU.mult))

            def split(src, dst, n):
                ch(v.tensor_copy(dst[:, :, 0:n], src[:, :, 0:n]))
                return v.tensor_tensor(dst[:, :, C:C + n], src[:, :, 0:n], dst[:, :, 0:n], ALU.subtract)

            v.wait_ge(S["s_set"], 2)
            for u in range(UNITS + 1):
                w = u - 1
                if u < UNITS:
                    v.wait_ge(S["s_qkv"], u + 1)
                    if u >= 1:
                        v.wait_ge(S["s_rep"], u)
                    v.tensor_tensor(v2.rearrange("p (n c) -> p n c", c=128), bank[2][:, 0:384].rearrange("p (n c) -> p n c", c=128),
                                    bc(bvr[:, :].rearrange("p (o c) -> p o c", o=1), [128, 3, 128]), ALU.add).then_inc(S["s_v2"], 1)
                if w >= 0:
                    v.wait_ge(S["s_av"], w + 1)
                    if w >= 1:
                        v.wait_ge(S["s_ot"], w)
                    o3 = o.rearrange("p (t c) -> p t c", c=C)
                    for i, n in ((0, 4), (1, 1)):
                        pr = bank[3 + i][:, 0:128 * n].rearrange("p (t w c) -> p t w c", w=2, c=C)
                        ch(v.tensor_scalar(o3[:, 4 * i:4 * i + n, :], pr[:, :, 0, :], cs[:, C_WIN:C_WIN + 1], None, ALU.mult))
                        l = v.scalar_tensor_tensor(o3[:, 4 * i:4 * i + n, :], pr[:, :, 1, :], cs[:, C_WIN + 1:C_WIN + 2], o3[:, 4 * i:4 * i + n, :],
                                                   ALU.mult, ALU.add)
                        if i == 0:
                            ch(l)
                        else:
                            l.then_inc(S["s_o"], 1)
                if u < UNITS:
                    v.wait_ge(S["s_sc"], u + 1)
                    if u >= 1:
                        v.wait_ge(S["s_ex"], 2 * u)
                    t0 = u % UPB * UT
                    for i, n in ((0, 4), (1, 1)):
                        dst = s1[:, 512 * i:512 * i + 128 * n].rearrange("p (t h k) -> p t h k", h=NH, k=WT)
                        src = bank[5 + i][:, 0:128 * n].rearrange("p (t h k) -> p t h k", h=NH, k=WT)
                        bb = bc(bias[:, t0 + 4 * i:t0 + 4 * i + n, :].rearrange("p t (o k) -> p t o k", o=1), [128, n, NH, WT])
                        l = v.tensor_tensor(dst, src, bb, ALU.add)
                        if i == 0:
                            ch(l)
                        else:
                            l.then_inc(S["s_s1"], 1)
                    v.wait_ge(S["s_s1"], 2 * u + 1)
                    v.tensor_reduce(mx, s1.rearrange("p (n k) -> p n k", k=WT), AX.X, ALU.max).then_inc(S["s_s1"], 1)
                if w >= 0:
                    v.wait_ge(S["s_op"], w + 1)
                    hu = h[:, unit_tiles(w), :]
                    l = v.tensor_tensor(hu, bank[2][:, 0:UT * C].rearrange("p (t c) -> p t c", c=C),
                                        bc(b2r[:, :].rearrange("p (o c) -> p o c", o=1), [128, UT, C]), ALU.add)
                    l.then_inc(S["s_h1"], 1)
                    v.wait_ge(S["s_h1"], w + 1)
                    last = w % UPB == UPB - 1
                    norm(hu, tk(ln_q[:, :]), last)
                    if w >= 1:
                        v.wait_ge(S["s_xn"], 16 * w)
                        v.wait_ge(S["s_xtp"], w)
                    if last or w % UPB == 0 and w:
                        ch(v.tensor_copy(xnu[:, :, 63:64], valid[:, :].rearrange("p (t o) -> p t o", o=1) if last else ones[:, 0:UT].rearrange("p (t o) -> p t o", o=1)))
                    split(tk(ln_q[:, :]), xnu, 63).then_inc(S["s_xnu"], 1)
                if u < UNITS:
                    v.wait_ge(S["s_ex"], 2 * u + 1)
                    if u >= 1:
                        v.wait_ge(S["s_pn"], u)
                    ch(v.tensor_reduce(den, pn.rearrange("p (n k) -> p n k", k=WT), AX.X, ALU.add))
                    v.reciprocal(rden, den).then_inc(S["s_ex"], 1)

            v.wait_ge(S["s_w2"], NW2)
            for wgt in (wq2, wk2, wv2):
                for hf in (1, 0):
                    l = v.tensor_scalar(wgt[:, 64 * hf:64 * hf + 64], wgt[:, 64 * hf:64 * hf + 64], wgt[:, 63:64], None, ALU.subtract)
                    if hf:
                        ch(l)
                l.then_inc(S["s_ab"], 1)
            v.wait_ge(S["s_wvt"], 2)
            ch(v.tensor_copy(wvx[:, 0:64], bank[3][:, 0:64]))
            ch(v.tensor_copy(wvx[:, 64:66], cs[:, C_ID + 63:C_ID + 65]))
            ch(v.tensor_copy(an[:, :], bank[2][:, 0:128]))
            v.tensor_reduce(sc[:, 0:1], an[:, :], AX.X, ALU.max, apply_absolute_value=True).then_inc(S["s_am"], 1)
            v.wait_ge(S["s_am"], 2)
            ch(v.tensor_scalar(sc[:, 1:2], sc[:, 1:2], 1e-30, None, ALU.max))
            ch(v.reciprocal(sc[:, 2:3], sc[:, 1:2]))
            ch(v.tensor_scalar(an[:, :], an[:, :], sc[:, 2:3], None, ALU.mult))
            for j in range(3):
                v.tensor_copy(a3[:, j, :], an[:, :]).then_inc(S["s_a3"], 1)
                if j < 2:
                    v.wait_ge(S["s_a3"], j + 1)
                    ch(v.tensor_tensor(an[:, :], an[:, :], a3[:, j, :], ALU.subtract))
            v.wait_ge(S["s_xn"], 16 * UNITS)
            v.wait_ge(S["s_xt"], UNITS)
            v.wait_ge(S["s_av"], UNITS)
            v.memset(zm, 0.0).then_inc(S["s_p1"], 1)
            v.wait_ge(S["s_p1"], 1)

            def q_low(i, hf, idx):
                v.wait_ge(S["s_qh"], 2 * i + hf + 1)
                c = slice(HF * hf, HF * hf + HF)
                v.tensor_tensor(ql[i % 2][:, c], bank[6 + idx % 2][:, 0:HF], qh[i % 2][:, c], ALU.subtract).then_inc(S["s_xd"], 1)

            def k_max(i, n, idx):
                v.wait_ge(S["s_x"], idx + 1)
                v.tensor_reduce(mxk[:, n // NKC, n % NKC:n % NKC + 1], bank[6 + idx % 2][:, 0:KC], AX.X, ALU.max).then_inc(S["s_xd"], 1)

            def q_shift(i, idx):
                v.wait_ge(S["s_xd"], idx)
                ch(v.tensor_reduce(mq, mxk, AX.X, ALU.max))
                v.tensor_scalar(zm[:, :, 63:64], mq.rearrange("p (t o) -> p t o", o=1), -1.0, None, ALU.mult).then_inc(S["s_lnq"], 1)
                for hf in range(2):
                    v.wait_ge(S["s_x"], idx + hf + 1)
                    if hf == 0:
                        v.wait_ge(S["s_xd"], idx)
                    c = slice(HF * hf, HF * hf + HF)
                    l = v.tensor_tensor(qh[i % 2][32:64, c], bank[6 + (idx + hf) % 2][32:64, 0:HF], qh[i % 2][32:64, c], ALU.add)
                    l.then_inc(S["s_xd"], 1)
                    v.wait_ge(S["s_xd"], idx + hf + 1)

            def close(i, idx):
                v.wait_ge(S["s_x"], idx + 1)
                pr = bank[6 + idx % 2][:, 0:66 * UT].rearrange("p (t c) -> p t c", c=66)
                a3_ = tk(att)
                ch(v.reciprocal(rd.rearrange("p (t o) -> p t o", o=1), pr[:, :, 64:65]))
                ch(v.tensor_scalar(rd, rd, float(C) ** -0.5, None, ALU.mult))
                l = v.tensor_tensor(a3_, pr[:, :, 0:C], bc(rd.rearrange("p (t o) -> p t o", o=1), [128, UT, C]), ALU.mult)
                l.then_inc(S["s_xd"], 1)
                v.wait_ge(S["s_xd"], idx + 1)
                hu = h[:, unit_tiles(i), :]
                ch(v.tensor_tensor(hu, hu, a3_, ALU.add))
                norm(hu, x3[:, unit_tiles(i), :], i % UPB == UPB - 1)

            q_low(0, 0, 0)
            q_low(0, 1, 1)
            for n in range(UT * NKC):
                k_max(0, n, 2 + n)
            q_shift(0, 37)
            for i in range(UNITS):
                done = 0
                for k in range(TILES):
                    s = i * TILES + k
                    if k % 5 not in (1, 3):
                        v.wait_ge(S["s_exp"], 2 * s + 2)
                        if s >= NP:
                            v.wait_ge(S["s_pv"], s - NP + 1)
                        pp = p32[s % NP]
                        v.tensor_tensor(plo[s % NP], pp, pp.bitcast(BF16)[:, 1::2], ALU.subtract).then_inc(S["s_lo"], 1)
                    if k == 4 and i >= 1:
                        close(i - 1, x_base(i))
                    if i + 1 < UNITS:
                        if k == QK:
                            q_low(i + 1, 0, x_base(i) + 1)
                            q_low(i + 1, 1, x_base(i) + 2)
                        if k >= 6:
                            want = min(UT * NKC, -(-UT * NKC * (k - 5) // 17))
                            while done < want:
                                k_max(i + 1, done, x_base(i) + 3 + done)
                                done += 1
                        if k == 24:
                            q_shift(i + 1, x_base(i) + 38)
            close(UNITS - 1, x_base(UNITS - 1) + 1)
            for b in range(B):
                l = v.tensor_reduce(acc3[:, b, :], x3[:, b * TILES:(b + 1) * TILES, :].rearrange("p t c -> p c t"), AX.X, ALU.add)
                if b < B - 1:
                    ch(l)
            l.then_inc(S["s_r"], 1)
            v.wait_ge(S["s_rc"], 1)
            v.tensor_scalar(acc3t[0:64, :], bank[6][0:64, 0:B], 1.0 / NTOK, None, ALU.mult).then_inc(S["s_r"], 1)
            v.wait_ge(S["s_rc"], 2)
            R = lambda j, n=NE: rt[0:B, 8 * j:8 * j + n]
            ch(v.tensor_tensor(R(1), bank[6][0:B, 16:16 + NE], brr[:, :], ALU.add))

            def softmax(src, dst, k):
                ch(v.tensor_reduce(R(2, 1), src, AX.X, ALU.max))
                v.tensor_scalar(R(3), src, R(2, 1), None, ALU.subtract).then_inc(S["s_k1"], 1)
                v.wait_ge(S["s_fx"], k)
                ch(v.tensor_reduce(R(5, 1), R(4), AX.X, ALU.add))
                ch(v.reciprocal(R(6, 1), R(5, 1)))
                return v.tensor_scalar(dst, R(4), R(6, 1), None, ALU.mult)

            softmax(R(1), R(0), 1).then_inc(S["s_r"], 1)
            v.wait_ge(S["s_rc"], 3)
            ch(v.tensor_scalar(R(7), bank[6][0:B, 32:32 + NE], float(NTOK), None, ALU.mult))
            ch(v.tensor_scalar(R(8), R(7), CAPACITY, None, ALU.is_gt))
            ch(v.reciprocal(R(9), R(7)))
            ch(v.tensor_scalar(R(9), R(9), CAPACITY, -1.0, ALU.mult, ALU.add))
            ch(v.tensor_tensor(R(9), R(9), R(8), ALU.mult))
            ch(v.tensor_scalar(R(9), R(9), 1.0, None, ALU.add))
            ch(v.tensor_tensor(R(9), R(9), R(0), ALU.mult))
            ch(softmax(R(9), R(1), 2))
            for k in range(2):
                hot = R(12 + k)
                ch(v.tensor_reduce(R(10 + k, 1), R(1), AX.X, ALU.max))
                ch(v.tensor_scalar(R(14), R(1), R(10 + k, 1), None, ALU.is_equal))
                ch(v.tensor_tensor(R(14), R(14), cs[0:B, C_RANK:C_RANK + NE], ALU.mult))
                ch(v.tensor_reduce(R(15, 1), R(14), AX.X, ALU.max))
                ch(v.tensor_scalar(hot, cs[0:B, C_RANK:C_RANK + NE], R(15, 1), None, ALU.is_equal))
                if k == 0:
                    ch(v.scalar_tensor_tensor(R(1), hot, -2.0, R(1), ALU.mult, ALU.add))
            ch(v.tensor_copy(R(16, 1), R(10, 1)))
            ch(v.tensor_copy(R(16, 2)[:, 1:2], R(11, 1)))
            ch(v.tensor_reduce(R(2, 1), R(16, 2), AX.X, ALU.max))
            v.tensor_scalar(R(17, 2), R(16, 2), R(2, 1), None, ALU.subtract).then_inc(S["s_k1"], 1)
            v.wait_ge(S["s_fx"], 3)
            ch(v.tensor_reduce(R(5, 1), R(18, 2), AX.X, ALU.add))
            ch(v.reciprocal(R(6, 1), R(5, 1)))
            ch(v.tensor_scalar(R(19, 2), R(18, 2), R(6, 1), None, ALU.mult))
            cf4 = cf[0:B, :].rearrange("p (z b k e) -> p z b k e", z=2, b=B, k=2)
            for b in range(B):
                for k in range(2):
                    ch(v.tensor_scalar(cf4[:, 0, b, k, :], R(12 + k), cs[0:B, C_DIAG + b:C_DIAG + b + 1], None, ALU.mult))
                    ch(v.tensor_scalar(cf4[:, 1, b, k, :], cf4[:, 0, b, k, :], R(19, 2)[:, k:k + 1], None, ALU.mult))
            v.tensor_copy(R(2, 1), R(5, 1)).then_inc(S["s_r"], 1)
            v.wait_ge(S["s_rc"], 4)
            ch(v.tensor_copy(cf[:, :], bank[6][:, 64:64 + 4 * B * NE]))
            cz = cf[:, :].rearrange("p (z n e) -> p z n e", z=2, e=NE)
            for n in range(2 * B):
                for e in range(NE):
                    co = cz[:, 0, n, e:e + 1]
                    if e == 0:
                        ch(v.tensor_scalar(w1f, w1d[:, e, :], co, None, ALU.mult))
                    else:
                        ch(v.scalar_tensor_tensor(w1f, w1d[:, e, :], co, w1f, ALU.mult, ALU.add))
                for j in range(3):
                    ch(v.tensor_copy(w1s[:, n, j, :], w1f))
                    if j < 2:
                        ch(v.tensor_tensor(w1f, w1f, w1s[:, n, j, :], ALU.subtract))
                for e in range(NE):
                    cw = cz[:, 1, n, e:e + 1]
                    if e == 0:
                        ch(v.tensor_scalar(w2s[:, n, :], w2d[:, e, :], cw, None, ALU.mult))
                    else:
                        ch(v.scalar_tensor_tensor(w2s[:, n, :], w2d[:, e, :], cw, w2s[:, n, :], ALU.mult, ALU.add))
                ch(v.tensor_tensor(ln_s[:, 0:NE], b1d[:, :], cz[:, 0, n, :], ALU.mult))
                ch(v.tensor_reduce(b1s[:, n:n + 1], ln_s[:, 0:NE], AX.X, ALU.add))
                for e in range(NE):
                    cw = cz[:, 1, n, e:e + 1]
                    if e == 0 and n % 2 == 0:
                        ch(v.tensor_scalar(b2s[:, n // 2, :], fb2r[:, e, :], cw, None, ALU.mult))
                    else:
                        ch(v.scalar_tensor_tensor(b2s[:, n // 2, :], fb2r[:, e, :], cw, b2s[:, n // 2, :], ALU.mult, ALU.add))
            v.tensor_copy(R(2, 1), R(5, 1)).then_inc(S["s_w1"], 1)

            def give(u):
                if u >= 1:
                    v.wait_ge(S["s_x3p"], u)
                split(x3[:, unit_tiles(u), :], xn3, C).then_inc(S["s_x3"], 1)

            give(0)
            stores = [0]
            for u in range(UNITS):
                if u + 1 < UNITS:
                    give(u + 1)
                v.wait_ge(S["s_y"], u + 1)
                if u >= 1:
                    v.wait_ge(S["s_yo"], u)
                b = u // UPB
                x3u, y3 = x3[:, unit_tiles(u), :], tk(y1)
                l = v.tensor_tensor(y3, bank[6 + u % 2][:, 0:UT * C].rearrange("p (t c) -> p t c", c=C), x3u, ALU.add)
                l.then_inc(S["s_yd"], 1)
                v.wait_ge(S["s_yd"], u + 1)
                ch(v.tensor_tensor(y3, y3, bc(b2s[:, b, :].rearrange("p (o c) -> p o c", o=1), [128, UT, C]), ALU.add))
                norm(y3, y3, False)
                ch(v.tensor_tensor(y3, y3, bc(gar[:, :].rearrange("p (o c) -> p o c", o=1), [128, UT, C]), ALU.mult))
                ch(v.tensor_tensor(y3, y3, bc(ber[:, :].rearrange("p (o c) -> p o c", o=1), [128, UT, C]), ALU.add))
                if u >= 2:
                    v.wait_ge(S[f"s_out{u % 2}"], 16 * stored(u - 2))
                v.tensor_tensor(yo[u % 2], y3, h[:, unit_tiles(u), :], ALU.add).then_inc(S["s_yo"], 1)



_W = ["x", "wq_t", "wk_t", "wv_t", "bq", "bk", "bv", "w2_t", "b2", "pos", "Wq", "Wk", "Wv", "Wr", "br", "W1", "b1_t", "W2", "fb2", "gamma", "beta", "cst"]


def kernel(**i):
    import concourse.bacc as bacc
    from concourse.bass_utils import run_bass_kernel_spmd as run

    a = {k: np.asarray(v) for k, v in i.items()}
    w1 = a["L0_tok_w1"].reshape(C, 3, C)
    b1 = a["L0_tok_b1"].reshape(C, 3)
    he = np.arange(C).reshape(C // NH, NH).T.reshape(-1)
    given = {
        "x": a["x"], "wq_t": w1[:, 0].T, "wk_t": w1[:, 1].T, "wv_t": w1[he, 2].T,
        "bq": b1[:, 0:1], "bk": b1[:, 1:2], "bv": b1[he, 2].reshape(1, C), "w2_t": a["L0_tok_w2"].T,
        "b2": a["L0_tok_b2"].reshape(1, C), "pos": a["L0_tok_pos_emb"], "Wq": a["L0_attn_Wq"], "Wk": a["L0_attn_Wk"], "Wv": a["L0_attn_Wv"],
        "Wr": a["L0_ffn_Wr"], "br": a["L0_ffn_br"].reshape(1, NE), "W1": a["L0_ffn_W1"], "b1_t": a["L0_ffn_b1"].T, "W2": a["L0_ffn_W2"],
        "fb2": a["L0_ffn_b2"], "gamma": a["L0_ffn_gamma"].reshape(1, C), "beta": a["L0_ffn_beta"].reshape(1, C), "cst": constants(),
    }
    nc = bacc.Bacc("TRN2", target_bir_lowering=False, num_devices=1)
    arrays, args = {}, []
    for name in _W:
        arrays[f"in_{name}"] = np.ascontiguousarray(given[name])
        args.append(nc.dram_tensor(f"in_{name}", arrays[f"in_{name}"].shape, mybir.dt.from_np(arrays[f"in_{name}"].dtype), kind="ExternalInput").ap())
    args.append(nc.dram_tensor("out", (B, NTOK, C), F32, kind="ExternalOutput").ap())
    vit_tower(nc, *args)
    r = run(nc, [arrays], core_ids=[0])
    return r.results[0]["out"]
```

```python
import math

import numpy as np
import concourse.bass as bass
from concourse import mybir
from contextlib import ExitStack

F32 = mybir.dt.float32
F16 = mybir.dt.float16
BF16 = mybir.dt.bfloat16
I32 = mybir.dt.int32
LOW = F16
ALU = mybir.AluOpType
ACT = mybir.ActivationFunctionType
AX = mybir.AxisListType

B, C, HT = 4, 64, 56
WS, NH = 4, 8
WT = WS * WS
NTOK = HT * HT
NW = HT // WS
NPAIR = NW * NW // 2
TILES = -(-NTOK // 128)
UT = 5
UPB = TILES // UT
UNITS = B * UPB
UP = UT * 4
UC = UP * WT
UTOK = UT * 128
HF = UTOK // 2
NE, NF = 8, 128
EPS = 1e-5
RW = HT + 2
RAWW = 6 + HT * RW + 2
KC = 448
NKC = NTOK // KC
CAPACITY = float(math.ceil(B * NTOK * 1.25 / NE))
MAGIC = float(0x5F3759DF)

C_ID, C_REP, C_HEAD, C_PAR, C_WIN, C_EDGE = 0, 128, 384, 392, 408, 410
C_RANK = C_EDGE + TILES * WT
C_DIAG = C_RANK + NE
C_END = C_DIAG + B


def constants():
    p = np.arange(128)
    c = np.zeros((128, C_END), np.float32)
    c[:, C_ID:C_ID + 128] = np.eye(128)
    for j in range(8):
        m = np.arange(32)
        c[:, C_REP + 32 * j:C_REP + 32 * j + 32] = (p[:, None] // WT == j) & (p[:, None] % WT == m[None] % WT)
    c[:, C_HEAD:C_HEAD + NH] = p[:, None] % NH == np.arange(NH)[None]
    c[:, C_PAR:C_PAR + 16] = p[:, None] % 32 // 16 == np.arange(16)[None] // 8
    c[:, C_WIN:C_WIN + 2] = p[:, None] % 32 // 16 == np.arange(2)[None]
    half = WS // 2
    edge = np.zeros((128, TILES, WT), np.float32)
    for t in range(TILES):
        for q in range(128):
            pair = 4 * t + q // 32
            if pair >= NPAIR:
                continue
            wi, wj = pair // (NW // 2), 2 * (pair % (NW // 2)) + q % 32 // 16
            qi, qj = q % WT // WS, q % WS
            for k in range(WT):
                ki, kj = k // WS, k % WS
                if (wi == NW - 1 and (qi >= half) != (ki >= half)) or (wj == NW - 1 and (qj >= half) != (kj >= half)):
                    edge[q, t, k] = -1e30
    c[:, C_EDGE:C_EDGE + TILES * WT] = edge.reshape(128, -1)
    c[:, C_RANK:C_RANK + NE] = NE - np.arange(NE)[None]
    c[:, C_DIAG:C_DIAG + B] = p[:, None] == np.arange(B)[None]
    return c


def vit_tower(nc, x, wq_t, wk_t, wv_t, bq, bk, bv, w2_t, b2, pos, Wq, Wk, Wv, Wr, br, W1, b1_t, W2, fb2, gamma, beta, cst, out, tok):
    ctx = ExitStack()
    with ctx:
        def sb(name, shape, dt=F32):
            return ctx.enter_context(nc.sbuf_tensor(name, shape, dt))

        def sem(name):
            return ctx.enter_context(nc.semaphore(name))

        bank = [ctx.enter_context(nc.psum_tensor(f"bank{i}", [128, 512], F32)) for i in range(8)]

        xw = sb("xw", [128, UNITS * UC])
        x3 = xw[:, :].rearrange("p (t c) -> p t c", c=C)
        h = sb("h", [128, B * TILES, C])
        xn = sb("xn", [128, B * TILES, 128], F16)
        xt = sb("xt", [128, B * TILES * 128], F16)
        cs = sb("cs", [128, C_END])
        id16 = sb("id16", [128, 128], F16)
        bias = sb("bias", [128, TILES, WT])
        posq = sb("posq", [128, WT])
        valid = sb("valid", [128, UT])
        wqb, wkb, wvb, w2b = (sb(n, [128, 128]) for n in ("wqb", "wkb", "wvb", "w2b"))
        bqc, bkc, bqs = (sb(n, [128, 1]) for n in ("bqc", "bkc", "bqs"))
        bkm = sb("bkm", [128, NH])
        bvr = sb("bvr", [128, 128])
        b2r = sb("b2r", [128, C])
        ident = cs[:, C_ID:C_ID + 128]

        scr = sb("scr", [128, 21900])
        at = [0]

        def cut(n, dt=F32):
            words = n if dt in (F32, I32) else -(-n // 2)
            a = scr[:, at[0]:at[0] + words]
            at[0] += words
            assert at[0] <= 21900, at[0]
            return a if dt == F32 else a.bitcast(dt)

        raw = [cut(RAWW) for _ in range(2)]
        xu = [cut(384) for _ in range(2)]
        qb = [cut(UP * 32).rearrange("p (n q) -> p n q", q=32) for _ in range(2)]
        km = cut(UP * 128).rearrange("p (n h k) -> p n h k", h=NH, k=WT)
        v2 = cut(384)
        rs = cut(768)
        kk = cut(UC)
        vb = [cut(8 * 3 * 2 * C).rearrange("p (n c) -> p n c", c=C) for _ in range(2)]
        s1 = cut(UTOK)
        mx, den, rden = (cut(UT * NH) for _ in range(3))
        pn = cut(UTOK)
        pts = cut(UTOK)
        o = cut(6 * C)
        ots = cut(384)
        rd0 = cut(1)
        xnu = cut(UTOK, F16).rearrange("p (t c) -> p t c", c=128)
        end1 = at[0]
        ln_s = sb("ln_s", [128, 8 * UT])
        ln_c = sb("ln_c", [128, UT * C])
        ln_q = sb("ln_q", [128, UT * C])

        at[0] = 0
        NP = 6
        VLAG = 4
        LEAD = 28
        p32 = [cut(UTOK) for _ in range(NP)]
        plo = [cut(UTOK, LOW) for _ in range(NP)]
        qh = [cut(UTOK, F16) for _ in range(3)]
        ql = [cut(UTOK, F16) for _ in range(3)]
        un = cut(UTOK)
        att = cut(UT * C)
        rd = cut(UT)
        mxk = cut(UT * NKC).rearrange("p (t k) -> p t k", k=NKC)
        mq = cut(UT)
        zm = cut(UT * C, F16).rearrange("p (t c) -> p t c", c=C)
        xn3 = cut(UTOK, F16).rearrange("p (t c) -> p t c", c=128)
        xt3 = [cut(UTOK, F16) for _ in range(2)]
        hs = [[cut(UTOK) for _ in range(2)] for _ in range(2)]
        y1 = cut(UT * C)
        yo = [cut(UT * C).rearrange("p (t c) -> p t c", c=C) for _ in range(2)]
        hl = [[cut(UTOK, LOW) for _ in range(2)] for _ in range(2)]
        y2 = [cut(UT * C) for _ in range(2)]
        w2f = cut(C)
        w1d = cut(NE * NF).rearrange("p (e f) -> p e f", f=NF)
        w2d = cut(NE * C).rearrange("p (e c) -> p e c", c=C)
        b1d = cut(NE)
        fb2r = cut(NE * C).rearrange("p (e c) -> p e c", c=C)
        acc3 = cut(B * C).rearrange("p (b c) -> p b c", c=C)
        acc3t = cut(B)
        rt = cut(160)
        cf = cut(2 * B * NE * 2)
        w1f = cut(NF)
        w1s = cut(B * 2 * 3 * NF, BF16).rearrange("p (n j f) -> p n j f", j=3, f=NF)
        w2s = cut(B * 2 * 3 * C, BF16).rearrange("p (n j c) -> p n j c", j=3, c=C)
        b1s = cut(B * 2)
        b2s = cut(B * C).rearrange("p (b c) -> p b c", c=C)

        wq2, wk2, wv2 = (sb(n, [64, 128]) for n in ("wq2", "wk2", "wv2"))
        an = sb("an", [128, 128])
        a3 = sb("a3", [128, 3, 128], BF16)
        wvx = sb("wvx", [128, 66])
        sc = sb("sc", [128, 4])
        wr = sb("wr", [64, NE])
        brr = sb("brr", [B, NE])
        gar, ber = (sb(n, [128, C]) for n in ("gar", "ber"))
        ones = sb("ones", [128, 128])

        names = """s_cst s_w s_w2 s_raw s_raw1 s_wrap s_xw s_v s_a s_g s_set s_xu s_qkv s_qb s_km s_v2 s_rep s_rs s_vb s_sc s_s1 s_s2 s_ex s_pn
            s_pt s_pts s_av s_o s_ot s_ots s_op s_h1 s_xnu s_xtp s_xt s_xn s_p1
            s_w3 s_w2b s_kk s_vbp s_vba s_k2 s_pos s_tok0 s_tok1 s_hl s_y2 s_w0 s_ab s_am s_a3 s_wvt s_e s_exp s_lo s_logp s_pv s_un s_x s_xd s_qh s_lnq s_p2 s_fx
            s_r s_rc s_w1 s_x3 s_x3p s_xt3 s_hp s_hs s_y s_yd s_yo s_out0 s_out1 s_k0 s_k1""".split()
        S = {n: sem(n) for n in names}
        block = ctx.enter_context(nc.Block())

        class Chain:

            def __init__(self, eng, name):
                self.eng, self.sem, self.n = eng, S[name], 0

            def __call__(self, ins):
                self.n += 1
                ins.then_inc(self.sem, 1)
                self.eng.wait_ge(self.sem, self.n)

        def halves(ap):
            return ap.rearrange("p (n q) -> p n q", q=WT)

        def bc(ap, shape):
            return ap.to_broadcast(shape)

        def tk(ap, c=C):
            return ap.rearrange("p (t c) -> p t c", c=c)

        def unit_tiles(u):
            return slice(u * UT, u * UT + UT)

        jobs, njobs, query_job, shift_job, finish_job = {}, 0, {}, {}, {}
        for g in range(-LEAD, UNITS * TILES):
            jobs[g] = []
            for j in range(UNITS):
                k = g - TILES * j
                if k == TILES + VLAG + 2 and j < UNITS - 1:
                    finish_job[j] = njobs
                    jobs[g].append(("F", j, 0, njobs))
                    njobs += 1
                if k == -2:
                    shift_job[j] = njobs
                    for hf in range(2):
                        jobs[g].append(("T", j, hf, njobs))
                        njobs += 1
                if k == -LEAD:
                    query_job[j] = njobs
                    for hf in range(2):
                        jobs[g].append(("Q", j, hf, njobs))
                        njobs += 1
                for n in range(UT * NKC):
                    if k == 1 - LEAD + n * 24 // (UT * NKC):
                        jobs[g].append(("M", j, n, njobs))
                        njobs += 1
        finish_job[UNITS - 1] = njobs

        def pool_low(s):
            return s % 5 in (0, 2, 4)

        def lows(s):
            return s // 5 * (3 if pool_low(s) else 2) + s % 5 // 2 + 1

        @block.sync
        def _(sp):
            def load_x(b):
                for hf in range(2):
                    off = 4 * (1 - hf)
                    im = raw[b % 2][64 * hf:64 * hf + 64, off:off + HT * RW].rearrange("p (r c) -> p r c", c=RW)
                    sp.dma_start(im[:, 0:HT - 2, 0:HT], x[b, :, 2:HT, :]).then_inc(S[f"s_raw{b % 2 or ''}"], 16)
                    sp.dma_start(im[:, HT - 2:HT, 0:HT], x[b, :, 0:2, :]).then_inc(S[f"s_raw{b % 2 or ''}"], 16)

            load_x(0)
            sp.wait_ge(S["s_k0"], 1)
            for w, s in ((wqb, wq_t), (wkb, wk_t), (wvb, wv_t), (w2b, w2_t)):
                for hf in range(2):
                    sp.dma_start(w[64 * hf:64 * hf + 64, 64 * hf:64 * hf + 64], s).then_inc(S["s_w"], 16)
            for d, s in ((bqc, bq), (bkc, bk)):
                for hf in range(2):
                    sp.dma_start(d[64 * hf:64 * hf + 64, :], s).then_inc(S["s_w"], 16)
            for hf in range(2):
                sp.dma_start(bvr[:, 64 * hf:64 * hf + 64], bv.to_broadcast([128, C])).then_inc(S["s_w"], 16)
            sp.dma_start(b2r[:, :], b2.to_broadcast([128, C])).then_inc(S["s_w"], 16)
            load_x(1)
            for d, s in ((wq2, Wq), (wk2, Wk), (wv2, Wv)):
                for hf in range(2):
                    sp.dma_start(d[:, 64 * hf:64 * hf + 64], s).then_inc(S["s_w2"], 16)
            sp.dma_start(wr[:, :], Wr).then_inc(S["s_w2"], 16)
            sp.dma_start(brr[:, :], br.to_broadcast([B, NE])).then_inc(S["s_w2"], 16)
            sp.dma_start(gar[:, :], gamma.to_broadcast([128, C])).then_inc(S["s_w2"], 16)
            sp.dma_start(ber[:, :], beta.to_broadcast([128, C])).then_inc(S["s_w2"], 16)
            for u in range(UNITS):
                b = (u + 7) // UPB
                if u % UPB == 3 and b < B:
                    sp.wait_ge(S["s_xw"], NW * (b - 1))
                    load_x(b)
                sp.wait_ge(S["s_xnu"], u + 1)
                sp.dma_start(xn[:, unit_tiles(u), :], xnu).then_inc(S["s_xn"], 16)
            sp.wait_ge(S["s_p1"], 1)
            for hf in range(2):
                sp.dma_start(w1d[64 * hf:64 * hf + 64], W1.rearrange("e d f -> d e f")).then_inc(S["s_w3"], 16)
            sp.dma_start(w2d, W2.rearrange("e f d -> f e d")).then_inc(S["s_w3"], 16)
            sp.dma_start(b1d, b1_t).then_inc(S["s_w3"], 16)
            sp.dma_start(fb2r, fb2.rearrange("(o e) d -> o e d", o=1).to_broadcast([128, NE, C])).then_inc(S["s_w3"], 16)

            def bands(u):
                sp.wait_ge(S[f"s_tok{u % 2}"], 16 * (u // 2 + 1))
                b, s_ = u // UPB, u % UPB
                for a_ in range(8 * UT * s_ // NW, min(NW, 8 * UT * (s_ + 1) // NW)):
                    dst = out[b].rearrange("(a i b j) c -> a b i (j c)", a=NW, i=WS, b=NW)[a_]
                    src = tok[b].rearrange("(n i j) c -> n i (j c)", i=WS, j=WS)[a_ * NW:(a_ + 1) * NW]
                    sp.dma_start(dst, src).then_inc(S["s_out0"], 16)

            for u in range(UNITS):
                sp.wait_ge(S["s_yo"], u + 1)
                dst = tok[u // UPB].rearrange("(t p) c -> p t c", p=128)[:, u % UPB * UT:u % UPB * UT + UT, :]
                sp.dma_start(dst, yo[u % 2]).then_inc(S[f"s_tok{u % 2}"], 16)
                if u >= 1:
                    bands(u - 1)
            bands(UNITS - 1)
            sp.wait_ge(S["s_out0"], 16 * B * NW)

        NW1 = 16 * (8 + 4 + 2 + 1)
        NW2 = 16 * (6 + 4)

        @block.gpsimd
        def _(g):
            ch = Chain(g, "s_g")
            for b in range(B):
                ch(g.memset(xw[:, b * UPB * UC + NPAIR * WT:(b + 1) * UPB * UC], 0.0))
            ch(g.memset(ones[:, :], 1.0))
            ch(g.memset(valid[:, :], 1.0))
            ch(g.memset(valid[64:128, UT - 1:UT], 0.0))
            g.wait_ge(S["s_cst"], 16)
            g.tensor_copy(id16[:, :], ident).then_inc(S["s_set"], 1)
            g.wait_ge(S["s_set"], 1)

            def wrap(b):
                g.wait_ge(S[f"s_raw{b % 2 or ''}"], 64 * (b // 2 + 1))
                rows = raw[b % 2][64:128, 0:HT * RW].rearrange("p (r c) -> p r c", c=RW)
                ch(g.tensor_copy(rows[:, :, HT:HT + 2], rows[:, :, 0:2]))

            def order(b, wi):
                band = raw[b % 2][:, 6 + wi * WS * RW:6 + (wi + 1) * WS * RW].rearrange("p (i c) -> p i c", c=RW)
                src = band[:, :, 0:56].rearrange("p i (m q) -> p m i q", q=8)[:, :, :, 0:4]
                at0 = b * UPB * UC + wi * (NW // 2) * WT
                dst = xw[:, at0:at0 + (NW // 2) * WT].rearrange("p (m i q) -> p m i q", i=WS, q=WS)
                g.tensor_copy(dst, src).then_inc(S["s_xw"], 1)
                g.wait_ge(S["s_xw"], NW * b + wi + 1)

            def v_mask(u):
                g.wait_ge(S["s_rs"], u + 1)
                if u >= 2:
                    g.wait_ge(S["s_av"], u - 1)
                for q in range(2):
                    r = slice(32 * q, 32 * q + 32)
                    g.tensor_tensor(vb[u % 2][r, :, 16 * q:16 * q + 16], rs[r, :].rearrange("p (n c) -> p n c", c=16),
                                    bc(cs[r, C_PAR:C_PAR + 16].rearrange("p (o c) -> p o c", o=1), [32, 48, 16]), ALU.mult).then_inc(S["s_vbp"], 1)
                    g.wait_ge(S["s_vbp"], 2 * u + q + 1)

            def s_shift(u):
                g.wait_ge(S["s_s1"], 2 * u + 2)
                s = s1.rearrange("p (n k) -> p n k", k=WT)
                g.tensor_tensor(s, s, bc(mx.rearrange("p (n o) -> p n o", o=1), [128, UT * NH, WT]), ALU.subtract).then_inc(S["s_s2"], 1)
                g.wait_ge(S["s_s2"], u + 1)

            def p_norm(u):
                g.wait_ge(S["s_ex"], 2 * u + 2)
                g.tensor_tensor(pn.rearrange("p (n k) -> p n k", k=WT), pn.rearrange("p (n k) -> p n k", k=WT),
                                bc(rden.rearrange("p (n o) -> p n o", o=1), [128, UT * NH, WT]), ALU.mult).then_inc(S["s_pn"], 1)
                g.wait_ge(S["s_pn"], u + 1)

            wrap(0)
            for wi in range(NW):
                order(0, wi)
                if wi == 5:
                    g.wait_ge(S["s_pos"], 16 * WT)
                    g.tensor_tensor(bias[:, :, :], cs[:, C_EDGE:C_EDGE + TILES * WT].rearrange("p (t k) -> p t k", k=WT),
                                    bc(posq[:, :].rearrange("p (o k) -> p o k", o=1), [128, TILES, WT]), ALU.add).then_inc(S["s_set"], 1)
                    g.wait_ge(S["s_set"], 2)
            for u in range(UNITS + 1):
                if u >= 1:
                    s_shift(u - 1)
                    p_norm(u - 1)
                if u < UNITS:
                    v_mask(u)
                    b, s_ = u // UPB + 1, u % UPB
                    if b < B:
                        if s_ == 0:
                            wrap(b)
                        for wi in range(3 * s_, min(NW, 3 * s_ + 3)):
                            order(b, wi)
            g.wait_ge(S["s_am"], 1)
            g.partition_all_reduce(sc[:, 1:2], sc[:, 0:1], 128, bass.bass_isa.ReduceOp.max).then_inc(S["s_am"], 1)
            for s in range(UNITS * TILES):
                if pool_low(s):
                    g.wait_ge(S["s_exp"], 2 * s + 2)
                    if s >= NP:
                        g.wait_ge(S["s_pv"], s - NP + 1)
                    pp = p32[s % NP]
                    g.tensor_tensor(plo[s % NP], pp, pp.bitcast(BF16)[:, 1::2], ALU.subtract).then_inc(S["s_logp"], 1)
                    g.wait_ge(S["s_logp"], lows(s))

            def out_rest(u):
                g.wait_ge(S["s_y2"], u + 1)
                y3 = tk(y2[u % 2])
                ch(g.tensor_tensor(y3, y3, bc(gar[:, :].rearrange("p (o c) -> p o c", o=1), [128, UT, C]), ALU.mult))
                ch(g.tensor_tensor(y3, y3, bc(ber[:, :].rearrange("p (o c) -> p o c", o=1), [128, UT, C]), ALU.add))
                if u >= 2:
                    g.wait_ge(S[f"s_tok{u % 2}"], 16 * (u // 2))
                g.tensor_tensor(yo[u % 2], y3, h[:, unit_tiles(u), :], ALU.add).then_inc(S["s_yo"], 1)
                g.wait_ge(S["s_yo"], u + 1)

            for u in range(UNITS):
                for k in range(2):
                    g.wait_ge(S["s_hs"], 4 * u + 2 * k + 2)
                    if u >= 2:
                        g.wait_ge(S["s_y"], u - 1)
                    hh = hs[u % 2][k]
                    g.tensor_tensor(hl[u % 2][k], hh, hh.bitcast(BF16)[:, 1::2], ALU.subtract).then_inc(S["s_hl"], 1)
                    g.wait_ge(S["s_hl"], 2 * u + k + 1)
                if u >= 1:
                    out_rest(u - 1)
            out_rest(UNITS - 1)

        @block.scalar
        def _(a):
            ch = Chain(a, "s_a")
            a.dma_start(cs[:, :], cst).then_inc(S["s_cst"], 16)
            for q in range(WT):
                qi, qj = q // WS, q % WS
                src = pos[3 - qi:7 - qi, 3 - qj:7 - qj].rearrange("(o a) b -> o a b", o=1).to_broadcast([8, WS, WS])
                a.dma_start(posq[q:q + 7 * 16 + 1:16, :].rearrange("p (a b) -> p a b", b=WS), src).then_inc(S["s_pos"], 16)
            a.wait_ge(S["s_w"], NW1)
            a.wait_ge(S["s_cst"], 16)
            ch(a.activation(bqs[:, :], bqc[:, :], ACT.Copy, scale=float(1 / math.sqrt(C / NH))))

            def x_copy(u):
                b, s_ = u // UPB, u % UPB
                a.wait_ge(S["s_xw"], NW * b + min(NW, -(-UP * (s_ + 1) // (NW // 2))))
                if u >= 2:
                    a.wait_ge(S["s_qkv"], u - 1)
                a.activation(xu[u % 2][:, 0:UC], xw[:, u * UC:(u + 1) * UC], ACT.Copy).then_inc(S["s_xu"], 1)

            a.wait_ge(S["s_k2"], 1)
            x_copy(0)
            for u in range(UNITS + 3):
                e, f, d = u - 1, u - 2, u - 3
                if 0 <= f < UNITS:
                    a.wait_ge(S["s_pt"], f + 1)
                    if f >= 1:
                        a.wait_ge(S["s_av"], f)
                    for i, n in ((0, 512), (1, 128)):
                        a.activation(pts[:, 512 * i:512 * i + n], bank[3 + i][:, 0:n], ACT.Copy).then_inc(S["s_pts"], 1)
                if u < UNITS:
                    a.wait_ge(S["s_qkv"], u + 1)
                    if u >= 2:
                        a.wait_ge(S["s_sc"], u - 1)
                    for hf in range(2):
                        r = slice(64 * hf, 64 * hf + 64)
                        a.activation(qb[u % 2][r, :, 16 * hf:16 * hf + 16], halves(bank[0][r, 0:UC]), ACT.Identity,
                                     bias=bqs[r, :], scale=float(1 / math.sqrt(C / NH))).then_inc(S["s_qb"], 1)
                    if u >= 1:
                        a.wait_ge(S["s_km"], 8 * u)
                    a.activation(kk, bank[1][:, 0:UC], ACT.Identity, bias=bkc[:, :]).then_inc(S["s_kk"], 1)
                if 0 <= e < UNITS:
                    a.wait_ge(S["s_s2"], e + 1)
                    if e >= 1:
                        a.wait_ge(S["s_pt"], e)
                    a.activation(pn, s1, ACT.Exp).then_inc(S["s_ex"], 1)
                if u < UNITS:
                    a.wait_ge(S["s_rep"], u + 1)
                    if u >= 1:
                        a.wait_ge(S["s_vbp"], 2 * u)
                        a.wait_ge(S["s_vba"], 4 * u)
                    for i in range(2):
                        l = a.activation(rs[:, 384 * i:384 * i + 384], bank[3 + i][:, 0:384], ACT.Copy)
                        if i == 0:
                            ch(l)
                        else:
                            l.then_inc(S["s_rs"], 1)
                if 0 <= f < UNITS:
                    a.wait_ge(S["s_ot"], f + 1)
                    if f >= 1:
                        a.wait_ge(S["s_op"], f)
                    a.activation(ots, bank[7][:, 0:384], ACT.Copy).then_inc(S["s_ots"], 1)
                if u < UNITS:
                    a.wait_ge(S["s_rs"], u + 1)
                    if u >= 2:
                        a.wait_ge(S["s_av"], u - 1)
                    for q in range(2, 4):
                        r = slice(32 * q, 32 * q + 32)
                        for par in range(2):
                            c0 = 16 * q + 8 * par
                            a.activation(vb[u % 2][r, :, c0:c0 + 8], rs[r, :].rearrange("p (n c) -> p n c", c=16)[:, :, 8 * par:8 * par + 8], ACT.Copy,
                                         scale=cs[r, C_WIN + par:C_WIN + par + 1]).then_inc(S["s_vba"], 1)
                if 0 <= d < UNITS:
                    a.wait_ge(S["s_xtp"], d + 1)
                    a.activation(xt[:, d * UTOK:(d + 1) * UTOK], bank[2][:, :].bitcast(F16)[:, 0:UTOK], ACT.Copy).then_inc(S["s_xt"], 1)
                if u + 1 < UNITS:
                    x_copy(u + 1)
            a.wait_ge(S["s_a3"], 3)
            a.wait_ge(S["s_p1"], 1)

            def q_high(i, hf, idx):
                if i >= 3 and hf == 0:
                    a.wait_ge(S["s_e"], 2 * TILES * (i - 2))
                a.wait_ge(S["s_x"], idx + 1)
                a.activation(qh[i % 3][:, HF * hf:HF * hf + HF], bank[6 + idx % 2][:, 0:HF], ACT.Copy).then_inc(S["s_qh"], 1)

            def unnorm(i):
                a.wait_ge(S["s_pv"], (i + 1) * TILES)
                if i >= 1:
                    a.wait_ge(S["s_x"], finish_job[i - 1] + 1)
                for hf in range(2):
                    a.activation(un[:, HF * hf:HF * hf + HF], bank[4 + hf][:, 0:HF], ACT.Copy).then_inc(S["s_un"], 1)

            for g in range(-LEAD, UNITS * TILES):
                for kind, i, n, idx in jobs[g]:
                    if kind == "Q":
                        q_high(i, n, idx)
                if g >= 0:
                    if g % TILES == VLAG and g > TILES:
                        unnorm(g // TILES - 1)
                    if g >= NP:
                        a.wait_ge(S["s_pv"], g - NP + 1)
                    for hf in range(2):
                        a.wait_ge(S["s_e"], 2 * g + hf + 1)
                        a.activation(p32[g % NP][:, HF * hf:HF * hf + HF], bank[(2 * g + hf) % 4][:, 0:HF], ACT.Exp, scale=sc[:, 1:2]).then_inc(S["s_exp"], 1)
            unnorm(UNITS - 1)
            for j, (src, dst, n) in enumerate(((3, 4, NE), (3, 4, NE), (17, 18, 2))):
                a.wait_ge(S["s_k1"], j + 1)
                a.activation(rt[0:B, 8 * dst:8 * dst + n], rt[0:B, 8 * src:8 * src + n], ACT.Exp).then_inc(S["s_fx"], 1)
            for u in range(UNITS):
                a.wait_ge(S["s_x3p"], u + 1)
                if u >= 2:
                    a.wait_ge(S["s_hp"], 4 * (u - 1))
                a.activation(xt3[u % 2], bank[u % 2][:, :].bitcast(F16)[:, 0:UTOK], ACT.Copy).then_inc(S["s_xt3"], 1)
                if u >= 2:
                    a.wait_ge(S["s_y"], u - 1)
                if u % UPB == 0:
                    a.wait_ge(S["s_w1"], 2 * (u // UPB) + 2)
                for k in range(2):
                    for hf in range(2):
                        n = 2 * k + hf
                        a.wait_ge(S["s_hp"], 4 * u + n + 1)
                        bk_ = 2 * (u // UPB) + k
                        a.activation(hs[u % 2][k][:, HF * hf:HF * hf + HF], bank[2 + n][:, 0:HF], ACT.Gelu, bias=b1s[:, bk_:bk_ + 1])\
                            .then_inc(S["s_hs"], 1)

        @block.tensor
        def _(t):
            t.wait_ge(S["s_w"], NW1)
            t.wait_ge(S["s_cst"], 16)
            t.wait_ge(S["s_set"], 1)
            t.wait_ge(S["s_k2"], 1)
            for u in range(UNITS + 3):
                e, f, d = u - 1, u - 2, u - 3
                if 0 <= e < UNITS:
                    t.wait_ge(S["s_qb"], 2 * e + 2)
                    t.wait_ge(S["s_km"], 8 * e + 8)
                    if e >= 1:
                        t.wait_ge(S["s_s1"], 2 * e)
                    for p in range(UP):
                        tt, q = p // 4, p % 4
                        l = t.matmul(bank[5 + tt // 4][32 * q:32 * q + 32, tt % 4 * 128:tt % 4 * 128 + 128],
                                     qb[e % 2][:, p, :], km[:, p, :, :], start=True, stop=True)
                    l.then_inc(S["s_sc"], 1)
                if 0 <= f < UNITS:
                    t.wait_ge(S["s_pn"], f + 1)
                    t.wait_ge(S["s_rs"], min(f + 2, UNITS))
                    for i in range(UT):
                        l = t.transpose(bank[3 + i // 4][:, i % 4 * 128:i % 4 * 128 + 128], pn[:, i * 128:i * 128 + 128], ident)
                    l.then_inc(S["s_pt"], 1)
                if u < UNITS:
                    t.wait_ge(S["s_xu"], u + 1)
                    if u >= 1:
                        t.wait_ge(S["s_qb"], 2 * u)
                        t.wait_ge(S["s_kk"], u)
                        t.wait_ge(S["s_v2"], u)
                    if u >= 3:
                        t.wait_ge(S["s_o"], u - 2)
                    if u >= 4:
                        t.wait_ge(S["s_xt"], u - 3)
                    t.matmul(bank[0][:, 0:UC], wqb[:, :], xw[:, u * UC:(u + 1) * UC], start=True, stop=True)
                    t.matmul(bank[1][:, 0:UC], wkb[:, :], xw[:, u * UC:(u + 1) * UC], start=True, stop=True)
                    for j in range(3):
                        l = t.matmul(bank[2][:, 128 * j:128 * j + 128], xu[u % 2][:, 128 * j:128 * j + 128], wvb[:, :], start=True, stop=True)
                    l.then_inc(S["s_qkv"], 1)
                    t.wait_ge(S["s_v2"], u + 1)
                    if f >= 0:
                        t.wait_ge(S["s_pts"], 2 * f + 2)
                    if u >= 1:
                        t.wait_ge(S["s_rs"], u)
                    for j in range(8):
                        for q in range(4):
                            l = t.matmul(bank[3 + j // 4][32 * q:32 * q + 32, j % 4 * 96:j % 4 * 96 + 96], cs[:, C_REP + 32 * j:C_REP + 32 * j + 32],
                                         v2.rearrange("p (n c) -> p n c", c=C)[:, :, 16 * q:16 * q + 16], start=True, stop=True)
                    l.then_inc(S["s_rep"], 1)
                if 0 <= f < UNITS:
                    t.wait_ge(S["s_pts"], 2 * f + 2)
                    t.wait_ge(S["s_vbp"], 2 * f + 2)
                    t.wait_ge(S["s_vba"], 4 * f + 4)
                    if u < UNITS:
                        t.wait_ge(S["s_qb"], 2 * u + 2)
                        t.wait_ge(S["s_kk"], u + 1)
                    if f >= 1:
                        t.wait_ge(S["s_o"], f)
                    for p in range(UP):
                        tt, q = p // 4, p % 4
                        w0 = (3 * (p % 8) + p // 8) * 2
                        l = t.matmul(bank[tt // 4][32 * q:32 * q + 32, tt % 4 * 128:tt % 4 * 128 + 128],
                                     pts[:, tt * 128 + 32 * q:tt * 128 + 32 * q + 32], vb[f % 2][:, w0:w0 + 2, :], start=True, stop=True)
                    l.then_inc(S["s_av"], 1)
                    t.wait_ge(S["s_o"], f + 1)
                    if f >= 1:
                        t.wait_ge(S["s_h1"], f)
                    for j in range(3):
                        l = t.transpose(bank[7][:, 128 * j:128 * j + 128], o[:, 128 * j:128 * j + 128], ident)
                    l.then_inc(S["s_ot"], 1)
                if 0 <= d < UNITS:
                    t.wait_ge(S["s_xnu"], d + 1)
                    t.wait_ge(S["s_v2"], min(u + 1, UNITS))
                    if d >= 1:
                        t.wait_ge(S["s_xt"], d)
                    for i in range(UT):
                        l = t.transpose(bank[2][:, :].bitcast(F16)[:, i * 128:i * 128 + 128], xnu[:, i, :], id16[:, :])
                    l.then_inc(S["s_xtp"], 1)
                if 0 <= f < UNITS:
                    t.wait_ge(S["s_ots"], f + 1)
                    for j in range(3):
                        l = t.matmul(bank[7][:, 128 * j:128 * j + 128], ots[:, 128 * j:128 * j + 128], w2b[:, :], start=True, stop=True)
                    l.then_inc(S["s_op"], 1)
            t.wait_ge(S["s_ab"], 3)
            t.wait_ge(S["s_xt"], UNITS)
            t.matmul(bank[2][:, 0:128], wq2[:, :], wk2[:, :], start=True, stop=True).then_inc(S["s_wvt"], 1)
            t.transpose(bank[3][:, 0:64], wv2[:, :], cs[0:64, C_ID:C_ID + 64]).then_inc(S["s_wvt"], 1)
            t.wait_ge(S["s_a3"], 3)
            t.wait_ge(S["s_p1"], 1)
            t.wait_ge(S["s_xt"], UNITS)
            t.wait_ge(S["s_xn"], 16 * UNITS)

            def xslot(idx):
                if idx >= 2:
                    t.wait_ge(S["s_xd"], idx - 1)
                return bank[6 + idx % 2]

            def q_proj(i, hf, idx):
                bk_ = xslot(idx)
                c0 = i * UTOK + hf * HF
                for j in range(3):
                    l = t.matmul(bk_[:, 0:HF], a3[:, j, :], xt[:, c0:c0 + HF], start=j == 0, stop=j == 2)
                l.then_inc(S["s_x"], 1)

            def q_max(i, n, idx):
                tt, kc = n // NKC, n % NKC
                bk_ = xslot(idx)
                c0 = i // UPB * TILES * 128 + kc * KC
                if n == 0:
                    t.wait_ge(S["s_qh"], 2 * i + 2)
                t.matmul(bk_[:, 0:KC], qh[i % 3][:, tt * 128:tt * 128 + 128], xt[:, c0:c0 + KC], start=True, stop=True).then_inc(S["s_x"], 1)

            def max_rows(i, hf, idx):
                t.wait_ge(S["s_lnq"], i + 1)
                bk_ = xslot(idx)
                for c0 in (0, 128, 256):
                    lo = hf * HF + c0
                    n = min(128, HF - c0)
                    while n > 0:
                        tt, p0 = lo // 128, lo % 128
                        m = min(n, 128 - p0)
                        l = t.matmul(bk_[0:64, lo - hf * HF:lo - hf * HF + m], zm[:, tt, :], id16[:, p0:p0 + m], start=True, stop=True)
                        lo += m
                        n -= m
                l.then_inc(S["s_x"], 1)

            def finish(i, idx):
                t.wait_ge(S["s_un"], 2 * i + 2)
                bk_ = xslot(idx)
                for j in range(UT):
                    l = t.matmul(bk_[:, 66 * j:66 * j + 66], un[:, 128 * j:128 * j + 128], wvx[:, :], start=True, stop=True)
                l.then_inc(S["s_x"], 1)

            def energies(i, k):
                s = i * TILES + k
                if k == 0:
                    t.wait_ge(S["s_xd"], shift_job[i] + 2)
                kt = i // UPB * TILES + k
                for hf in range(2):
                    n = 2 * s + hf
                    if n >= 4:
                        t.wait_ge(S["s_exp"], n - 3)
                    for j, q in enumerate((qh, ql)):
                        l = t.matmul(bank[n % 4][:, 0:HF], xt[:, kt * 128:kt * 128 + 128], q[i % 3][:, HF * hf:HF * hf + HF], start=j == 0, stop=j == 1)
                    l.then_inc(S["s_e"], 1)

            def values(s):
                i, k = s // TILES, s % TILES
                kt = i // UPB * TILES + k
                if k == 0 and i >= 1:
                    t.wait_ge(S["s_un"], 2 * i)
                t.wait_ge(S["s_logp" if pool_low(s) else "s_lo"], lows(s))
                t.wait_ge(S["s_exp"], 2 * s + 2)
                for hf in range(2):
                    c0 = HF * hf
                    t.matmul(bank[4 + hf][:, 0:HF], xn[:, kt, :], p32[s % NP].bitcast(BF16)[:, 2 * c0 + 1:2 * c0 + 2 * HF:2], start=k == 0, stop=False)
                    l = t.matmul(bank[4 + hf][:, 0:HF], xn[:, kt, :], plo[s % NP][:, c0:c0 + HF], start=False, stop=k == TILES - 1)
                l.then_inc(S["s_pv"], 1)

            for g in range(-LEAD, UNITS * TILES + VLAG):
                if 0 <= g < UNITS * TILES:
                    energies(g // TILES, g % TILES)
                if g >= VLAG:
                    values(g - VLAG)
                for kind, i, n, idx in jobs.get(g, ()):
                    {"Q": lambda: q_proj(i, n, idx), "M": lambda: q_max(i, n, idx), "T": lambda: max_rows(i, n, idx), "F": lambda: finish(i, idx)}[kind]()
            finish(UNITS - 1, finish_job[UNITS - 1])
            t.wait_ge(S["s_r"], 1)
            for b in range(B):
                l = t.matmul(bank[6][0:64, b:b + 1], acc3[:, b, :], ones[:, 0:1], start=True, stop=True)
            l.then_inc(S["s_rc"], 1)
            t.wait_ge(S["s_r"], 2)
            t.matmul(bank[6][0:B, 16:16 + NE], acc3t[0:64, :], wr[:, :], start=True, stop=True).then_inc(S["s_rc"], 1)
            t.wait_ge(S["s_r"], 3)
            t.matmul(bank[6][0:B, 32:32 + NE], ones[0:B, 0:B], rt[0:B, 0:NE], start=True, stop=True).then_inc(S["s_rc"], 1)
            t.wait_ge(S["s_r"], 4)
            t.matmul(bank[6][:, 64:64 + 4 * B * NE], ones[0:B, :], cf[0:B, :], start=True, stop=True).then_inc(S["s_rc"], 1)

            def second(u):
                if u >= 2:
                    t.wait_ge(S["s_yd"], u - 1)
                if u % UPB == 0:
                    t.wait_ge(S["s_w2b"], 2 * (u // UPB) + 2)
                t.wait_ge(S["s_hs"], 4 * u + 4)
                t.wait_ge(S["s_hl"], 2 * u + 2)
                for i in range(UT):
                    for m in range(4):
                        k = m % 2
                        hh = hs[u % 2][k].bitcast(BF16)[:, 256 * i + 1:256 * i + 256:2] if m < 2 else hl[u % 2][k][:, 128 * i:128 * i + 128]
                        for j in range(3):
                            l = t.matmul(bank[6 + u % 2][:, C * i:C * i + C], hh, w2s[:, 2 * (u // UPB) + k, j, :],
                                         start=m == 0 and j == 0, stop=m == 3 and j == 2)
                l.then_inc(S["s_y"], 1)

            for u in range(UNITS):
                t.wait_ge(S["s_x3"], u + 1)
                if u >= 2:
                    t.wait_ge(S["s_xt3"], u - 1)
                for i in range(UT):
                    l = t.transpose(bank[u % 2][:, :].bitcast(F16)[:, i * 128:i * 128 + 128], xn3[:, i, :], id16[:, :])
                l.then_inc(S["s_x3p"], 1)
                t.wait_ge(S["s_xt3"], u + 1)
                if u % UPB == 0:
                    t.wait_ge(S["s_w1"], 2 * (u // UPB) + 2)
                for k in range(2):
                    for hf in range(2):
                        n = 2 * k + hf
                        if u >= 1:
                            t.wait_ge(S["s_hs"], 4 * (u - 1) + n + 1)
                        for j in range(3):
                            l = t.matmul(bank[2 + n][:, 0:HF], w1s[:, 2 * (u // UPB) + k, j, :], xt3[u % 2][:, HF * hf:HF * hf + HF], start=j == 0, stop=j == 2)
                        l.then_inc(S["s_hp"], 1)
                if u >= 1:
                    second(u - 1)
            second(UNITS - 1)

        @block.vector
        def _(v_):
            v = v_
            ch = Chain(v, "s_v")

            def rsqrt(y, var):
                t0, t1 = ln_s[:, 5 * UT:6 * UT], ln_s[:, 6 * UT:7 * UT]
                ch(v.tensor_scalar(t0.bitcast(I32), var.bitcast(I32), 1, None, ALU.logical_shift_right))
                ch(v.tensor_scalar(y.bitcast(I32), t0.bitcast(I32), -1.0, MAGIC, ALU.mult, ALU.add))
                for _ in range(3):
                    ch(v.tensor_tensor(t0, y, y, ALU.mult))
                    ch(v.tensor_tensor(t1, t0, var, ALU.mult))
                    ch(v.tensor_scalar(t1, t1, -0.5, 1.5, ALU.mult, ALU.add))
                    ch(v.tensor_tensor(y, y, t1, ALU.mult))

            def norm(src, dst, masked, signal=None):
                s, m, q, var, y = (ln_s[:, j * UT:(j + 1) * UT] for j in range(5))
                c3, q3 = tk(ln_c[:, :]), tk(ln_q[:, :])
                ch(v.tensor_reduce(s, src, AX.X, ALU.add))
                ch(v.tensor_scalar(m, s, 1.0 / C, None, ALU.mult))
                ch(v.tensor_tensor(c3, src, bc(m.rearrange("p (t o) -> p t o", o=1), [128, UT, C]), ALU.subtract))
                ch(v.tensor_tensor(q3, c3, c3, ALU.mult))
                ch(v.tensor_reduce(q, q3, AX.X, ALU.add))
                ch(v.tensor_scalar(var, q, 1.0 / C, EPS, ALU.mult, ALU.add))
                rsqrt(y, var)
                if masked:
                    ch(v.tensor_tensor(y, y, valid[:, :], ALU.mult))
                l = v.tensor_tensor(dst, c3, bc(y.rearrange("p (t o) -> p t o", o=1), [128, UT, C]), ALU.mult)
                if signal is None:
                    ch(l)
                else:
                    l.then_inc(signal, 1)

            def split(src, dst, n):
                ch(v.tensor_copy(dst[:, :, 0:n], src[:, :, 0:n]))
                return v.tensor_tensor(dst[:, :, C:C + n], src[:, :, 0:n], dst[:, :, 0:n], ALU.subtract)

            for w in (wqb, wkb, wvb, w2b):
                ch(v.memset(w[:, :], 0.0))
            ch(v.memset(o, 0.0))
            v.memset(rd0, 0.0).then_inc(S["s_k0"], 1)
            for x_ in xu:
                ch(v.memset(x_, 0.0))
            ch(v.memset(xnu[:, :, :], 1.0))
            for b_ in qb:
                ch(v.memset(b_, 0.0))
            ch(v.memset(vb[0], 0.0))
            v.memset(vb[1], 0.0).then_inc(S["s_k2"], 1)
            v.wait_ge(S["s_k0"], 1)
            v.wait_ge(S["s_cst"], 16)
            v.wait_ge(S["s_w"], NW1)
            for u in range(UNITS + 2):
                e, w = u - 1, u - 2
                if 0 <= e < UNITS:
                    v.wait_ge(S["s_sc"], e + 1)
                    if e >= 1:
                        v.wait_ge(S["s_ex"], 2 * e)
                    if e == 0:
                        v.wait_ge(S["s_set"], 2)
                    t0 = e % UPB * UT
                    for i, n in ((0, 4), (1, 1)):
                        dst = s1[:, 512 * i:512 * i + 128 * n].rearrange("p (t h k) -> p t h k", h=NH, k=WT)
                        src = bank[5 + i][:, 0:128 * n].rearrange("p (t h k) -> p t h k", h=NH, k=WT)
                        bb = bc(bias[:, t0 + 4 * i:t0 + 4 * i + n, :].rearrange("p t (o k) -> p t o k", o=1), [128, n, NH, WT])
                        l = v.tensor_tensor(dst, src, bb, ALU.add)
                        if i == 0:
                            ch(l)
                        else:
                            l.then_inc(S["s_s1"], 1)
                    v.wait_ge(S["s_s1"], 2 * e + 1)
                    v.tensor_reduce(mx, s1.rearrange("p (n k) -> p n k", k=WT), AX.X, ALU.max).then_inc(S["s_s1"], 1)
                if u < UNITS:
                    v.wait_ge(S["s_qkv"], u + 1)
                    if u >= 1:
                        v.wait_ge(S["s_rep"], u)
                    v.tensor_tensor(v2.rearrange("p (n c) -> p n c", c=128), bank[2][:, 0:384].rearrange("p (n c) -> p n c", c=128),
                                    bc(bvr[:, :].rearrange("p (o c) -> p o c", o=1), [128, 3, 128]), ALU.add).then_inc(S["s_v2"], 1)

                def keys(heads):
                    v.wait_ge(S["s_kk"], u + 1)
                    for hh in heads:
                        v.tensor_scalar(km[:, :, hh, :], halves(kk), cs[:, C_HEAD + hh:C_HEAD + hh + 1], None, ALU.mult).then_inc(S["s_km"], 1)

                if u < UNITS:
                    keys(range(4))
                if 0 <= e < UNITS:
                    v.wait_ge(S["s_ex"], 2 * e + 1)
                    if e >= 1:
                        v.wait_ge(S["s_pn"], e)
                    ch(v.tensor_reduce(den, pn.rearrange("p (n k) -> p n k", k=WT), AX.X, ALU.add))
                    v.reciprocal(rden, den).then_inc(S["s_ex"], 1)
                if 0 <= w < UNITS:
                    v.wait_ge(S["s_av"], w + 1)
                    if w >= 1:
                        v.wait_ge(S["s_ot"], w)
                    o3 = o.rearrange("p (t c) -> p t c", c=C)
                    for i, n in ((0, 4), (1, 1)):
                        pr = bank[i][:, 0:128 * n].rearrange("p (t w c) -> p t w c", w=2, c=C)
                        ch(v.tensor_scalar(o3[:, 4 * i:4 * i + n, :], pr[:, :, 0, :], cs[:, C_WIN:C_WIN + 1], None, ALU.mult))
                        l = v.scalar_tensor_tensor(o3[:, 4 * i:4 * i + n, :], pr[:, :, 1, :], cs[:, C_WIN + 1:C_WIN + 2], o3[:, 4 * i:4 * i + n, :],
                                                   ALU.mult, ALU.add)
                        if i == 0:
                            ch(l)
                        else:
                            l.then_inc(S["s_o"], 1)
                if u < UNITS:
                    keys(range(4, 8))
                if 0 <= w < UNITS:
                    v.wait_ge(S["s_op"], w + 1)
                    hu = h[:, unit_tiles(w), :]
                    l = v.tensor_tensor(hu, bank[7][:, 0:UT * C].rearrange("p (t c) -> p t c", c=C),
                                        bc(b2r[:, :].rearrange("p (o c) -> p o c", o=1), [128, UT, C]), ALU.add)
                    l.then_inc(S["s_h1"], 1)
                    v.wait_ge(S["s_h1"], w + 1)
                    last = w % UPB == UPB - 1
                    norm(hu, tk(ln_q[:, :]), last)
                    if w >= 1:
                        v.wait_ge(S["s_xn"], 16 * w)
                        v.wait_ge(S["s_xtp"], w)
                    if last or w % UPB == 0 and w:
                        ch(v.tensor_copy(xnu[:, :, 63:64], valid[:, :].rearrange("p (t o) -> p t o", o=1) if last else ones[:, 0:UT].rearrange("p (t o) -> p t o", o=1)))
                    split(tk(ln_q[:, :]), xnu, 63).then_inc(S["s_xnu"], 1)

            v.wait_ge(S["s_w2"], NW2)
            for wgt in (wq2, wk2, wv2):
                for hf in (1, 0):
                    l = v.tensor_scalar(wgt[:, 64 * hf:64 * hf + 64], wgt[:, 64 * hf:64 * hf + 64], wgt[:, 63:64], None, ALU.subtract)
                    if hf:
                        ch(l)
                l.then_inc(S["s_ab"], 1)
            v.wait_ge(S["s_wvt"], 2)
            ch(v.tensor_copy(wvx[:, 0:64], bank[3][:, 0:64]))
            ch(v.tensor_copy(wvx[:, 64:66], cs[:, C_ID + 63:C_ID + 65]))
            ch(v.tensor_copy(an[:, :], bank[2][:, 0:128]))
            v.tensor_reduce(sc[:, 0:1], an[:, :], AX.X, ALU.max, apply_absolute_value=True).then_inc(S["s_am"], 1)
            v.wait_ge(S["s_am"], 2)
            ch(v.tensor_scalar(sc[:, 1:2], sc[:, 1:2], 1e-30, None, ALU.max))
            ch(v.reciprocal(sc[:, 2:3], sc[:, 1:2]))
            ch(v.tensor_scalar(an[:, :], an[:, :], sc[:, 2:3], None, ALU.mult))
            for j in range(3):
                v.tensor_copy(a3[:, j, :], an[:, :]).then_inc(S["s_a3"], 1)
                if j < 2:
                    v.wait_ge(S["s_a3"], j + 1)
                    ch(v.tensor_tensor(an[:, :], an[:, :], a3[:, j, :], ALU.subtract))
            v.wait_ge(S["s_xn"], 16 * UNITS)
            v.wait_ge(S["s_xt"], UNITS)
            v.wait_ge(S["s_av"], UNITS)
            v.memset(zm, 0.0).then_inc(S["s_p1"], 1)
            v.wait_ge(S["s_p1"], 1)

            def q_low(i, hf, idx):
                v.wait_ge(S["s_qh"], 2 * i + hf + 1)
                c = slice(HF * hf, HF * hf + HF)
                v.tensor_tensor(ql[i % 3][:, c], bank[6 + idx % 2][:, 0:HF], qh[i % 3][:, c], ALU.subtract).then_inc(S["s_xd"], 1)

            def k_max(i, n, idx):
                v.wait_ge(S["s_x"], idx + 1)
                if n == 0 and i >= 1:
                    v.wait_ge(S["s_lnq"], i)
                v.tensor_reduce(mxk[:, n // NKC, n % NKC:n % NKC + 1], bank[6 + idx % 2][:, 0:KC], AX.X, ALU.max).then_inc(S["s_xd"], 1)

            def q_shift(i, n, idx):
                v.wait_ge(S["s_x"], idx + 1)
                c = slice(HF * n, HF * n + HF)
                v.tensor_tensor(qh[i % 3][32:64, c], bank[6 + idx % 2][32:64, 0:HF], qh[i % 3][32:64, c], ALU.add).then_inc(S["s_xd"], 1)

            def top(i):
                v.wait_ge(S["s_xd"], shift_job[i])
                if i >= 1:
                    v.wait_ge(S["s_x"], shift_job[i - 1] + 2)
                ch(v.tensor_reduce(mq, mxk, AX.X, ALU.max))
                v.tensor_scalar(zm[:, :, 63:64], mq.rearrange("p (t o) -> p t o", o=1), -1.0, None, ALU.mult).then_inc(S["s_lnq"], 1)

            def close(i, idx):
                v.wait_ge(S["s_x"], idx + 1)
                pr = bank[6 + idx % 2][:, 0:66 * UT].rearrange("p (t c) -> p t c", c=66)
                a3_ = tk(att)
                ch(v.reciprocal(rd.rearrange("p (t o) -> p t o", o=1), pr[:, :, 64:65]))
                ch(v.tensor_scalar(rd, rd, float(C) ** -0.5, None, ALU.mult))
                l = v.tensor_tensor(a3_, pr[:, :, 0:C], bc(rd.rearrange("p (t o) -> p t o", o=1), [128, UT, C]), ALU.mult)
                l.then_inc(S["s_xd"], 1)
                v.wait_ge(S["s_xd"], idx + 1)
                hu = h[:, unit_tiles(i), :]
                ch(v.tensor_tensor(hu, hu, a3_, ALU.add))
                norm(hu, x3[:, unit_tiles(i), :], i % UPB == UPB - 1)

            def low(s):
                v.wait_ge(S["s_exp"], 2 * s + 2)
                if s >= NP:
                    v.wait_ge(S["s_pv"], s - NP + 1)
                pp = p32[s % NP]
                v.tensor_tensor(plo[s % NP], pp, pp.bitcast(BF16)[:, 1::2], ALU.subtract).then_inc(S["s_lo"], 1)

            for g in range(-LEAD, UNITS * TILES + 1):
                for kind, i, n, idx in jobs.get(g, ()):
                    if kind == "F":
                        close(i, idx)
                    elif kind == "T":
                        if n == 0:
                            top(i)
                        q_shift(i, n, idx)
                    elif kind == "Q":
                        q_low(i, n, idx)
                    else:
                        k_max(i, n, idx)
                if g >= 1 and not pool_low(g - 1):
                    low(g - 1)
            close(UNITS - 1, finish_job[UNITS - 1])
            for b in range(B):
                l = v.tensor_reduce(acc3[:, b, :], x3[:, b * TILES:(b + 1) * TILES, :].rearrange("p t c -> p c t"), AX.X, ALU.add)
                if b < B - 1:
                    ch(l)
            l.then_inc(S["s_r"], 1)
            v.wait_ge(S["s_rc"], 1)
            v.tensor_scalar(acc3t[0:64, :], bank[6][0:64, 0:B], 1.0 / NTOK, None, ALU.mult).then_inc(S["s_r"], 1)
            v.wait_ge(S["s_rc"], 2)
            R = lambda j, n=NE: rt[0:B, 8 * j:8 * j + n]
            ch(v.tensor_tensor(R(1), bank[6][0:B, 16:16 + NE], brr[:, :], ALU.add))

            def softmax(src, dst, k):
                ch(v.tensor_reduce(R(2, 1), src, AX.X, ALU.max))
                v.tensor_scalar(R(3), src, R(2, 1), None, ALU.subtract).then_inc(S["s_k1"], 1)
                v.wait_ge(S["s_fx"], k)
                ch(v.tensor_reduce(R(5, 1), R(4), AX.X, ALU.add))
                ch(v.reciprocal(R(6, 1), R(5, 1)))
                return v.tensor_scalar(dst, R(4), R(6, 1), None, ALU.mult)

            softmax(R(1), R(0), 1).then_inc(S["s_r"], 1)
            v.wait_ge(S["s_rc"], 3)
            ch(v.tensor_scalar(R(7), bank[6][0:B, 32:32 + NE], float(NTOK), None, ALU.mult))
            ch(v.tensor_scalar(R(8), R(7), CAPACITY, None, ALU.is_gt))
            ch(v.reciprocal(R(9), R(7)))
            ch(v.tensor_scalar(R(9), R(9), CAPACITY, -1.0, ALU.mult, ALU.add))
            ch(v.tensor_tensor(R(9), R(9), R(8), ALU.mult))
            ch(v.tensor_scalar(R(9), R(9), 1.0, None, ALU.add))
            ch(v.tensor_tensor(R(9), R(9), R(0), ALU.mult))
            ch(softmax(R(9), R(1), 2))
            for k in range(2):
                hot = R(12 + k)
                ch(v.tensor_reduce(R(10 + k, 1), R(1), AX.X, ALU.max))
                ch(v.tensor_scalar(R(14), R(1), R(10 + k, 1), None, ALU.is_equal))
                ch(v.tensor_tensor(R(14), R(14), cs[0:B, C_RANK:C_RANK + NE], ALU.mult))
                ch(v.tensor_reduce(R(15, 1), R(14), AX.X, ALU.max))
                ch(v.tensor_scalar(hot, cs[0:B, C_RANK:C_RANK + NE], R(15, 1), None, ALU.is_equal))
                if k == 0:
                    ch(v.scalar_tensor_tensor(R(1), hot, -2.0, R(1), ALU.mult, ALU.add))
            ch(v.tensor_copy(R(16, 1), R(10, 1)))
            ch(v.tensor_copy(R(16, 2)[:, 1:2], R(11, 1)))
            ch(v.tensor_reduce(R(2, 1), R(16, 2), AX.X, ALU.max))
            v.tensor_scalar(R(17, 2), R(16, 2), R(2, 1), None, ALU.subtract).then_inc(S["s_k1"], 1)
            v.wait_ge(S["s_fx"], 3)
            ch(v.tensor_reduce(R(5, 1), R(18, 2), AX.X, ALU.add))
            ch(v.reciprocal(R(6, 1), R(5, 1)))
            ch(v.tensor_scalar(R(19, 2), R(18, 2), R(6, 1), None, ALU.mult))
            cf4 = cf[0:B, :].rearrange("p (z b k e) -> p z b k e", z=2, b=B, k=2)
            for b in range(B):
                for k in range(2):
                    ch(v.tensor_scalar(cf4[:, 0, b, k, :], R(12 + k), cs[0:B, C_DIAG + b:C_DIAG + b + 1], None, ALU.mult))
                    ch(v.tensor_scalar(cf4[:, 1, b, k, :], cf4[:, 0, b, k, :], R(19, 2)[:, k:k + 1], None, ALU.mult))
            v.tensor_copy(R(2, 1), R(5, 1)).then_inc(S["s_r"], 1)
            v.wait_ge(S["s_rc"], 4)
            ch(v.tensor_copy(cf[:, :], bank[6][:, 64:64 + 4 * B * NE]))
            cz = cf[:, :].rearrange("p (z n e) -> p z n e", z=2, e=NE)
            v.wait_ge(S["s_w3"], 16 * 5)

            def choose(n):
                for e in range(NE):
                    co = cz[:, 0, n, e:e + 1]
                    if e == 0:
                        ch(v.tensor_scalar(w1f, w1d[:, e, :], co, None, ALU.mult))
                    else:
                        ch(v.scalar_tensor_tensor(w1f, w1d[:, e, :], co, w1f, ALU.mult, ALU.add))
                for j in range(3):
                    ch(v.tensor_copy(w1s[:, n, j, :], w1f))
                    if j < 2:
                        ch(v.tensor_tensor(w1f, w1f, w1s[:, n, j, :], ALU.subtract))
                ch(v.tensor_tensor(ln_s[:, 0:NE], b1d, cz[:, 0, n, :], ALU.mult))
                v.tensor_reduce(b1s[:, n:n + 1], ln_s[:, 0:NE], AX.X, ALU.add).then_inc(S["s_w1"], 1)
                v.wait_ge(S["s_w1"], n + 1)
                for e in range(NE):
                    cw = cz[:, 1, n, e:e + 1]
                    if e == 0:
                        ch(v.tensor_scalar(w2f, w2d[:, e, :], cw, None, ALU.mult))
                    else:
                        ch(v.scalar_tensor_tensor(w2f, w2d[:, e, :], cw, w2f, ALU.mult, ALU.add))
                    if e == 0 and n % 2 == 0:
                        ch(v.tensor_scalar(b2s[:, n // 2, :], fb2r[:, e, :], cw, None, ALU.mult))
                    else:
                        ch(v.scalar_tensor_tensor(b2s[:, n // 2, :], fb2r[:, e, :], cw, b2s[:, n // 2, :], ALU.mult, ALU.add))
                for j in range(3):
                    l = v.tensor_copy(w2s[:, n, j, :], w2f)
                    if j < 2:
                        ch(l)
                        ch(v.tensor_tensor(w2f, w2f, w2s[:, n, j, :], ALU.subtract))
                    else:
                        l.then_inc(S["s_w2b"], 1)
                        v.wait_ge(S["s_w2b"], n + 1)

            def give(u):
                if u >= 1:
                    v.wait_ge(S["s_x3p"], u)
                split(x3[:, unit_tiles(u), :], xn3, C).then_inc(S["s_x3"], 1)

            give(0)
            choose(0)
            choose(1)
            for u in range(UNITS):
                if u + 1 < UNITS:
                    give(u + 1)
                b = u // UPB
                if b + 1 < B and u % UPB in (1, 3):
                    choose(2 * b + 2 + u % UPB // 2)
                v.wait_ge(S["s_y"], u + 1)
                if u >= 1:
                    v.wait_ge(S["s_y2"], u)
                x3u, y3 = x3[:, unit_tiles(u), :], tk(y1)
                l = v.tensor_tensor(y3, bank[6 + u % 2][:, 0:UT * C].rearrange("p (t c) -> p t c", c=C), x3u, ALU.add)
                l.then_inc(S["s_yd"], 1)
                v.wait_ge(S["s_yd"], u + 1)
                ch(v.tensor_tensor(y3, y3, bc(b2s[:, b, :].rearrange("p (o c) -> p o c", o=1), [128, UT, C]), ALU.add))
                if u >= 2:
                    v.wait_ge(S["s_yo"], u - 1)
                norm(y3, tk(y2[u % 2]), False, S["s_y2"])


_W = ["x", "wq_t", "wk_t", "wv_t", "bq", "bk", "bv", "w2_t", "b2", "pos", "Wq", "Wk", "Wv", "Wr", "br", "W1", "b1_t", "W2", "fb2", "gamma", "beta", "cst"]


def kernel(**i):
    import concourse.bacc as bacc
    from concourse.bass_utils import run_bass_kernel_spmd as run

    a = {k: np.asarray(v) for k, v in i.items()}
    w1 = a["L0_tok_w1"].reshape(C, 3, C)
    b1 = a["L0_tok_b1"].reshape(C, 3)
    he = np.arange(C).reshape(C // NH, NH).T.reshape(-1)
    given = {
        "x": a["x"], "wq_t": w1[:, 0].T, "wk_t": w1[:, 1].T, "wv_t": w1[he, 2].T,
        "bq": b1[:, 0:1], "bk": b1[:, 1:2], "bv": b1[he, 2].reshape(1, C), "w2_t": a["L0_tok_w2"].T,
        "b2": a["L0_tok_b2"].reshape(1, C), "pos": a["L0_tok_pos_emb"], "Wq": a["L0_attn_Wq"], "Wk": a["L0_attn_Wk"], "Wv": a["L0_attn_Wv"],
        "Wr": a["L0_ffn_Wr"], "br": a["L0_ffn_br"].reshape(1, NE), "W1": a["L0_ffn_W1"], "b1_t": a["L0_ffn_b1"].T, "W2": a["L0_ffn_W2"],
        "fb2": a["L0_ffn_b2"], "gamma": a["L0_ffn_gamma"].reshape(1, C), "beta": a["L0_ffn_beta"].reshape(1, C), "cst": constants(),
    }
    nc = bacc.Bacc("TRN2", target_bir_lowering=False, num_devices=1)
    arrays, args = {}, []
    for name in _W:
        arrays[f"in_{name}"] = np.ascontiguousarray(given[name])
        args.append(nc.dram_tensor(f"in_{name}", arrays[f"in_{name}"].shape, mybir.dt.from_np(arrays[f"in_{name}"].dtype), kind="ExternalInput").ap())
    args.append(nc.dram_tensor("out", (B, NTOK, C), F32, kind="ExternalOutput").ap())
    args.append(nc.dram_tensor("tokens", (B, TILES * 128, C), F32, kind="Internal").ap())
    vit_tower(nc, *args)
    r = run(nc, [arrays], core_ids=[0])
    return r.results[0]["out"]
```

```python
import math

import numpy as np
import concourse.bass as bass
from concourse import mybir
from contextlib import ExitStack

F32 = mybir.dt.float32
F16 = mybir.dt.float16
BF16 = mybir.dt.bfloat16
I32 = mybir.dt.int32
LOW = F16
ALU = mybir.AluOpType
ACT = mybir.ActivationFunctionType
AX = mybir.AxisListType

B, C, HT = 4, 64, 56
WS, NH = 4, 8
WT = WS * WS
NTOK = HT * HT
NW = HT // WS
NPAIR = NW * NW // 2
TILES = -(-NTOK // 128)
UT = 5
UPB = TILES // UT
UNITS = B * UPB
UP = UT * 4
UC = UP * WT
UTOK = UT * 128
HF = UTOK // 2
NE, NF = 8, 128
EPS = 1e-5
RW = HT + 2
RAWW = 6 + HT * RW + 2
KC = 448
NKC = NTOK // KC
CAPACITY = float(math.ceil(B * NTOK * 1.25 / NE))
MAGIC = float(0x5F3759DF)

HEAD_ROWS = 20

C_ID, C_REP, C_HEAD, C_PAR, C_WIN, C_EDGE = 0, 128, 384, 392, 408, 410
C_RANK = C_EDGE + TILES * WT
C_DIAG = C_RANK + NE
C_END = C_DIAG + B


def constants():
    p = np.arange(128)
    c = np.zeros((128, C_END), np.float32)
    c[:, C_ID:C_ID + 128] = np.eye(128)
    for j in range(8):
        m = np.arange(32)
        c[:, C_REP + 32 * j:C_REP + 32 * j + 32] = (p[:, None] // WT == j) & (p[:, None] % WT == m[None] % WT)
    c[:, C_HEAD:C_HEAD + NH] = p[:, None] % NH == np.arange(NH)[None]
    c[:, C_PAR:C_PAR + 16] = p[:, None] % 32 // 16 == np.arange(16)[None] // 8
    c[:, C_WIN:C_WIN + 2] = p[:, None] % 32 // 16 == np.arange(2)[None]
    half = WS // 2
    edge = np.zeros((128, TILES, WT), np.float32)
    for t in range(TILES):
        for q in range(128):
            pair = 4 * t + q // 32
            if pair >= NPAIR:
                continue
            wi, wj = pair // (NW // 2), 2 * (pair % (NW // 2)) + q % 32 // 16
            qi, qj = q % WT // WS, q % WS
            for k in range(WT):
                ki, kj = k // WS, k % WS
                if (wi == NW - 1 and (qi >= half) != (ki >= half)) or (wj == NW - 1 and (qj >= half) != (kj >= half)):
                    edge[q, t, k] = -1e30
    c[:, C_EDGE:C_EDGE + TILES * WT] = edge.reshape(128, -1)
    c[:, C_RANK:C_RANK + NE] = NE - np.arange(NE)[None]
    c[:, C_DIAG:C_DIAG + B] = p[:, None] == np.arange(B)[None]
    return c


W_Q, W_K, W_V, W_O, W_BV, W_B2, W_POS, W_BQ, W_BK = 0, 128, 256, 384, 512, 640, 704, 720, 721
W_END = 722


def vit_tower(nc, x, wts, Wq, Wk, Wv, Wr, br, W1, b1_t, W2, fb2, gamma, beta, cst, out, tok):
    ctx = ExitStack()
    with ctx:
        def sb(name, shape, dt=F32):
            return ctx.enter_context(nc.sbuf_tensor(name, shape, dt))

        def sem(name):
            return ctx.enter_context(nc.semaphore(name))

        bank = [ctx.enter_context(nc.psum_tensor(f"bank{i}", [128, 512], F32)) for i in range(8)]

        xw = sb("xw", [128, UNITS * UC])
        x3 = xw[:, :].rearrange("p (t c) -> p t c", c=C)
        h = sb("h", [128, B * TILES, C])
        xn = sb("xn", [128, B * TILES, 128], F16)
        xt = sb("xt", [128, B * TILES * 128], F16)
        cs = sb("cs", [128, C_END])
        id16 = sb("id16", [128, 128], F16)
        bias = sb("bias", [128, TILES, WT])
        wt = sb("wt", [128, W_END])
        posq = wt[:, W_POS:W_POS + WT]
        valid = sb("valid", [128, UT])
        wqb, wkb, wvb, w2b = (wt[:, c:c + 128] for c in (W_Q, W_K, W_V, W_O))
        bqc, bkc = wt[:, W_BQ:W_BQ + 1], wt[:, W_BK:W_BK + 1]
        bvr, b2r = wt[:, W_BV:W_BV + 128], wt[:, W_B2:W_B2 + C]
        bqs = sb("bqs", [128, 1])
        acc3 = sb("acc3", [128, B - 1, C])
        ident = cs[:, C_ID:C_ID + 128]

        scr = sb("scr", [128, 22300])
        at = [0]

        def cut(n, dt=F32):
            words = n if dt in (F32, I32) else -(-n // 2)
            a = scr[:, at[0]:at[0] + words]
            at[0] += words
            assert at[0] <= 22300, at[0]
            return a if dt == F32 else a.bitcast(dt)

        raw = [cut(RAWW) for _ in range(2)]
        xu = [cut(384) for _ in range(2)]
        qb = [cut(UP * 32).rearrange("p (n q) -> p n q", q=32) for _ in range(2)]
        km = cut(UP * 128).rearrange("p (n h k) -> p n h k", h=NH, k=WT)
        v2 = cut(384)
        rs = cut(768)
        kk = cut(UC)
        vb = [cut(8 * 3 * 2 * C).rearrange("p (n c) -> p n c", c=C) for _ in range(2)]
        s1 = cut(UTOK)
        mx, den, rden = (cut(UT * NH) for _ in range(3))
        pn = cut(UTOK)
        pts = cut(UTOK)
        o = cut(6 * C)
        ots = cut(384)
        xnu = cut(UTOK, F16).rearrange("p (t c) -> p t c", c=128)
        ln_s = sb("ln_s", [128, 8 * UT])
        ln_c = sb("ln_c", [128, UT * C])
        ln_q = sb("ln_q", [128, UT * C])

        at[0] = 0
        NP = 6
        LOWLAG = 2
        LOWCYC, LOWPOOL = 4, (0, 1, 2)
        VLAG = 4
        LEAD = 30
        p32 = [cut(UTOK) for _ in range(NP)]
        plo = [cut(UTOK, LOW) for _ in range(NP)]
        qh = [cut(UTOK, F16) for _ in range(3)]
        ql = [cut(UTOK, F16) for _ in range(3)]
        un = cut(UTOK)
        att = cut(UT * C)
        rd = cut(UT)
        mxk = [cut(UT * NKC).rearrange("p (t k) -> p t k", k=NKC) for _ in range(2)]
        mq = cut(UT)
        zm = cut(UT * C, F16).rearrange("p (t c) -> p t c", c=C)
        xn3 = [cut(UTOK, F16).rearrange("p (t c) -> p t c", c=128) for _ in range(3)]
        xt3 = [cut(UTOK, F16) for _ in range(2)]
        hs = [[cut(UTOK) for _ in range(2)] for _ in range(2)]
        y1 = cut(UT * C)
        yo = [cut(UT * C).rearrange("p (t c) -> p t c", c=C) for _ in range(2)]
        hl = [[cut(UTOK, LOW) for _ in range(2)] for _ in range(2)]
        y2 = [cut(UT * C) for _ in range(2)]
        w2f = ln_q[:, NF:NF + C]
        wd = cut(NE * (NF + 2 * C)).rearrange("p (e c) -> p e c", e=NE)
        w1d, w2d = wd[:, :, 0:NF], wd[:, :, NF:NF + 2 * C]
        b1d = cut(NE)
        pick = [cut(128) for _ in range(NE)]
        gate = cut(2 * B)
        acc3t = cut(B)
        rt = cut(160)
        cf = cut(2 * B * NE * 2)
        w1f = ln_q[:, 0:NF]
        ln_s3 = [ln_s, cut(6 * UT)]
        ln_c3 = [ln_c[:, :], cut(UT * C)]
        w1s = cut(B * 2 * 3 * NF, BF16).rearrange("p (n j f) -> p n j f", j=3, f=NF)
        w2s = cut(B * 2 * 3 * C, BF16).rearrange("p (n j c) -> p n j c", j=3, c=C)
        b1s = cut(B * 2)
        b2s = cut(B * C).rearrange("p (b c) -> p b c", c=C)

        wq2, wk2, wv2 = (sb(n, [64, 128]) for n in ("wq2", "wk2", "wv2"))
        an = sb("an", [128, 128])
        a3 = sb("a3", [128, 3, 128], BF16)
        wvx = sb("wvx", [128, 66])
        sc = sb("sc", [128, 4])
        wr = sb("wr", [64, NE])
        brr = sb("brr", [B, NE])
        gar, ber = (sb(n, [128, C]) for n in ("gar", "ber"))
        ones = sb("ones", [128, 128])

        S = {n: sem(n) for n in (
            "consts_loaded",
            "win_weights_loaded",
            "glob_weights_loaded",
            "expert_weights_loaded",
            "band_ordered",
            "vector_chain",
            "norm_tail_chain",
            "scalar_chain",
            "gpsimd_chain",
            "setup_done",
            "buffers_zeroed",
            "x_copied",
            "qkv_ready",
            "queries_placed",
            "keys_biased",
            "key_head_masked",
            "values_biased",
            "values_repeated",
            "repeated_copied",
            "values_placed_pool",
            "values_placed_act",
            "win_scores_ready",
            "scores_max_ready",
            "scores_shifted",
            "win_exp_ready",
            "win_probs_ready",
            "probs_transposed",
            "probs_t_copied",
            "win_out_ready",
            "win_out_picked",
            "win_out_transposed",
            "win_out_t_copied",
            "projection_ready",
            "residual_ready",
            "tokens_normed",
            "tokens_stored",
            "tokens_transposed",
            "tokens_t_copied",
            "window_phase_done",
            "glob_weights_centred",
            "glob_products_ready",
            "product_max_ready",
            "product_part_ready",
            "job_computed",
            "job_used",
            "query_high",
            "maxima_ready",
            "energies_ready",
            "exp_ready",
            "low_ready_vector",
            "low_ready_pool",
            "step_added",
            "sums_copied",
            "expert_input_ready",
            "expert_input_high",
            "expert_input_split",
            "expert_input_transposed",
            "expert_input_t_copied",
            "router_step_vector",
            "router_step_tensor",
            "logits_shifted",
            "router_exp_ready",
            "diagonal_ready",
            "expert_added",
            "first_weights_ready",
            "second_weights_ready",
            "hidden_sums_ready",
            "hidden_ready",
            "hidden_low_pool",
            "hidden_low_vector",
            "residual_biased",
            "expert_out_ready",
            "expert_out_read",
            "out_normed",
            "out_ready",
            "out_stored",
            "image_head_loaded",
            "image_loaded0", "image_loaded1",
            "tokens_out0", "tokens_out1",
        )}
        block = ctx.enter_context(nc.Block())

        class Chain:

            def __init__(self, eng, name):
                self.eng, self.sem, self.n = eng, S[name], 0

            def __call__(self, ins, lag=0, meanwhile=None):
                self.n += 1
                ins.then_inc(self.sem, 1)
                if meanwhile:
                    meanwhile()
                if self.n > lag:
                    self.eng.wait_ge(self.sem, self.n - lag)

        def halves(ap):
            return ap.rearrange("p (n q) -> p n q", q=WT)

        def bc(ap, shape):
            return ap.to_broadcast(shape)

        def tk(ap, c=C):
            return ap.rearrange("p (t c) -> p t c", c=c)

        def unit_tiles(u):
            return slice(u * UT, u * UT + UT)

        jobs, njobs, maxima_jobs, shift_job, finish_job = {}, 0, {}, {}, {}
        for g in range(-LEAD, UNITS * TILES):
            jobs[g] = []
            for j in range(UNITS):
                k = g - TILES * j
                for n in range(UT * NKC):
                    if k == 2 - LEAD + n * TILES // (UT * NKC):
                        jobs[g].append(("M", j, n, njobs))
                        njobs += 1
                        maxima_jobs[j] = njobs
            for j in range(UNITS):
                k = g - TILES * j
                if k == TILES + VLAG + 2 and j < UNITS - 1:
                    finish_job[j] = njobs
                    jobs[g].append(("F", j, 0, njobs))
                    njobs += 1
                for kind, first, step in (("T", shift_job, -2), ("Q", {}, -LEAD)):
                    if k == step:
                        first[j] = njobs
                        for hf in range(2):
                            jobs[g].append((kind, j, hf, njobs))
                            njobs += 1
        finish_job[UNITS - 1] = njobs

        def pool_low(s):
            return s % LOWCYC in LOWPOOL

        def lows(s):
            return sum(pool_low(r) == pool_low(s) for r in range(s % LOWCYC + 1)) + s // LOWCYC * (len(LOWPOOL) if pool_low(s) else LOWCYC - len(LOWPOOL))

        def chosen(n):
            return bank[7 if n == 1 else 1]

        @block.sync
        def _(sp):
            def load_x(b):
                head = HEAD_ROWS if b == 0 else 0
                image = []
                for hf in range(2):
                    off = 4 * (1 - hf)
                    image.append(raw[b % 2][64 * hf:64 * hf + 64, off:off + HT * RW].rearrange("p (r c) -> p r c", c=RW))
                    if head:
                        sp.dma_start(image[hf][:, 0:head, 0:HT], x[b, :, 2:2 + head, :]).then_inc(S["image_head_loaded"], 16)
                for hf, im in enumerate(image):
                    sp.dma_start(im[:, head:HT - 2, 0:HT], x[b, :, 2 + head:HT, :]).then_inc(S[f"image_loaded{b % 2}"], 16)
                    sp.dma_start(im[:, HT - 2:HT, 0:HT], x[b, :, 0:2, :]).then_inc(S[f"image_loaded{b % 2}"], 16)

            sp.dma_start(wt[:, :], wts).then_inc(S["win_weights_loaded"], 16)
            load_x(0)
            load_x(1)
            for d, s in ((wq2, Wq), (wk2, Wk), (wv2, Wv)):
                for hf in range(2):
                    sp.dma_start(d[:, 64 * hf:64 * hf + 64], s).then_inc(S["glob_weights_loaded"], 16)
            sp.dma_start(wr[:, :], Wr).then_inc(S["glob_weights_loaded"], 16)
            sp.dma_start(brr[:, :], br.to_broadcast([B, NE])).then_inc(S["glob_weights_loaded"], 16)
            sp.dma_start(gar[:, :], gamma.to_broadcast([128, C])).then_inc(S["glob_weights_loaded"], 16)
            sp.dma_start(ber[:, :], beta.to_broadcast([128, C])).then_inc(S["glob_weights_loaded"], 16)
            for u in range(UNITS):
                b = u // UPB + 2
                if u % UPB == 0 and b < B:
                    sp.wait_ge(S["band_ordered"], NW * (b - 1))
                    load_x(b)
                sp.wait_ge(S["tokens_normed"], u + 1)
                sp.dma_start(xn[:, unit_tiles(u), :], xnu).then_inc(S["tokens_stored"], 16)
            sp.wait_ge(S["window_phase_done"], 1)
            for hf in range(2):
                sp.dma_start(w1d[64 * hf:64 * hf + 64], W1.rearrange("e d f -> d e f")).then_inc(S["expert_weights_loaded"], 16)
            sp.dma_start(w2d[:, :, 0:C], W2.rearrange("e f d -> f e d")).then_inc(S["expert_weights_loaded"], 16)
            sp.dma_start(b1d, b1_t).then_inc(S["expert_weights_loaded"], 16)
            sp.dma_start(w2d[:, :, C:2 * C], fb2.rearrange("(o e) d -> o e d", o=1).to_broadcast([128, NE, C])).then_inc(S["expert_weights_loaded"], 16)

            def bands(u):
                sp.wait_ge(S[f"tokens_out{u % 2}"], 16 * (u // 2 + 1))
                b, s_ = u // UPB, u % UPB
                for a_ in range(8 * UT * s_ // NW, min(NW, 8 * UT * (s_ + 1) // NW)):
                    dst = out[b].rearrange("(a i b j) c -> a b i (j c)", a=NW, i=WS, b=NW)[a_]
                    src = tok[b].rearrange("(n i j) c -> n i (j c)", i=WS, j=WS)[a_ * NW:(a_ + 1) * NW]
                    sp.dma_start(dst, src).then_inc(S["out_stored"], 16)

            for u in range(UNITS):
                sp.wait_ge(S["out_ready"], u + 1)
                dst = tok[u // UPB].rearrange("(t p) c -> p t c", p=128)[:, u % UPB * UT:u % UPB * UT + UT, :]
                sp.dma_start(dst, yo[u % 2]).then_inc(S[f"tokens_out{u % 2}"], 16)
                if u >= 1:
                    bands(u - 1)
            bands(UNITS - 1)
            sp.wait_ge(S["out_stored"], 16 * B * NW)

        NW1 = 16
        NW2 = 16 * (6 + 4)

        @block.gpsimd
        def _(g):
            ch = Chain(g, "gpsimd_chain")
            for b in range(B):
                ch(g.memset(xw[:, b * UPB * UC + NPAIR * WT:(b + 1) * UPB * UC], 0.0))
            ch(g.memset(ones[:, :], 1.0))
            ch(g.memset(valid[:, :], 1.0))
            ch(g.memset(valid[64:128, UT - 1:UT], 0.0))
            g.wait_ge(S["consts_loaded"], 16)
            g.tensor_copy(id16[:, :], ident).then_inc(S["setup_done"], 1)
            g.wait_ge(S["setup_done"], 1)

            def wrap(b, r0=0, r1=HT):
                if r1 < HT:
                    g.wait_ge(S["image_head_loaded"], 32)
                else:
                    g.wait_ge(S[f"image_loaded{b % 2}"], 64 * (b // 2 + 1))
                rows = raw[b % 2][64:128, 0:HT * RW].rearrange("p (r c) -> p r c", c=RW)
                ch(g.tensor_copy(rows[:, r0:r1, HT:HT + 2], rows[:, r0:r1, 0:2]))

            def order(b, wi):
                band = raw[b % 2][:, 6 + wi * WS * RW:6 + (wi + 1) * WS * RW].rearrange("p (i c) -> p i c", c=RW)
                src = band[:, :, 0:56].rearrange("p i (m q) -> p m i q", q=8)[:, :, :, 0:4]
                at0 = b * UPB * UC + wi * (NW // 2) * WT
                dst = xw[:, at0:at0 + (NW // 2) * WT].rearrange("p (m i q) -> p m i q", i=WS, q=WS)
                g.tensor_copy(dst, src).then_inc(S["band_ordered"], 1)
                g.wait_ge(S["band_ordered"], NW * b + wi + 1)

            def v_mask(u):
                g.wait_ge(S["repeated_copied"], u + 1)
                if u >= 2:
                    g.wait_ge(S["win_out_ready"], u - 1)
                for q in range(2):
                    r = slice(32 * q, 32 * q + 32)
                    g.tensor_tensor(vb[u % 2][r, :, 16 * q:16 * q + 16], rs[r, :].rearrange("p (n c) -> p n c", c=16),
                                    bc(cs[r, C_PAR:C_PAR + 16].rearrange("p (o c) -> p o c", o=1), [32, 48, 16]), ALU.mult).then_inc(S["values_placed_pool"], 1)
                    g.wait_ge(S["values_placed_pool"], 2 * u + q + 1)

            def s_shift(u):
                g.wait_ge(S["scores_max_ready"], 2 * u + 2)
                s = s1.rearrange("p (n k) -> p n k", k=WT)
                g.tensor_tensor(s, s, bc(mx.rearrange("p (n o) -> p n o", o=1), [128, UT * NH, WT]), ALU.subtract).then_inc(S["scores_shifted"], 1)
                g.wait_ge(S["scores_shifted"], u + 1)

            def p_norm(u):
                g.wait_ge(S["win_exp_ready"], 2 * u + 2)
                g.tensor_tensor(pn.rearrange("p (n k) -> p n k", k=WT), pn.rearrange("p (n k) -> p n k", k=WT),
                                bc(rden.rearrange("p (n o) -> p n o", o=1), [128, UT * NH, WT]), ALU.mult).then_inc(S["win_probs_ready"], 1)
                g.wait_ge(S["win_probs_ready"], u + 1)

            wrap(0, 0, HEAD_ROWS)
            for wi in range(NW):
                if wi == HEAD_ROWS // WS - 1:
                    wrap(0, HEAD_ROWS)
                order(0, wi)
                if wi == 5:
                    g.wait_ge(S["win_weights_loaded"], NW1)
                    g.tensor_tensor(bias[:, :, :], cs[:, C_EDGE:C_EDGE + TILES * WT].rearrange("p (t k) -> p t k", k=WT),
                                    bc(posq.rearrange("p (o k) -> p o k", o=1), [128, TILES, WT]), ALU.add).then_inc(S["setup_done"], 1)
                    g.wait_ge(S["setup_done"], 2)
            for u in range(UNITS + 1):
                if u >= 1:
                    s_shift(u - 1)
                    p_norm(u - 1)
                if u < UNITS:
                    v_mask(u)
                    b, s_ = u // UPB + 1, u % UPB
                    if b < B:
                        if s_ == 0:
                            wrap(b)
                        for wi in range(3 * s_, min(NW, 3 * s_ + 3)):
                            order(b, wi)
            g.wait_ge(S["product_max_ready"], 1)
            g.partition_all_reduce(sc[:, 1:2], sc[:, 0:1], 128, bass.bass_isa.ReduceOp.max).then_inc(S["product_max_ready"], 1)

            def add_beta(i):
                g.wait_ge(S["expert_input_ready"], i + 1)
                hu = h[:, unit_tiles(i), :]
                ch(g.tensor_tensor(hu, hu, bc(ber[:, :].rearrange("p (o c) -> p o c", o=1), [128, UT, C]), ALU.add))

            g.wait_ge(S["glob_weights_loaded"], NW2)
            for s in range(UNITS * TILES):
                if pool_low(s):
                    g.wait_ge(S["exp_ready"], 2 * s + 2)
                    if s >= NP:
                        g.wait_ge(S["step_added"], s - NP + 1)
                    pp = p32[s % NP]
                    g.tensor_tensor(plo[s % NP], pp, pp.bitcast(BF16)[:, 1::2], ALU.subtract).then_inc(S["low_ready_pool"], 1)
                    g.wait_ge(S["low_ready_pool"], lows(s))
                i = (s - 48) // TILES
                if s % TILES == 48 % TILES and 0 <= i < UNITS - 2:
                    add_beta(i)
            add_beta(UNITS - 2)
            add_beta(UNITS - 1)

            def out_rest(u):
                g.wait_ge(S["out_normed"], u + 1)
                y3 = tk(y2[u % 2])
                ch(g.tensor_tensor(y3, y3, bc(gar[:, :].rearrange("p (o c) -> p o c", o=1), [128, UT, C]), ALU.mult))
                if u >= 2:
                    g.wait_ge(S[f"tokens_out{u % 2}"], 16 * (u // 2))
                g.tensor_tensor(yo[u % 2], y3, h[:, unit_tiles(u), :], ALU.add).then_inc(S["out_ready"], 1)
                g.wait_ge(S["out_ready"], u + 1)

            for u in range(UNITS):
                g.wait_ge(S["expert_input_split"], u + 1)
                g.wait_ge(S["second_weights_ready"], 2 * (u // UPB) + 2)
                x3u = x3[:, unit_tiles(u), :]
                g.tensor_tensor(x3u, x3u, bc(b2s[:, u // UPB, :].rearrange("p (o c) -> p o c", o=1), [128, UT, C]), ALU.add).then_inc(S["residual_biased"], 1)
                for k in range(2 - u % 2):
                    g.wait_ge(S["hidden_ready"], 4 * u + 2 * k + 2)
                    if u >= 2:
                        g.wait_ge(S["expert_out_ready"], u - 1)
                    hh = hs[u % 2][k]
                    g.tensor_tensor(hl[u % 2][k], hh, hh.bitcast(BF16)[:, 1::2], ALU.subtract).then_inc(S["hidden_low_pool"], 1)
                    g.wait_ge(S["hidden_low_pool"], (3 * u + 1) // 2 + k + 1)
                if u >= 2:
                    out_rest(u - 2)
            out_rest(UNITS - 2)
            out_rest(UNITS - 1)

        @block.scalar
        def _(a):
            ch = Chain(a, "scalar_chain")
            a.dma_start(cs[:, :], cst).then_inc(S["consts_loaded"], 16)
            a.wait_ge(S["win_weights_loaded"], NW1)
            a.wait_ge(S["consts_loaded"], 16)
            ch(a.activation(bqs[:, :], bqc, ACT.Copy, scale=float(1 / math.sqrt(C / NH))))

            def x_copy(u):
                b, s_ = u // UPB, u % UPB
                a.wait_ge(S["band_ordered"], NW * b + min(NW, -(-UP * (s_ + 1) // (NW // 2))))
                if u >= 2:
                    a.wait_ge(S["qkv_ready"], u - 1)
                a.activation(xu[u % 2][:, 0:UC], xw[:, u * UC:(u + 1) * UC], ACT.Copy).then_inc(S["x_copied"], 1)

            a.wait_ge(S["buffers_zeroed"], 1)
            x_copy(0)
            for u in range(UNITS + 4):
                e, f, d, g = u - 1, u - 2, u - 3, u - 4
                if 0 <= d < UNITS:
                    a.wait_ge(S["win_out_transposed"], d + 1)
                    if d >= 1:
                        a.wait_ge(S["projection_ready"], d)
                    a.activation(ots, bank[7][:, 0:384], ACT.Copy).then_inc(S["win_out_t_copied"], 1)
                if 0 <= f < UNITS:
                    a.wait_ge(S["probs_transposed"], f + 1)
                    if f >= 1:
                        a.wait_ge(S["win_out_ready"], f)
                    for i, n in ((0, 512), (1, 128)):
                        a.activation(pts[:, 512 * i:512 * i + n], bank[3 + i][:, 0:n], ACT.Copy).then_inc(S["probs_t_copied"], 1)
                if u < UNITS:
                    a.wait_ge(S["qkv_ready"], u + 1)
                    if u >= 2:
                        a.wait_ge(S["win_scores_ready"], u - 1)
                    for hf in range(2):
                        r = slice(64 * hf, 64 * hf + 64)
                        a.activation(qb[u % 2][r, :, 16 * hf:16 * hf + 16], halves(bank[0][r, 0:UC]), ACT.Identity,
                                     bias=bqs[r, :], scale=float(1 / math.sqrt(C / NH))).then_inc(S["queries_placed"], 1)
                    if u >= 1:
                        a.wait_ge(S["key_head_masked"], 8 * u)
                    a.activation(kk, bank[1][:, 0:UC], ACT.Identity, bias=bkc).then_inc(S["keys_biased"], 1)
                if 0 <= e < UNITS:
                    a.wait_ge(S["scores_shifted"], e + 1)
                    if e >= 1:
                        a.wait_ge(S["probs_transposed"], e)
                    a.activation(pn, s1, ACT.Exp).then_inc(S["win_exp_ready"], 1)
                if u < UNITS:
                    a.wait_ge(S["values_repeated"], u + 1)
                    if u >= 1:
                        a.wait_ge(S["values_placed_pool"], 2 * u)
                        a.wait_ge(S["values_placed_act"], 4 * u)
                    for i in range(2):
                        l = a.activation(rs[:, 384 * i:384 * i + 384], bank[3 + i][:, 0:384], ACT.Copy)
                        if i == 0:
                            ch(l)
                        else:
                            l.then_inc(S["repeated_copied"], 1)
                if u < UNITS:
                    a.wait_ge(S["repeated_copied"], u + 1)
                    if u >= 2:
                        a.wait_ge(S["win_out_ready"], u - 1)
                    for q in range(2, 4):
                        r = slice(32 * q, 32 * q + 32)
                        for par in range(2):
                            c0 = 16 * q + 8 * par
                            a.activation(vb[u % 2][r, :, c0:c0 + 8], rs[r, :].rearrange("p (n c) -> p n c", c=16)[:, :, 8 * par:8 * par + 8], ACT.Copy,
                                         scale=cs[r, C_WIN + par:C_WIN + par + 1]).then_inc(S["values_placed_act"], 1)
                if 0 <= g < UNITS:
                    a.wait_ge(S["tokens_transposed"], g + 1)
                    a.activation(xt[:, g * UTOK:(g + 1) * UTOK], bank[2][:, :].bitcast(F16)[:, 0:UTOK], ACT.Copy).then_inc(S["tokens_t_copied"], 1)
                if u + 1 < UNITS:
                    x_copy(u + 1)
            a.wait_ge(S["product_part_ready"], 3)
            a.wait_ge(S["window_phase_done"], 1)

            def q_high(i, hf, idx):
                if i >= 3 and hf == 0:
                    a.wait_ge(S["energies_ready"], 2 * TILES * (i - 2))
                a.wait_ge(S["job_computed"], idx + 1)
                a.activation(qh[i % 3][:, HF * hf:HF * hf + HF], bank[6 + idx % 2][:, 0:HF], ACT.Copy).then_inc(S["query_high"], 1)

            def unnorm(i):
                a.wait_ge(S["step_added"], (i + 1) * TILES)
                if i >= 1:
                    a.wait_ge(S["job_computed"], finish_job[i - 1] + 1)
                for hf in range(2):
                    a.activation(un[:, HF * hf:HF * hf + HF], bank[4 + hf][:, 0:HF], ACT.Copy).then_inc(S["sums_copied"], 1)

            for g in range(-LEAD, UNITS * TILES):
                for kind, i, n, idx in jobs[g]:
                    if kind == "Q":
                        q_high(i, n, idx)
                if g >= 0:
                    if g % TILES == VLAG and g > TILES:
                        unnorm(g // TILES - 1)
                    if g >= NP:
                        a.wait_ge(S["step_added"], g - NP + 1)
                    for hf in range(2):
                        a.wait_ge(S["energies_ready"], 2 * g + hf + 1)
                        a.activation(p32[g % NP][:, HF * hf:HF * hf + HF], bank[(2 * g + hf) % 4][:, 0:HF], ACT.Exp, scale=sc[:, 1:2]).then_inc(S["exp_ready"], 1)
            unnorm(UNITS - 1)
            def x_high(u):
                if u >= 3:
                    a.wait_ge(S["expert_input_transposed"], u - 2)
                a.activation(xn3[u % 3][:, :, 0:C], x3[:, unit_tiles(u), :], ACT.Copy).then_inc(S["expert_input_high"], 1)

            def pick_expert(n):
                for e in range(NE):
                    m = n * NE + e
                    if m >= NE:
                        a.wait_ge(S["expert_added"], m - NE + 1)
                    a.activation(pick[e], ident, ACT.Copy, scale=cf[:, m:m + 1]).then_inc(S["diagonal_ready"], 1)

            a.wait_ge(S["expert_input_ready"], UNITS)
            x_high(0)
            x_high(1)
            x_high(2)
            for j, (src, dst, n) in enumerate(((3, 4, NE), (3, 4, NE), (17, 18, 2))):
                a.wait_ge(S["logits_shifted"], j + 1)
                a.activation(rt[0:B, 8 * dst:8 * dst + n], rt[0:B, 8 * src:8 * src + n], ACT.Exp).then_inc(S["router_exp_ready"], 1)
            a.wait_ge(S["router_step_vector"], 4)
            pick_expert(0)
            pick_expert(1)
            for u in range(UNITS):
                a.wait_ge(S["expert_input_transposed"], u + 1)
                if u >= 2:
                    a.wait_ge(S["hidden_sums_ready"], 4 * (u - 1))
                a.activation(xt3[u % 2], bank[0][:, :].bitcast(F16)[:, 0:UTOK], ACT.Copy).then_inc(S["expert_input_t_copied"], 1)
                if u + 3 < UNITS:
                    x_high(u + 3)
                if u >= 2:
                    a.wait_ge(S["expert_out_ready"], u - 1)
                if u % UPB == 0:
                    a.wait_ge(S["first_weights_ready"], 2 * (u // UPB) + 2)
                for k in range(2):
                    for hf in range(2):
                        n = 2 * k + hf
                        a.wait_ge(S["hidden_sums_ready"], 4 * u + n + 1)
                        bk_ = 2 * (u // UPB) + k
                        a.activation(hs[u % 2][k][:, HF * hf:HF * hf + HF], bank[2 + n][:, 0:HF], ACT.Gelu, bias=b1s[:, bk_:bk_ + 1])\
                            .then_inc(S["hidden_ready"], 1)
                if u // UPB + 1 < B and u % UPB in (1, 2):
                    pick_expert(2 * (u // UPB) + 1 + u % UPB)

        @block.tensor
        def _(t):
            t.wait_ge(S["win_weights_loaded"], NW1)
            t.wait_ge(S["consts_loaded"], 16)
            t.wait_ge(S["setup_done"], 1)
            t.wait_ge(S["buffers_zeroed"], 1)
            for u in range(UNITS + 4):
                e, f, d, g = u - 1, u - 2, u - 3, u - 4
                if 0 <= e < UNITS:
                    t.wait_ge(S["queries_placed"], 2 * e + 2)
                    t.wait_ge(S["key_head_masked"], 8 * e + 8)
                    if e >= 1:
                        t.wait_ge(S["scores_max_ready"], 2 * e)
                    for p in range(UP):
                        tt, q = p // 4, p % 4
                        l = t.matmul(bank[5 + tt // 4][32 * q:32 * q + 32, tt % 4 * 128:tt % 4 * 128 + 128],
                                     qb[e % 2][:, p, :], km[:, p, :, :], start=True, stop=True)
                    l.then_inc(S["win_scores_ready"], 1)
                if 0 <= d < UNITS:
                    t.wait_ge(S["win_out_picked"], d + 1)
                    if d >= 1:
                        t.wait_ge(S["residual_ready"], d)
                    for j in range(3):
                        l = t.transpose(bank[7][:, 128 * j:128 * j + 128], o[:, 128 * j:128 * j + 128], ident)
                    l.then_inc(S["win_out_transposed"], 1)
                if 0 <= f < UNITS:
                    t.wait_ge(S["win_probs_ready"], f + 1)
                    t.wait_ge(S["repeated_copied"], min(f + 2, UNITS))
                    for i in range(UT):
                        l = t.transpose(bank[3 + i // 4][:, i % 4 * 128:i % 4 * 128 + 128], pn[:, i * 128:i * 128 + 128], ident)
                    l.then_inc(S["probs_transposed"], 1)
                if u < UNITS:
                    t.wait_ge(S["x_copied"], u + 1)
                    if u >= 1:
                        t.wait_ge(S["queries_placed"], 2 * u)
                        t.wait_ge(S["keys_biased"], u)
                        t.wait_ge(S["values_biased"], u)
                    if u >= 3:
                        t.wait_ge(S["win_out_picked"], u - 2)
                    if u >= 5:
                        t.wait_ge(S["tokens_t_copied"], u - 4)
                    t.matmul(bank[0][:, 0:UC], wqb, xw[:, u * UC:(u + 1) * UC], start=True, stop=True)
                    t.matmul(bank[1][:, 0:UC], wkb, xw[:, u * UC:(u + 1) * UC], start=True, stop=True)
                    for j in range(3):
                        l = t.matmul(bank[2][:, 128 * j:128 * j + 128], xu[u % 2][:, 128 * j:128 * j + 128], wvb, start=True, stop=True)
                    l.then_inc(S["qkv_ready"], 1)
                if 0 <= d < UNITS:
                    t.wait_ge(S["win_out_t_copied"], d + 1)
                    for j in range(3):
                        l = t.matmul(bank[7][:, 128 * j:128 * j + 128], ots[:, 128 * j:128 * j + 128], w2b, start=True, stop=True)
                    l.then_inc(S["projection_ready"], 1)
                if u < UNITS:
                    t.wait_ge(S["values_biased"], u + 1)
                    if f >= 0:
                        t.wait_ge(S["probs_t_copied"], 2 * f + 2)
                    if u >= 1:
                        t.wait_ge(S["repeated_copied"], u)
                    for j in range(8):
                        for q in range(4):
                            l = t.matmul(bank[3 + j // 4][32 * q:32 * q + 32, j % 4 * 96:j % 4 * 96 + 96], cs[:, C_REP + 32 * j:C_REP + 32 * j + 32],
                                         v2.rearrange("p (n c) -> p n c", c=C)[:, :, 16 * q:16 * q + 16], start=True, stop=True)
                    l.then_inc(S["values_repeated"], 1)
                if 0 <= g < UNITS:
                    t.wait_ge(S["tokens_normed"], g + 1)
                    t.wait_ge(S["values_biased"], min(u + 1, UNITS))
                    if g >= 1:
                        t.wait_ge(S["tokens_t_copied"], g)
                    for i in range(UT):
                        l = t.transpose(bank[2][:, :].bitcast(F16)[:, i * 128:i * 128 + 128], xnu[:, i, :], id16[:, :])
                    l.then_inc(S["tokens_transposed"], 1)
                if 0 <= f < UNITS:
                    t.wait_ge(S["probs_t_copied"], 2 * f + 2)
                    t.wait_ge(S["values_placed_pool"], 2 * f + 2)
                    t.wait_ge(S["values_placed_act"], 4 * f + 4)
                    if u < UNITS:
                        t.wait_ge(S["queries_placed"], 2 * u + 2)
                        t.wait_ge(S["keys_biased"], u + 1)
                    if f >= 1:
                        t.wait_ge(S["win_out_picked"], f)
                    for p in range(UP):
                        tt, q = p // 4, p % 4
                        w0 = (3 * (p % 8) + p // 8) * 2
                        l = t.matmul(bank[tt // 4][32 * q:32 * q + 32, tt % 4 * 128:tt % 4 * 128 + 128],
                                     pts[:, tt * 128 + 32 * q:tt * 128 + 32 * q + 32], vb[f % 2][:, w0:w0 + 2, :], start=True, stop=True)
                    l.then_inc(S["win_out_ready"], 1)
            t.wait_ge(S["glob_weights_centred"], 3)
            t.wait_ge(S["tokens_t_copied"], UNITS)
            t.matmul(bank[2][:, 0:128], wq2[:, :], wk2[:, :], start=True, stop=True).then_inc(S["glob_products_ready"], 1)
            t.transpose(bank[3][:, 0:64], wv2[:, :], cs[0:64, C_ID:C_ID + 64]).then_inc(S["glob_products_ready"], 1)
            t.wait_ge(S["product_part_ready"], 3)
            t.wait_ge(S["window_phase_done"], 1)
            t.wait_ge(S["tokens_t_copied"], UNITS)
            t.wait_ge(S["tokens_stored"], 16 * UNITS)

            def xslot(idx):
                if idx >= 2:
                    t.wait_ge(S["job_used"], idx - 1)
                return bank[6 + idx % 2]

            def q_proj(i, hf, idx):
                bk_ = xslot(idx)
                c0 = i * UTOK + hf * HF
                for j in range(3):
                    l = t.matmul(bk_[:, 0:HF], a3[:, j, :], xt[:, c0:c0 + HF], start=j == 0, stop=j == 2)
                l.then_inc(S["job_computed"], 1)

            def q_max(i, n, idx):
                tt, kc = n // NKC, n % NKC
                bk_ = xslot(idx)
                c0 = i // UPB * TILES * 128 + kc * KC
                if n == 0:
                    t.wait_ge(S["query_high"], 2 * i + 2)
                t.matmul(bk_[:, 0:KC], qh[i % 3][:, tt * 128:tt * 128 + 128], xt[:, c0:c0 + KC], start=True, stop=True).then_inc(S["job_computed"], 1)

            def max_rows(i, hf, idx):
                t.wait_ge(S["maxima_ready"], i + 1)
                bk_ = xslot(idx)
                for c0 in (0, 128, 256):
                    lo = hf * HF + c0
                    n = min(128, HF - c0)
                    while n > 0:
                        tt, p0 = lo // 128, lo % 128
                        m = min(n, 128 - p0)
                        l = t.matmul(bk_[0:64, lo - hf * HF:lo - hf * HF + m], zm[:, tt, :], id16[:, p0:p0 + m], start=True, stop=True)
                        lo += m
                        n -= m
                l.then_inc(S["job_computed"], 1)

            def finish(i, _, idx):
                t.wait_ge(S["sums_copied"], 2 * i + 2)
                bk_ = xslot(idx)
                for j in range(UT):
                    l = t.matmul(bk_[:, 66 * j:66 * j + 66], un[:, 128 * j:128 * j + 128], wvx[:, :], start=True, stop=True)
                l.then_inc(S["job_computed"], 1)

            def energies(i, k):
                s = i * TILES + k
                if k == 0:
                    t.wait_ge(S["job_used"], shift_job[i] + 2)
                kt = i // UPB * TILES + k
                for hf in range(2):
                    n = 2 * s + hf
                    if n >= 4:
                        t.wait_ge(S["exp_ready"], n - 3)
                    for j, q in enumerate((qh, ql)):
                        l = t.matmul(bank[n % 4][:, 0:HF], xt[:, kt * 128:kt * 128 + 128], q[i % 3][:, HF * hf:HF * hf + HF], start=j == 0, stop=j == 1)
                    l.then_inc(S["energies_ready"], 1)

            def values(s):
                i, k = s // TILES, s % TILES
                kt = i // UPB * TILES + k
                if k == 0 and i >= 1:
                    t.wait_ge(S["sums_copied"], 2 * i)
                t.wait_ge(S["low_ready_pool" if pool_low(s) else "low_ready_vector"], lows(s))
                t.wait_ge(S["exp_ready"], 2 * s + 2)
                for hf in range(2):
                    c0 = HF * hf
                    t.matmul(bank[4 + hf][:, 0:HF], xn[:, kt, :], p32[s % NP].bitcast(BF16)[:, 2 * c0 + 1:2 * c0 + 2 * HF:2], start=k == 0, stop=False)
                    l = t.matmul(bank[4 + hf][:, 0:HF], xn[:, kt, :], plo[s % NP][:, c0:c0 + HF], start=False, stop=k == TILES - 1)
                l.then_inc(S["step_added"], 1)

            serve = {"Q": q_proj, "M": q_max, "T": max_rows, "F": finish}
            for g in range(-LEAD, UNITS * TILES + VLAG):
                if 0 <= g < UNITS * TILES:
                    energies(g // TILES, g % TILES)
                todo = jobs.get(g, [])
                for kind, i, n, idx in todo[:2]:
                    serve[kind](i, n, idx)
                if g >= VLAG:
                    values(g - VLAG)
                for kind, i, n, idx in todo[2:]:
                    serve[kind](i, n, idx)
            finish(UNITS - 1, 0, finish_job[UNITS - 1])
            t.wait_ge(S["expert_input_ready"], UNITS - 1)
            for b in range(B - 1):
                t.matmul(bank[4][0:64, 384 + b:385 + b], acc3[:, b, :], ones[:, 0:1], start=True, stop=True)
            for i in range(TILES):
                if i == TILES - UT:
                    t.wait_ge(S["expert_input_ready"], UNITS)
                l = t.matmul(bank[4][0:64, 383 + B:384 + B], x3[:, (B - 1) * TILES + i, :], ones[:, 0:1], start=i == 0, stop=i == TILES - 1)
            l.then_inc(S["router_step_tensor"], 1)
            t.wait_ge(S["router_step_vector"], 1)
            t.matmul(bank[6][0:B, 16:16 + NE], acc3t[0:64, :], wr[:, :], start=True, stop=True).then_inc(S["router_step_tensor"], 1)
            t.wait_ge(S["router_step_vector"], 2)
            t.matmul(bank[6][0:B, 32:32 + NE], ones[0:B, 0:B], rt[0:B, 0:NE], start=True, stop=True).then_inc(S["router_step_tensor"], 1)
            t.wait_ge(S["router_step_vector"], 3)
            t.matmul(bank[6][:, 64:64 + 4 * B * NE], ones[0:B, :], cf[0:B, :], start=True, stop=True).then_inc(S["router_step_tensor"], 1)

            def select(n):
                if n >= 2:
                    t.wait_ge(S["second_weights_ready"], n)
                for e in range(NE):
                    m = n * NE + e
                    t.wait_ge(S["diagonal_ready"], m + 1)
                    t.matmul(chosen(n)[:, 0:NF + 2 * C], pick[e], wd[:, e, :], start=e == 0, stop=e == NE - 1).then_inc(S["expert_added"], 1)

            def second(u):
                if u >= 2:
                    t.wait_ge(S["expert_out_read"], u - 1)
                if u % UPB == 0:
                    t.wait_ge(S["second_weights_ready"], 2 * (u // UPB) + 2)
                t.wait_ge(S["hidden_ready"], 4 * u + 4)
                t.wait_ge(S["hidden_low_pool"], (3 * u + 4) // 2)
                if u % 2:
                    t.wait_ge(S["hidden_low_vector"], u // 2 + 1)
                for i in range(UT):
                    for m in range(4):
                        k = m % 2
                        hh = hs[u % 2][k].bitcast(BF16)[:, 256 * i + 1:256 * i + 256:2] if m < 2 else hl[u % 2][k][:, 128 * i:128 * i + 128]
                        for j in range(3):
                            l = t.matmul(bank[6 + u % 2][:, C * i:C * i + C], hh, w2s[:, 2 * (u // UPB) + k, j, :],
                                         start=m == 0 and j == 0, stop=m == 3 and j == 2)
                l.then_inc(S["expert_out_ready"], 1)

            def turn(u):
                t.wait_ge(S["expert_input_split"], u + 1)
                if u >= 1:
                    t.wait_ge(S["expert_input_t_copied"], u)
                for i in range(UT):
                    l = t.transpose(bank[0][:, :].bitcast(F16)[:, i * 128:i * 128 + 128], xn3[u % 3][:, i, :], id16[:, :])
                l.then_inc(S["expert_input_transposed"], 1)

            t.wait_ge(S["exp_ready"], 2 * UNITS * TILES)
            turn(0)
            t.wait_ge(S["expert_weights_loaded"], 16 * 5)
            select(0)
            select(1)
            for u in range(UNITS):
                if u + 1 < UNITS:
                    turn(u + 1)
                t.wait_ge(S["expert_input_t_copied"], u + 1)
                if u % UPB == 0:
                    t.wait_ge(S["first_weights_ready"], 2 * (u // UPB) + 2)
                for k in range(2):
                    for hf in range(2):
                        n = 2 * k + hf
                        if u >= 1:
                            t.wait_ge(S["hidden_ready"], 4 * (u - 1) + n + 1)
                        for j in range(3):
                            l = t.matmul(bank[2 + n][:, 0:HF], w1s[:, 2 * (u // UPB) + k, j, :], xt3[u % 2][:, HF * hf:HF * hf + HF], start=j == 0, stop=j == 2)
                        l.then_inc(S["hidden_sums_ready"], 1)
                if u >= 1:
                    second(u - 1)
                if u // UPB + 1 < B and u % UPB in (2, 3):
                    select(2 * (u // UPB) + u % UPB)
            second(UNITS - 1)

        @block.vector
        def _(v_):
            v = v_
            ch = Chain(v, "vector_chain")

            NORM = 9

            def norm_stage(j, src, dst, masked, signal=None, meanwhile=None):
                s, m, q, var, y, t = (ln_s[:, k * UT:(k + 1) * UT] for k in range(6))
                c3, q3 = tk(ln_c[:, :]), tk(ln_q[:, :])
                if j == 0:
                    ch(v.tensor_reduce(s, src, AX.X, ALU.add), 0, meanwhile)
                    ch(v.tensor_scalar(m, s, 1.0 / C, None, ALU.mult), 0, meanwhile)
                elif j == 1:
                    ch(v.tensor_tensor(c3, bc(m.rearrange("p (t o) -> p t o", o=1), [128, UT, C]), src, ALU.subtract), 0, meanwhile)
                elif j == 2:
                    ch(v.tensor_tensor(q3, c3, c3, ALU.mult), 0, meanwhile)
                elif j == 3:
                    ch(v.tensor_reduce(q, q3, AX.X, ALU.add), 0, meanwhile)
                    ch(v.tensor_scalar(var, q, 1.0 / C, EPS, ALU.mult, ALU.add), 0, meanwhile)
                elif j == 4:
                    ch(v.tensor_scalar(t.bitcast(I32), var.bitcast(I32), 1, None, ALU.logical_shift_right), 0, meanwhile)
                    ch(v.tensor_scalar(y.bitcast(I32), t.bitcast(I32), -1.0, MAGIC, ALU.mult, ALU.add), 0, meanwhile)
                    ch(v.tensor_scalar(var, var, 0.5, None, ALU.mult), 0, meanwhile)
                elif j <= 7:
                    ch(v.tensor_tensor(t, y, y, ALU.mult), 0, meanwhile)
                    ch(v.tensor_tensor(t, t, var, ALU.mult), 0, meanwhile)
                    ch(v.scalar_tensor_tensor(y, t, 1.5, y, ALU.subtract, ALU.mult), 0, meanwhile)
                else:
                    if masked:
                        ch(v.tensor_tensor(y, y, valid[:, :], ALU.mult))
                    l = v.tensor_tensor(dst, c3, bc(y.rearrange("p (t o) -> p t o", o=1), [128, UT, C]), ALU.mult)
                    if signal is None:
                        ch(l)
                    else:
                        l.then_inc(signal, 1)

            def norm(src, dst, masked, signal=None):
                for j in range(NORM):
                    norm_stage(j, src, dst, masked, signal)

            def split(src, dst, n):
                ch(v.tensor_copy(dst[:, :, 0:n], src[:, :, 0:n]))
                return v.tensor_tensor(dst[:, :, C:C + n], src[:, :, 0:n], dst[:, :, 0:n], ALU.subtract)

            ch(v.memset(o, 0.0))
            for x_ in xu:
                ch(v.memset(x_, 0.0))
            ch(v.memset(xnu[:, :, :], 1.0))
            for b_ in qb:
                ch(v.memset(b_, 0.0))
            ch(v.memset(vb[0], 0.0))
            v.memset(vb[1], 0.0).then_inc(S["buffers_zeroed"], 1)
            v.wait_ge(S["consts_loaded"], 16)
            v.wait_ge(S["win_weights_loaded"], NW1)
            for u in range(UNITS + 3):
                e, w, d = u - 1, u - 2, u - 3
                if 0 <= e < UNITS:
                    v.wait_ge(S["win_scores_ready"], e + 1)
                    if e >= 1:
                        v.wait_ge(S["win_exp_ready"], 2 * e)
                    if e == 0:
                        v.wait_ge(S["setup_done"], 2)
                    t0 = e % UPB * UT
                    for i, n in ((0, 4), (1, 1)):
                        dst = s1[:, 512 * i:512 * i + 128 * n].rearrange("p (t h k) -> p t h k", h=NH, k=WT)
                        src = bank[5 + i][:, 0:128 * n].rearrange("p (t h k) -> p t h k", h=NH, k=WT)
                        bb = bc(bias[:, t0 + 4 * i:t0 + 4 * i + n, :].rearrange("p t (o k) -> p t o k", o=1), [128, n, NH, WT])
                        l = v.tensor_tensor(dst, src, bb, ALU.add)
                        if i == 0:
                            ch(l, 1)
                            score_part = ch.n
                        else:
                            l.then_inc(S["scores_max_ready"], 1)
                if u < UNITS:
                    v.wait_ge(S["qkv_ready"], u + 1)
                    if u >= 1:
                        v.wait_ge(S["values_repeated"], u)
                    v.tensor_tensor(v2.rearrange("p (n c) -> p n c", c=128), bank[2][:, 0:384].rearrange("p (n c) -> p n c", c=128),
                                    bc(bvr.rearrange("p (o c) -> p o c", o=1), [128, 3, 128]), ALU.add).then_inc(S["values_biased"], 1)
                if 0 <= e < UNITS:
                    v.wait_ge(S["vector_chain"], score_part)
                    v.wait_ge(S["scores_max_ready"], 2 * e + 1)
                    v.tensor_reduce(mx, s1.rearrange("p (n k) -> p n k", k=WT), AX.X, ALU.max).then_inc(S["scores_max_ready"], 1)

                heads = list(range(NH)) if u < UNITS else []

                def next_key():
                    if heads:
                        hh = heads.pop(0)
                        v.tensor_scalar(km[:, :, hh, :], halves(kk), cs[:, C_HEAD + hh:C_HEAD + hh + 1], None, ALU.mult).then_inc(S["key_head_masked"], 1)

                if d >= 0:
                    v.wait_ge(S["projection_ready"], d + 1)
                    hu = h[:, unit_tiles(d), :]
                    l = v.tensor_tensor(hu, bank[7][:, 0:UT * C].rearrange("p (t c) -> p t c", c=C),
                                        bc(b2r.rearrange("p (o c) -> p o c", o=1), [128, UT, C]), ALU.add)
                    l.then_inc(S["residual_ready"], 1)
                    v.wait_ge(S["residual_ready"], d + 1)
                    if d >= 1:
                        v.wait_ge(S["tokens_normed"], d)
                if u < UNITS:
                    v.wait_ge(S["keys_biased"], u + 1)
                if d >= 0:
                    for j in range(4):
                        norm_stage(j, hu, tk(ln_q[:, :]), False, None, next_key)
                while heads:
                    next_key()
                if 0 <= e < UNITS:
                    v.wait_ge(S["win_exp_ready"], 2 * e + 1)
                    if e >= 1:
                        v.wait_ge(S["win_probs_ready"], e)
                    ch(v.tensor_reduce(den, pn.rearrange("p (n k) -> p n k", k=WT), AX.X, ALU.add), 1)
                    den_done = ch.n
                o3 = o.rearrange("p (t c) -> p t c", c=C)
                pair = [bank[i][:, 0:128 * n].rearrange("p (t w c) -> p t w c", w=2, c=C) for i, n in ((0, 4), (1, 1))]
                if 0 <= w < UNITS:
                    v.wait_ge(S["win_out_ready"], w + 1)
                    if w >= 1:
                        v.wait_ge(S["win_out_transposed"], w)
                    for i, n in ((0, 4), (1, 1)):
                        ch(v.tensor_scalar(o3[:, 4 * i:4 * i + n, :], pair[i][:, :, 0, :], cs[:, C_WIN:C_WIN + 1], None, ALU.mult), 1)
                    o_done = ch.n
                if 0 <= e < UNITS:
                    v.wait_ge(S["vector_chain"], den_done)
                    v.reciprocal(rden, den).then_inc(S["win_exp_ready"], 1)
                if 0 <= w < UNITS:
                    for i, n in ((0, 4), (1, 1)):
                        v.wait_ge(S["vector_chain"], o_done - 1 + i)
                        l = v.scalar_tensor_tensor(o3[:, 4 * i:4 * i + n, :], pair[i][:, :, 1, :], cs[:, C_WIN + 1:C_WIN + 2], o3[:, 4 * i:4 * i + n, :],
                                                   ALU.mult, ALU.add)
                        if i == 0:
                            ch(l, 1)
                        else:
                            v.wait_ge(S["vector_chain"], ch.n)
                            l.then_inc(S["win_out_picked"], 1)
                if d >= 0:
                    for j in range(4, NORM):
                        norm_stage(j, hu, tk(ln_q[:, :]), d % UPB == UPB - 1, None, next_key)
                    if d >= 1:
                        v.wait_ge(S["tokens_stored"], 16 * d)
                        v.wait_ge(S["tokens_transposed"], d)
                    if d % UPB == UPB - 1:
                        ch(v.tensor_copy(xnu[:, :, 63:64], valid[:, :].rearrange("p (t o) -> p t o", o=1)))
                    elif d % UPB == 0 and d:
                        ch(v.tensor_copy(xnu[:, :, 63:64], ones[:, 0:UT].rearrange("p (t o) -> p t o", o=1)))
                    split(tk(ln_q[:, :]), xnu, 63).then_inc(S["tokens_normed"], 1)
            v.wait_ge(S["glob_weights_loaded"], NW2)
            for wgt in (wq2, wk2, wv2):
                for hf in (1, 0):
                    l = v.tensor_scalar(wgt[:, 64 * hf:64 * hf + 64], wgt[:, 64 * hf:64 * hf + 64], wgt[:, 63:64], None, ALU.subtract)
                    if hf:
                        ch(l)
                l.then_inc(S["glob_weights_centred"], 1)
            v.wait_ge(S["glob_products_ready"], 2)
            ch(v.tensor_copy(wvx[:, 0:64], bank[3][:, 0:64]))
            ch(v.tensor_copy(wvx[:, 64:66], cs[:, C_ID + 63:C_ID + 65]))
            ch(v.tensor_copy(an[:, :], bank[2][:, 0:128]))
            v.tensor_reduce(sc[:, 0:1], an[:, :], AX.X, ALU.max, apply_absolute_value=True).then_inc(S["product_max_ready"], 1)
            v.wait_ge(S["product_max_ready"], 2)
            ch(v.tensor_scalar(sc[:, 1:2], sc[:, 1:2], 1e-30, None, ALU.max))
            ch(v.reciprocal(sc[:, 2:3], sc[:, 1:2]))
            ch(v.tensor_scalar(an[:, :], an[:, :], sc[:, 2:3], None, ALU.mult))
            for j in range(3):
                v.tensor_copy(a3[:, j, :], an[:, :]).then_inc(S["product_part_ready"], 1)
                if j < 2:
                    v.wait_ge(S["product_part_ready"], j + 1)
                    ch(v.tensor_tensor(an[:, :], an[:, :], a3[:, j, :], ALU.subtract))
            v.wait_ge(S["tokens_stored"], 16 * UNITS)
            v.wait_ge(S["tokens_t_copied"], UNITS)
            v.wait_ge(S["win_out_ready"], UNITS)
            v.memset(zm, 0.0).then_inc(S["window_phase_done"], 1)
            v.wait_ge(S["window_phase_done"], 1)

            def q_low(i, hf, idx):
                v.wait_ge(S["query_high"], 2 * i + hf + 1)
                c = slice(HF * hf, HF * hf + HF)
                v.tensor_tensor(ql[i % 3][:, c], bank[6 + idx % 2][:, 0:HF], qh[i % 3][:, c], ALU.subtract).then_inc(S["job_used"], 1)

            def k_max(i, n, idx):
                v.wait_ge(S["job_computed"], idx + 1)
                if n == 0 and i >= 2:
                    v.wait_ge(S["maxima_ready"], i - 1)
                v.tensor_reduce(mxk[i % 2][:, n // NKC, n % NKC:n % NKC + 1], bank[6 + idx % 2][:, 0:KC], AX.X, ALU.max).then_inc(S["job_used"], 1)

            def q_shift(i, n, idx):
                v.wait_ge(S["job_computed"], idx + 1)
                c = slice(HF * n, HF * n + HF)
                v.tensor_tensor(qh[i % 3][32:64, c], bank[6 + idx % 2][32:64, 0:HF], qh[i % 3][32:64, c], ALU.add).then_inc(S["job_used"], 1)

            def top(i):
                v.wait_ge(S["job_used"], maxima_jobs[i])
                if i >= 1:
                    v.wait_ge(S["job_computed"], shift_job[i - 1] + 2)
                ch(v.tensor_reduce(mq, mxk[i % 2], AX.X, ALU.max))
                v.tensor_scalar(zm[:, :, 63:64], mq.rearrange("p (t o) -> p t o", o=1), -1.0, None, ALU.mult).then_inc(S["maxima_ready"], 1)

            def close(i, idx):
                v.wait_ge(S["job_computed"], idx + 1)
                pr = bank[6 + idx % 2][:, 0:66 * UT].rearrange("p (t c) -> p t c", c=66)
                a3_ = tk(att)
                ch(v.reciprocal(rd.rearrange("p (t o) -> p t o", o=1), pr[:, :, 64:65]))
                ch(v.tensor_scalar(rd, rd, float(C) ** -0.5, None, ALU.mult))
                l = v.tensor_tensor(a3_, pr[:, :, 0:C], bc(rd.rearrange("p (t o) -> p t o", o=1), [128, UT, C]), ALU.mult)
                l.then_inc(S["job_used"], 1)
                v.wait_ge(S["job_used"], idx + 1)
                hu = h[:, unit_tiles(i), :]
                ch(v.tensor_tensor(hu, hu, a3_, ALU.add))

            def close_norm(i, j):
                norm_stage(j, h[:, unit_tiles(i), :], x3[:, unit_tiles(i), :], i % UPB == UPB - 1, S["expert_input_ready"])

            def low(s):
                v.wait_ge(S["exp_ready"], 2 * s + 2)
                if s >= NP:
                    v.wait_ge(S["step_added"], s - NP + 1)
                pp = p32[s % NP]
                v.tensor_tensor(plo[s % NP], pp, pp.bitcast(BF16)[:, 1::2], ALU.subtract).then_inc(S["low_ready_vector"], 1)

            for g in range(-LEAD, UNITS * TILES + LOWLAG):
                for kind, i, n, idx in jobs.get(g, ()):
                    if kind == "F":
                        close(i, idx)
                    elif kind == "T":
                        q_shift(i, n, idx)
                    elif kind == "Q":
                        q_low(i, n, idx)
                    else:
                        k_max(i, n, idx)
                if (g + 3) % TILES == 0 and 0 <= (g + 3) // TILES < UNITS:
                    top((g + 3) // TILES)
                if g >= LOWLAG and not pool_low(g - LOWLAG):
                    low(g - LOWLAG)
                i, j = divmod(g - (TILES + VLAG + 2) - 1, TILES)
                if 0 <= i < UNITS - 1 and j < NORM:
                    close_norm(i, j)
                if j == NORM + 1 and i % UPB == UPB - 1 and 0 <= i < UNITS - 1:
                    b = i // UPB
                    v.wait_ge(S["expert_input_ready"], i + 1)
                    ch(v.tensor_reduce(acc3[:, b, :], x3[:, b * TILES:(b + 1) * TILES, :].rearrange("p t c -> p c t"), AX.X, ALU.add))
            i = UNITS - 2
            for j in range(UNITS * TILES + LOWLAG - (i * TILES + TILES + VLAG + 2) - 1, NORM):
                close_norm(i, j)
            close(UNITS - 1, finish_job[UNITS - 1])
            for j in range(NORM):
                close_norm(UNITS - 1, j)
            def give(u):
                v.wait_ge(S["expert_input_high"], u + 1)
                q = xn3[u % 3]
                v.tensor_tensor(q[:, :, C:2 * C], x3[:, unit_tiles(u), :], q[:, :, 0:C], ALU.subtract).then_inc(S["expert_input_split"], 1)

            v.wait_ge(S["expert_input_ready"], UNITS)
            give(0)
            give(1)
            give(2)
            v.wait_ge(S["router_step_tensor"], 1)
            v.tensor_scalar(acc3t[0:64, :], bank[4][0:64, 384:384 + B], 1.0 / NTOK, None, ALU.mult).then_inc(S["router_step_vector"], 1)
            v.wait_ge(S["router_step_tensor"], 2)
            R = lambda j, n=NE: rt[0:B, 8 * j:8 * j + n]
            ch(v.tensor_tensor(R(1), bank[6][0:B, 16:16 + NE], brr[:, :], ALU.add))

            def softmax(src, dst, k):
                ch(v.tensor_reduce(R(2, 1), src, AX.X, ALU.max))
                v.tensor_scalar(R(3), src, R(2, 1), None, ALU.subtract).then_inc(S["logits_shifted"], 1)
                v.wait_ge(S["router_exp_ready"], k)
                ch(v.tensor_reduce(R(5, 1), R(4), AX.X, ALU.add))
                ch(v.reciprocal(R(6, 1), R(5, 1)))
                return v.tensor_scalar(dst, R(4), R(6, 1), None, ALU.mult)

            softmax(R(1), R(0), 1).then_inc(S["router_step_vector"], 1)
            v.wait_ge(S["router_step_tensor"], 3)
            ch(v.tensor_scalar(R(7), bank[6][0:B, 32:32 + NE], float(NTOK), None, ALU.mult))
            ch(v.tensor_scalar(R(8), R(7), CAPACITY, None, ALU.is_gt))
            ch(v.reciprocal(R(9), R(7)))
            ch(v.tensor_scalar(R(9), R(9), CAPACITY, -1.0, ALU.mult, ALU.add))
            ch(v.tensor_tensor(R(9), R(9), R(8), ALU.mult))
            ch(v.tensor_scalar(R(9), R(9), 1.0, None, ALU.add))
            ch(v.tensor_tensor(R(9), R(9), R(0), ALU.mult))
            ch(softmax(R(9), R(1), 2))
            for k in range(2):
                hot = R(12 + k)
                ch(v.tensor_reduce(R(10 + k, 1), R(1), AX.X, ALU.max))
                ch(v.tensor_scalar(R(14), R(1), R(10 + k, 1), None, ALU.is_equal))
                ch(v.tensor_tensor(R(14), R(14), cs[0:B, C_RANK:C_RANK + NE], ALU.mult))
                ch(v.tensor_reduce(R(15, 1), R(14), AX.X, ALU.max))
                ch(v.tensor_scalar(hot, cs[0:B, C_RANK:C_RANK + NE], R(15, 1), None, ALU.is_equal))
                if k == 0:
                    ch(v.scalar_tensor_tensor(R(1), hot, -2.0, R(1), ALU.mult, ALU.add))
            ch(v.tensor_copy(R(16, 1), R(10, 1)))
            ch(v.tensor_copy(R(16, 2)[:, 1:2], R(11, 1)))
            ch(v.tensor_reduce(R(2, 1), R(16, 2), AX.X, ALU.max))
            v.tensor_scalar(R(17, 2), R(16, 2), R(2, 1), None, ALU.subtract).then_inc(S["logits_shifted"], 1)
            v.wait_ge(S["router_exp_ready"], 3)
            ch(v.tensor_reduce(R(5, 1), R(18, 2), AX.X, ALU.add))
            ch(v.reciprocal(R(6, 1), R(5, 1)))
            ch(v.tensor_scalar(R(19, 2), R(18, 2), R(6, 1), None, ALU.mult))
            cf4 = cf[0:B, :].rearrange("p (z b k e) -> p z b k e", z=2, b=B, k=2)
            for b in range(B):
                for k in range(2):
                    ch(v.tensor_scalar(cf4[:, 0, b, k, :], R(12 + k), cs[0:B, C_DIAG + b:C_DIAG + b + 1], None, ALU.mult))
                    ch(v.tensor_scalar(cf4[:, 1, b, k, :], cf4[:, 0, b, k, :], R(19, 2)[:, k:k + 1], None, ALU.mult))
            v.tensor_copy(R(2, 1), R(5, 1)).then_inc(S["router_step_vector"], 1)
            v.wait_ge(S["router_step_tensor"], 4)
            v.tensor_copy(cf[:, :], bank[6][:, 64:64 + 4 * B * NE]).then_inc(S["router_step_vector"], 1)
            v.wait_ge(S["router_step_vector"], 4)
            cz = cf[:, :].rearrange("p (z n e) -> p z n e", z=2, e=NE)
            v.wait_ge(S["expert_weights_loaded"], 16 * 5)

            ch(v.tensor_reduce(gate, cz[:, 1], AX.X, ALU.add), 1)
            picked = w2f.rearrange("p (n e) -> p n e", e=NE)
            ch(v.tensor_tensor(picked, cz[:, 0], bc(b1d.rearrange("p (o e) -> p o e", o=1), [128, 2 * B, NE]), ALU.mult))
            ch(v.tensor_reduce(b1s, picked, AX.X, ALU.add))

            def choose(n):
                v.wait_ge(S["expert_added"], NE * n + NE)
                w1_, w2_, b2_ = w1s[:, n], w2s[:, n], b2s[:, n // 2, :]
                w1p, w2p, b2p, gt = chosen(n)[:, 0:128], chosen(n)[:, 128:192], chosen(n)[:, 192:256], gate[:, n:n + 1]
                ch(v.tensor_copy(w1_[:, 0, :], w1p), 1)
                ch(v.tensor_scalar(w2f, w2p, gt, None, ALU.mult), 1)
                ch(v.tensor_tensor(w1f, w1p, w1_[:, 0, :], ALU.subtract), 1)
                ch(v.tensor_copy(w2_[:, 0, :], w2f), 1)
                ch(v.tensor_copy(w1_[:, 1, :], w1f), 1)
                ch(v.tensor_tensor(w2f, w2f, w2_[:, 0, :], ALU.subtract), 1)
                ch(v.tensor_tensor(w1f, w1f, w1_[:, 1, :], ALU.subtract), 1)
                ch(v.tensor_copy(w2_[:, 1, :], w2f), 1)
                v.tensor_copy(w1_[:, 2, :], w1f).then_inc(S["first_weights_ready"], 1)
                v.wait_ge(S["vector_chain"], ch.n)
                ch(v.tensor_tensor(w2f, w2f, w2_[:, 1, :], ALU.subtract), 1)
                if n % 2 == 0:
                    ch(v.tensor_scalar(b2_, b2p, gt, None, ALU.mult), 1)
                else:
                    ch(v.scalar_tensor_tensor(b2_, b2p, gt, b2_, ALU.mult, ALU.add), 1)
                v.tensor_copy(w2_[:, 2, :], w2f).then_inc(S["second_weights_ready"], 1)
                v.wait_ge(S["vector_chain"], ch.n)
                v.wait_ge(S["first_weights_ready"], n + 1)
                v.wait_ge(S["second_weights_ready"], n + 1)

            choose(0)
            choose(1)
            tail_chain = Chain(v, "norm_tail_chain")

            def norm_head(u, src, meanwhile):
                s, m, q, var = (ln_s3[u % 2][:, k * UT:(k + 1) * UT] for k in range(4))
                c3, q3 = tk(ln_c3[u % 2]), tk(ln_q[:, :])
                ch(v.tensor_reduce(s, src, AX.X, ALU.add), 0, meanwhile)
                ch(v.tensor_scalar(m, s, 1.0 / C, None, ALU.mult), 0, meanwhile)
                ch(v.tensor_tensor(c3, bc(m.rearrange("p (t o) -> p t o", o=1), [128, UT, C]), src, ALU.subtract), 0, meanwhile)
                ch(v.tensor_tensor(q3, c3, c3, ALU.mult), 0, meanwhile)
                ch(v.tensor_reduce(q, q3, AX.X, ALU.add), 0, meanwhile)
                ch(v.tensor_scalar(var, q, 1.0 / C, EPS, ALU.mult, ALU.add), 0, meanwhile)

            def norm_tail(u):
                var, y, t = (ln_s3[u % 2][:, k * UT:(k + 1) * UT] for k in (3, 4, 5))

                def step(ins):
                    tail_chain.n += 1
                    ins.then_inc(tail_chain.sem, 1)

                def wait():
                    if tail_chain.n:
                        v.wait_ge(tail_chain.sem, tail_chain.n)

                step(v.tensor_scalar(t.bitcast(I32), var.bitcast(I32), 1, None, ALU.logical_shift_right))
                yield
                wait()
                step(v.tensor_scalar(y.bitcast(I32), t.bitcast(I32), -1.0, MAGIC, ALU.mult, ALU.add))
                yield
                wait()
                step(v.tensor_scalar(var, var, 0.5, None, ALU.mult))
                yield
                for _ in range(3):
                    wait()
                    step(v.tensor_tensor(t, y, y, ALU.mult))
                    yield
                    wait()
                    step(v.tensor_tensor(t, t, var, ALU.mult))
                    yield
                    wait()
                    step(v.scalar_tensor_tensor(y, t, 1.5, y, ALU.subtract, ALU.mult))
                    yield
                wait()
                if u >= 2:
                    v.wait_ge(S["out_ready"], u - 1)
                v.tensor_tensor(tk(y2[u % 2]), tk(ln_c3[u % 2]), bc(y.rearrange("p (t o) -> p t o", o=1), [128, UT, C]), ALU.mult)\
                    .then_inc(S["out_normed"], 1)
                yield

            for u in range(UNITS):
                tail = norm_tail(u - 1) if u >= 1 else iter(())

                def next_tail():
                    next(tail, None)

                if u + 3 < UNITS:
                    give(u + 3)
                    next_tail()
                b = u // UPB
                if b + 1 < B and u % UPB in (2, 3):
                    choose(2 * b + u % UPB)
                if u % 2 == 0:
                    v.wait_ge(S["hidden_ready"], 4 * (u + 1) + 4)
                    if u >= 1:
                        v.wait_ge(S["expert_out_ready"], u)
                    hh = hs[1][1]
                    v.tensor_tensor(hl[1][1], hh, hh.bitcast(BF16)[:, 1::2], ALU.subtract).then_inc(S["hidden_low_vector"], 1)
                    next_tail()
                v.wait_ge(S["expert_out_ready"], u + 1)
                v.wait_ge(S["residual_biased"], u + 1)
                y3 = tk(y1)
                l = v.tensor_tensor(y3, bank[6 + u % 2][:, 0:UT * C].rearrange("p (t c) -> p t c", c=C), x3[:, unit_tiles(u), :], ALU.add)
                l.then_inc(S["expert_out_read"], 1)
                next_tail()
                v.wait_ge(S["expert_out_read"], u + 1)
                norm_head(u, y3, next_tail)
                for _ in tail:
                    pass
            for _ in norm_tail(UNITS - 1):
                pass


_W = ["x", "wts", "Wq", "Wk", "Wv", "Wr", "br", "W1", "b1_t", "W2", "fb2", "gamma", "beta", "cst"]


def kernel(**i):
    import concourse.bacc as bacc
    from concourse.bass_utils import run_bass_kernel_spmd as run

    a = {k: np.asarray(v) for k, v in i.items()}
    w1 = a["L0_tok_w1"].reshape(C, 3, C)
    b1 = a["L0_tok_b1"].reshape(C, 3)
    he = np.arange(C).reshape(C // NH, NH).T.reshape(-1)
    wts = np.zeros((128, W_END), a["x"].dtype)
    for hf in range(2):
        r = slice(64 * hf, 64 * hf + 64)
        for c, m in ((W_Q, w1[:, 0]), (W_K, w1[:, 1]), (W_V, w1[he, 2]), (W_O, a["L0_tok_w2"])):
            wts[r, c + 64 * hf:c + 64 * hf + 64] = m.T
        wts[r, W_BQ], wts[r, W_BK] = b1[:, 0], b1[:, 1]
        wts[:, W_BV + 64 * hf:W_BV + 64 * hf + 64] = b1[he, 2]
    wts[:, W_B2:W_B2 + C] = a["L0_tok_b2"]
    for q in range(WT):
        wts[q::WT, W_POS:W_POS + WT] = a["L0_tok_pos_emb"][3 - q // WS:7 - q // WS, 3 - q % WS:7 - q % WS].reshape(-1)
    given = {
        "x": a["x"], "wts": wts, "Wq": a["L0_attn_Wq"], "Wk": a["L0_attn_Wk"], "Wv": a["L0_attn_Wv"],
        "Wr": a["L0_ffn_Wr"], "br": a["L0_ffn_br"].reshape(1, NE), "W1": a["L0_ffn_W1"], "b1_t": a["L0_ffn_b1"].T, "W2": a["L0_ffn_W2"],
        "fb2": a["L0_ffn_b2"], "gamma": a["L0_ffn_gamma"].reshape(1, C), "beta": a["L0_ffn_beta"].reshape(1, C), "cst": constants(),
    }
    nc = bacc.Bacc("TRN2", target_bir_lowering=False, num_devices=1)
    arrays, args = {}, []
    for name in _W:
        arrays[f"in_{name}"] = np.ascontiguousarray(given[name])
        args.append(nc.dram_tensor(f"in_{name}", arrays[f"in_{name}"].shape, mybir.dt.from_np(arrays[f"in_{name}"].dtype), kind="ExternalInput").ap())
    args.append(nc.dram_tensor("out", (B, NTOK, C), F32, kind="ExternalOutput").ap())
    args.append(nc.dram_tensor("tokens", (B, TILES * 128, C), F32, kind="Internal").ap())
    vit_tower(nc, *args)
    r = run(nc, [arrays], core_ids=[0])
    return r.results[0]["out"]
```
